# Optimizing a Trainium2 kernel written in Bass

```python
import numpy as np
import jax
import jax.numpy as jnp

def _softmax(x, axis=-1):
    return jax.nn.softmax(x, axis=axis)

def _gelu(x):
    return jax.nn.gelu(x, approximate=True)

def _silu(x):
    return jax.nn.silu(x)

def _sigmoid(x):
    return jax.nn.sigmoid(x)

def _layernorm(x, axis=-1, eps=1e-05):
    m = jnp.mean(x, axis=axis, keepdims=True)
    v = jnp.var(x, axis=axis, keepdims=True)
    return (x - m) / jnp.sqrt(v + eps)

def _scatter_add(tgt, idx, src, axis=0):
    return tgt.at[idx].add(src)

def _segment_sum(src, seg, n):
    return jax.ops.segment_sum(src, seg, n)
kernel_name = 'mk_adaln_ffn_d4_seqx_r8_044466'

def setup_inputs(seed: int=0):
    np.random.seed(seed)
    _w = jnp.asarray

    def _rec_inputs():
        import jax
        import jax.numpy as jnp
        _rk = jax.random.key(seed)
        x = -0.000125 + 0.9999 * jax.random.normal(jax.random.fold_in(_rk, 1), (4, 256, 256), jnp.float32)
        _lenS = 256 - jax.random.randint(jax.random.fold_in(_rk, 7), (4,), 0, max(1, 256 // 4) + 1, jnp.int32)
        _lenS2 = 256 - jax.random.randint(jax.random.fold_in(_rk, 8), (4,), 0, max(1, 256 // 4) + 1, jnp.int32)
        fside_BxSxS_0 = -1.52775e-05 + 0.999936 * jax.random.normal(jax.random.fold_in(_rk, 11), (4, 256, 256), jnp.float32)
        cond_512 = -5.03954e-05 + 1.00559 * jax.random.normal(jax.random.fold_in(_rk, 12), (4, 64), jnp.float32)
        return (x, fside_BxSxS_0, cond_512)
    x, fside_BxSxS_0, cond_512 = _rec_inputs()

    def _L0_cond_setup():
        import jax, jax.numpy as jnp
        from jax import lax
        import numpy as np
        B, T, C, TD = (8, 256, 256, 64)

        def _bi_wkv(r, k, v, w, u, time_emb):
            tf = jax.nn.sigmoid(jnp.sum(time_emb, axis=-1))[:, None, None]
            decay = jnp.exp(-jnp.exp(w.astype(jnp.float32)))[None, :] * (0.5 + 0.5 * tf[:, :, 0])
            kf = k.astype(jnp.float32)
            vf = v.astype(jnp.float32)
            ek = jnp.exp(jnp.minimum(kf, 30.0))
            ekv = ek * vf

            def step(carry, x):
                a, b = carry
                ekv_t, ek_t = x
                a = a * decay + ekv_t
                b = b * decay + ek_t
                return ((a, b), (a, b))
            ekv_t = jnp.swapaxes(ekv, 0, 1)
            ek_t = jnp.swapaxes(ek, 0, 1)
            init = (jnp.zeros_like(decay), jnp.zeros_like(decay))
            _, (nf, df) = lax.scan(step, init, (ekv_t, ek_t))
            _, (nb, db) = lax.scan(step, init, (ekv_t, ek_t), reverse=True)
            nf = jnp.swapaxes(nf, 0, 1)
            df = jnp.swapaxes(df, 0, 1)
            nb = jnp.swapaxes(nb, 0, 1)
            db = jnp.swapaxes(db, 0, 1)
            euk = jnp.exp(jnp.minimum(u.astype(jnp.float32)[None, None, :] + kf, 30.0))
            num = nf + nb - ekv + euk * vf
            den = df + db - ek + euk
            base = jax.nn.sigmoid(r.astype(jnp.float32)) * (num / jnp.maximum(den, 1e-08))
            out = base * (0.8 + 0.2 * tf)
            return out.astype(r.dtype)
        key = jax.random.key(seed)
        ks = jax.random.split(key, 6)
        return {'r': jax.random.normal(ks[0], (B, T, C), dtype=jnp.float32), 'k': jax.random.normal(ks[1], (B, T, C), dtype=jnp.float32), 'v': jax.random.normal(ks[2], (B, T, C), dtype=jnp.float32), 'w': jax.random.normal(ks[3], (C,), dtype=jnp.float32), 'u': jax.random.normal(ks[4], (C,), dtype=jnp.float32), 'time_emb': jax.random.normal(ks[5], (B, TD), dtype=jnp.float32)}
    _L0_cond_all = _L0_cond_setup()
    _L0_cond_in = {k: v for k, v in _L0_cond_all.items() if k in ('w', 'u')}
    del _L0_cond_all

    def _L0_ffn_setup():
        import jax, jax.numpy as jnp
        import numpy as np
        K_TOP = 2
        key = jax.random.key(seed)
        k0, k1, k2 = jax.random.split(key, 3)
        B, S, D, E, F = (4, 256, 256, 8, 256)
        x = jax.random.normal(k0, (B, S, D), dtype=jnp.float32)
        Wr = jax.random.normal(k1, (D, E), dtype=jnp.float32) * 0.02
        We = jax.random.normal(k2, (E, D, F), dtype=jnp.float32) * 0.02
        be = jnp.zeros((E, F), dtype=jnp.float32)
        return {'x': x, 'Wr': Wr, 'We': We, 'be': be}
    _L0_ffn_all = _L0_ffn_setup()
    _L0_ffn_in = {k: v for k, v in _L0_ffn_all.items() if k in ('Wr', 'We', 'be')}
    del _L0_ffn_all

    def _L1_cond_setup():
        import jax, jax.numpy as jnp
        from jax import lax
        import numpy as np
        B, T, C, TD = (8, 256, 256, 64)

        def _bi_wkv(r, k, v, w, u, time_emb):
            tf = jax.nn.sigmoid(jnp.sum(time_emb, axis=-1))[:, None, None]
            decay = jnp.exp(-jnp.exp(w.astype(jnp.float32)))[None, :] * (0.5 + 0.5 * tf[:, :, 0])
            kf = k.astype(jnp.float32)
            vf = v.astype(jnp.float32)
            ek = jnp.exp(jnp.minimum(kf, 30.0))
            ekv = ek * vf

            def step(carry, x):
                a, b = carry
                ekv_t, ek_t = x
                a = a * decay + ekv_t
                b = b * decay + ek_t
                return ((a, b), (a, b))
            ekv_t = jnp.swapaxes(ekv, 0, 1)
            ek_t = jnp.swapaxes(ek, 0, 1)
            init = (jnp.zeros_like(decay), jnp.zeros_like(decay))
            _, (nf, df) = lax.scan(step, init, (ekv_t, ek_t))
            _, (nb, db) = lax.scan(step, init, (ekv_t, ek_t), reverse=True)
            nf = jnp.swapaxes(nf, 0, 1)
            df = jnp.swapaxes(df, 0, 1)
            nb = jnp.swapaxes(nb, 0, 1)
            db = jnp.swapaxes(db, 0, 1)
            euk = jnp.exp(jnp.minimum(u.astype(jnp.float32)[None, None, :] + kf, 30.0))
            num = nf + nb - ekv + euk * vf
            den = df + db - ek + euk
            base = jax.nn.sigmoid(r.astype(jnp.float32)) * (num / jnp.maximum(den, 1e-08))
            out = base * (0.8 + 0.2 * tf)
            return out.astype(r.dtype)
        key = jax.random.key(seed)
        ks = jax.random.split(key, 6)
        return {'r': jax.random.normal(ks[0], (B, T, C), dtype=jnp.float32), 'k': jax.random.normal(ks[1], (B, T, C), dtype=jnp.float32), 'v': jax.random.normal(ks[2], (B, T, C), dtype=jnp.float32), 'w': jax.random.normal(ks[3], (C,), dtype=jnp.float32), 'u': jax.random.normal(ks[4], (C,), dtype=jnp.float32), 'time_emb': jax.random.normal(ks[5], (B, TD), dtype=jnp.float32)}
    _L1_cond_all = _L1_cond_setup()
    _L1_cond_in = {k: v for k, v in _L1_cond_all.items() if k in ('w', 'u')}
    del _L1_cond_all

    def _L1_ffn_setup():
        import jax, jax.numpy as jnp
        import numpy as np
        E = 8
        CAPACITY_FACTOR = 1.25
        B, T, H, I = (4, 128, 256, 176)
        key = jax.random.key(seed)
        k0, k1, k2, k3, k4 = jax.random.split(key, 5)
        x = jax.random.normal(k0, (B, T, H), jnp.float32)
        Wr = jax.random.normal(k1, (E, H), jnp.float32) * 0.02
        Wg = jax.random.normal(k2, (E, I, H), jnp.float32) * 0.02
        Wu = jax.random.normal(k3, (E, I, H), jnp.float32) * 0.02
        Wd = jax.random.normal(k4, (E, H, I), jnp.float32) * 0.02
        return {'x': x, 'Wr': Wr, 'Wg': Wg, 'Wu': Wu, 'Wd': Wd}
    _L1_ffn_all = _L1_ffn_setup()
    _L1_ffn_in = {k: v for k, v in _L1_ffn_all.items() if k in ('Wr', 'Wg', 'Wu', 'Wd')}
    del _L1_ffn_all

    def _L2_cond_setup():
        import jax, jax.numpy as jnp
        from jax import lax
        import numpy as np
        B, T, C, TD = (8, 256, 256, 64)

        def _bi_wkv(r, k, v, w, u, time_emb):
            tf = jax.nn.sigmoid(jnp.sum(time_emb, axis=-1))[:, None, None]
            decay = jnp.exp(-jnp.exp(w.astype(jnp.float32)))[None, :] * (0.5 + 0.5 * tf[:, :, 0])
            kf = k.astype(jnp.float32)
            vf = v.astype(jnp.float32)
            ek = jnp.exp(jnp.minimum(kf, 30.0))
            ekv = ek * vf

            def step(carry, x):
                a, b = carry
                ekv_t, ek_t = x
                a = a * decay + ekv_t
                b = b * decay + ek_t
                return ((a, b), (a, b))
            ekv_t = jnp.swapaxes(ekv, 0, 1)
            ek_t = jnp.swapaxes(ek, 0, 1)
            init = (jnp.zeros_like(decay), jnp.zeros_like(decay))
            _, (nf, df) = lax.scan(step, init, (ekv_t, ek_t))
            _, (nb, db) = lax.scan(step, init, (ekv_t, ek_t), reverse=True)
            nf = jnp.swapaxes(nf, 0, 1)
            df = jnp.swapaxes(df, 0, 1)
            nb = jnp.swapaxes(nb, 0, 1)
            db = jnp.swapaxes(db, 0, 1)
            euk = jnp.exp(jnp.minimum(u.astype(jnp.float32)[None, None, :] + kf, 30.0))
            num = nf + nb - ekv + euk * vf
            den = df + db - ek + euk
            base = jax.nn.sigmoid(r.astype(jnp.float32)) * (num / jnp.maximum(den, 1e-08))
            out = base * (0.8 + 0.2 * tf)
            return out.astype(r.dtype)
        key = jax.random.key(seed)
        ks = jax.random.split(key, 6)
        return {'r': jax.random.normal(ks[0], (B, T, C), dtype=jnp.float32), 'k': jax.random.normal(ks[1], (B, T, C), dtype=jnp.float32), 'v': jax.random.normal(ks[2], (B, T, C), dtype=jnp.float32), 'w': jax.random.normal(ks[3], (C,), dtype=jnp.float32), 'u': jax.random.normal(ks[4], (C,), dtype=jnp.float32), 'time_emb': jax.random.normal(ks[5], (B, TD), dtype=jnp.float32)}
    _L2_cond_all = _L2_cond_setup()
    _L2_cond_in = {k: v for k, v in _L2_cond_all.items() if k in ('w', 'u')}
    del _L2_cond_all

    def _L2_ffn_setup():
        import jax, jax.numpy as jnp
        import numpy as np
        K = 2

        def gelu(v):
            return jax.nn.gelu(v, approximate=False)
        key = jax.random.key(seed)
        ks = jax.random.split(key, 10)
        B, S, D, H, E = (4, 256, 256, 128, 8)
        SH = 2 * H
        u = lambda k_, shape, b: jax.random.uniform(k_, shape, jnp.float32, -b, b)
        return {'x': jax.random.normal(ks[0], (B, S, D), jnp.float32), 'gate_w': u(ks[1], (D, E), 1.0 / D), 'w1': u(ks[2], (E, D, H), 1.0 / D), 'b1': u(ks[3], (E, H), 1.0 / np.sqrt(D)), 'w2': u(ks[4], (E, H, D), 1.0 / H), 'b2': u(ks[5], (E, D), 1.0 / np.sqrt(H)), 'shared_w1': u(ks[6], (D, SH), 1.0 / D), 'shared_b1': u(ks[7], (SH,), 1.0 / np.sqrt(D)), 'shared_w2': u(ks[8], (SH, D), 1.0 / SH), 'shared_b2': u(ks[9], (D,), 1.0 / np.sqrt(SH))}
    _L2_ffn_all = _L2_ffn_setup()
    _L2_ffn_in = {k: v for k, v in _L2_ffn_all.items() if k in ('gate_w', 'w1', 'b1', 'w2', 'b2', 'shared_w1', 'shared_b1', 'shared_w2', 'shared_b2')}
    del _L2_ffn_all

    def _L3_cond_setup():
        import jax, jax.numpy as jnp
        from jax import lax
        import numpy as np
        B, T, C, TD = (8, 256, 256, 64)

        def _bi_wkv(r, k, v, w, u, time_emb):
            tf = jax.nn.sigmoid(jnp.sum(time_emb, axis=-1))[:, None, None]
            decay = jnp.exp(-jnp.exp(w.astype(jnp.float32)))[None, :] * (0.5 + 0.5 * tf[:, :, 0])
            kf = k.astype(jnp.float32)
            vf = v.astype(jnp.float32)
            ek = jnp.exp(jnp.minimum(kf, 30.0))
            ekv = ek * vf

            def step(carry, x):
                a, b = carry
                ekv_t, ek_t = x
                a = a * decay + ekv_t
                b = b * decay + ek_t
                return ((a, b), (a, b))
            ekv_t = jnp.swapaxes(ekv, 0, 1)
            ek_t = jnp.swapaxes(ek, 0, 1)
            init = (jnp.zeros_like(decay), jnp.zeros_like(decay))
            _, (nf, df) = lax.scan(step, init, (ekv_t, ek_t))
            _, (nb, db) = lax.scan(step, init, (ekv_t, ek_t), reverse=True)
            nf = jnp.swapaxes(nf, 0, 1)
            df = jnp.swapaxes(df, 0, 1)
            nb = jnp.swapaxes(nb, 0, 1)
            db = jnp.swapaxes(db, 0, 1)
            euk = jnp.exp(jnp.minimum(u.astype(jnp.float32)[None, None, :] + kf, 30.0))
            num = nf + nb - ekv + euk * vf
            den = df + db - ek + euk
            base = jax.nn.sigmoid(r.astype(jnp.float32)) * (num / jnp.maximum(den, 1e-08))
            out = base * (0.8 + 0.2 * tf)
            return out.astype(r.dtype)
        key = jax.random.key(seed)
        ks = jax.random.split(key, 6)
        return {'r': jax.random.normal(ks[0], (B, T, C), dtype=jnp.float32), 'k': jax.random.normal(ks[1], (B, T, C), dtype=jnp.float32), 'v': jax.random.normal(ks[2], (B, T, C), dtype=jnp.float32), 'w': jax.random.normal(ks[3], (C,), dtype=jnp.float32), 'u': jax.random.normal(ks[4], (C,), dtype=jnp.float32), 'time_emb': jax.random.normal(ks[5], (B, TD), dtype=jnp.float32)}
    _L3_cond_all = _L3_cond_setup()
    _L3_cond_in = {k: v for k, v in _L3_cond_all.items() if k in ('w', 'u')}
    del _L3_cond_all

    def _L3_ffn_setup():
        import jax, jax.numpy as jnp
        import numpy as np
        TOP_K = 4
        key = jax.random.key(seed)
        ks = jax.random.split(key, 8)
        B, S, H = (1, 128, 256)
        E, I = (60, 176)
        I_SH = 704
        s = 0.02
        return {'hidden_states': jax.random.normal(ks[0], (B, S, H), jnp.float32), 'gate_w': jax.random.normal(ks[1], (E, H), jnp.float32) * s, 'shared_gate_w': jax.random.normal(ks[2], (1, H), jnp.float32) * s, 'w13': jax.random.normal(ks[3], (E, 2 * I, H), jnp.float32) * s, 'w2': jax.random.normal(ks[4], (E, H, I), jnp.float32) * s, 'se_gate_up_w': jax.random.normal(ks[5], (2 * I_SH, H), jnp.float32) * s, 'se_down_w': jax.random.normal(ks[6], (H, I_SH), jnp.float32) * s}
    _L3_ffn_all = _L3_ffn_setup()
    _L3_ffn_in = {k: v for k, v in _L3_ffn_all.items() if k in ('gate_w', 'shared_gate_w', 'w13', 'w2', 'se_gate_up_w', 'se_down_w')}
    del _L3_ffn_all
    return {'x': x, 'fside_BxSxS_0': fside_BxSxS_0, 'cond_512': cond_512, 'L0_cond_w': _L0_cond_in['w'], 'L0_cond_u': _L0_cond_in['u'], 'L0_ffn_Wr': _L0_ffn_in['Wr'], 'L0_ffn_We': _L0_ffn_in['We'], 'L0_ffn_be': _L0_ffn_in['be'], 'L1_cond_w': _L1_cond_in['w'], 'L1_cond_u': _L1_cond_in['u'], 'L1_ffn_Wr': _L1_ffn_in['Wr'], 'L1_ffn_Wg': _L1_ffn_in['Wg'], 'L1_ffn_Wu': _L1_ffn_in['Wu'], 'L1_ffn_Wd': _L1_ffn_in['Wd'], 'L2_cond_w': _L2_cond_in['w'], 'L2_cond_u': _L2_cond_in['u'], 'L2_ffn_gate_w': _L2_ffn_in['gate_w'], 'L2_ffn_w1': _L2_ffn_in['w1'], 'L2_ffn_b1': _L2_ffn_in['b1'], 'L2_ffn_w2': _L2_ffn_in['w2'], 'L2_ffn_b2': _L2_ffn_in['b2'], 'L2_ffn_shared_w1': _L2_ffn_in['shared_w1'], 'L2_ffn_shared_b1': _L2_ffn_in['shared_b1'], 'L2_ffn_shared_w2': _L2_ffn_in['shared_w2'], 'L2_ffn_shared_b2': _L2_ffn_in['shared_b2'], 'L3_cond_w': _L3_cond_in['w'], 'L3_cond_u': _L3_cond_in['u'], 'L3_ffn_gate_w': _L3_ffn_in['gate_w'], 'L3_ffn_shared_gate_w': _L3_ffn_in['shared_gate_w'], 'L3_ffn_w13': _L3_ffn_in['w13'], 'L3_ffn_w2': _L3_ffn_in['w2'], 'L3_ffn_se_gate_up_w': _L3_ffn_in['se_gate_up_w'], 'L3_ffn_se_down_w': _L3_ffn_in['se_down_w']}

def reference(x, fside_BxSxS_0, cond_512, L0_cond_w, L0_cond_u, L0_ffn_Wr, L0_ffn_We, L0_ffn_be, L1_cond_w, L1_cond_u, L1_ffn_Wr, L1_ffn_Wg, L1_ffn_Wu, L1_ffn_Wd, L2_cond_w, L2_cond_u, L2_ffn_gate_w, L2_ffn_w1, L2_ffn_b1, L2_ffn_w2, L2_ffn_b2, L2_ffn_shared_w1, L2_ffn_shared_b1, L2_ffn_shared_w2, L2_ffn_shared_b2, L3_cond_w, L3_cond_u, L3_ffn_gate_w, L3_ffn_shared_gate_w, L3_ffn_w13, L3_ffn_w2, L3_ffn_se_gate_up_w, L3_ffn_se_down_w):
    import jax
    import jax.numpy as jnp

    def _L0_cond_ref(r, k, v, w, u, time_emb):
        import jax, jax.numpy as jnp
        from jax import lax
        import numpy as np
        B, T, C, TD = (8, 256, 256, 64)

        def _bi_wkv(r, k, v, w, u, time_emb):
            tf = jax.nn.sigmoid(jnp.sum(time_emb, axis=-1))[:, None, None]
            decay = jnp.exp(-jnp.exp(w.astype(jnp.float32)))[None, :] * (0.5 + 0.5 * tf[:, :, 0])
            kf = k.astype(jnp.float32)
            vf = v.astype(jnp.float32)
            ek = jnp.exp(jnp.minimum(kf, 30.0))
            ekv = ek * vf

            def step(carry, x):
                a, b = carry
                ekv_t, ek_t = x
                a = a * decay + ekv_t
                b = b * decay + ek_t
                return ((a, b), (a, b))
            ekv_t = jnp.swapaxes(ekv, 0, 1)
            ek_t = jnp.swapaxes(ek, 0, 1)
            init = (jnp.zeros_like(decay), jnp.zeros_like(decay))
            _, (nf, df) = lax.scan(step, init, (ekv_t, ek_t))
            _, (nb, db) = lax.scan(step, init, (ekv_t, ek_t), reverse=True)
            nf = jnp.swapaxes(nf, 0, 1)
            df = jnp.swapaxes(df, 0, 1)
            nb = jnp.swapaxes(nb, 0, 1)
            db = jnp.swapaxes(db, 0, 1)
            euk = jnp.exp(jnp.minimum(u.astype(jnp.float32)[None, None, :] + kf, 30.0))
            num = nf + nb - ekv + euk * vf
            den = df + db - ek + euk
            base = jax.nn.sigmoid(r.astype(jnp.float32)) * (num / jnp.maximum(den, 1e-08))
            out = base * (0.8 + 0.2 * tf)
            return out.astype(r.dtype)
        return _bi_wkv(r, k, v, w, u, time_emb)

    def _L0_ffn_ref(x, Wr, We, be):
        import jax, jax.numpy as jnp
        import numpy as np
        K_TOP = 2
        logits = jnp.einsum('bsd,de->bse', x, Wr)
        w, sel = jax.lax.top_k(logits, K_TOP)
        w = jax.nn.softmax(w, axis=-1)
        E = We.shape[0]
        gate = jnp.einsum('bsk,bske->bse', w, jax.nn.one_hot(sel, E, dtype=w.dtype))
        out = jnp.zeros(x.shape[:2] + (We.shape[2],), dtype=x.dtype)
        for e in range(E):
            out = out + gate[..., e:e + 1] * (jnp.einsum('bsd,df->bsf', x, We[e]) + be[e])
        return out

    def _L1_cond_ref(r, k, v, w, u, time_emb):
        import jax, jax.numpy as jnp
        from jax import lax
        import numpy as np
        B, T, C, TD = (8, 256, 256, 64)

        def _bi_wkv(r, k, v, w, u, time_emb):
            tf = jax.nn.sigmoid(jnp.sum(time_emb, axis=-1))[:, None, None]
            decay = jnp.exp(-jnp.exp(w.astype(jnp.float32)))[None, :] * (0.5 + 0.5 * tf[:, :, 0])
            kf = k.astype(jnp.float32)
            vf = v.astype(jnp.float32)
            ek = jnp.exp(jnp.minimum(kf, 30.0))
            ekv = ek * vf

            def step(carry, x):
                a, b = carry
                ekv_t, ek_t = x
                a = a * decay + ekv_t
                b = b * decay + ek_t
                return ((a, b), (a, b))
            ekv_t = jnp.swapaxes(ekv, 0, 1)
            ek_t = jnp.swapaxes(ek, 0, 1)
            init = (jnp.zeros_like(decay), jnp.zeros_like(decay))
            _, (nf, df) = lax.scan(step, init, (ekv_t, ek_t))
            _, (nb, db) = lax.scan(step, init, (ekv_t, ek_t), reverse=True)
            nf = jnp.swapaxes(nf, 0, 1)
            df = jnp.swapaxes(df, 0, 1)
            nb = jnp.swapaxes(nb, 0, 1)
            db = jnp.swapaxes(db, 0, 1)
            euk = jnp.exp(jnp.minimum(u.astype(jnp.float32)[None, None, :] + kf, 30.0))
            num = nf + nb - ekv + euk * vf
            den = df + db - ek + euk
            base = jax.nn.sigmoid(r.astype(jnp.float32)) * (num / jnp.maximum(den, 1e-08))
            out = base * (0.8 + 0.2 * tf)
            return out.astype(r.dtype)
        return _bi_wkv(r, k, v, w, u, time_emb)

    def _L1_ffn_ref(x, Wr, Wg, Wu, Wd):
        import jax, jax.numpy as jnp
        import numpy as np
        E = 8
        CAPACITY_FACTOR = 1.25
        B, T, H, I = (4, 128, 256, 176)
        Bb, Tt, Hh = x.shape
        N = Bb * Tt
        cap = max(1, int(CAPACITY_FACTOR * (N * 2 / E)))
        xf = x.reshape(N, Hh)
        logits = jnp.einsum('nh,eh->ne', xf, Wr)
        gate = jax.nn.softmax(logits, axis=-1)
        top2_val, top2_idx = jax.lax.top_k(gate, 2)
        flat_idx = jnp.concatenate([top2_idx[:, 0], top2_idx[:, 1]])
        flat_val = jnp.concatenate([top2_val[:, 0], top2_val[:, 1]])
        onehot = jax.nn.one_hot(flat_idx, E, dtype=jnp.int32)
        rank = (jnp.cumsum(onehot, axis=0) * onehot).sum(-1)
        keep = rank <= cap
        w_assign = jnp.where(keep, flat_val, 0.0)
        tok = jnp.tile(jnp.arange(N), 2)
        comb = jnp.zeros((N, E), x.dtype).at[tok, flat_idx].add(w_assign)
        g = jax.nn.silu(jnp.einsum('nh,eih->eni', xf, Wg))
        u = jnp.einsum('nh,eih->eni', xf, Wu)
        out_e = jnp.einsum('eni,ehi->enh', g * u, Wd)
        y = jnp.einsum('ne,enh->nh', comb, out_e)
        return y.reshape(Bb, Tt, Hh)

    def _L2_cond_ref(r, k, v, w, u, time_emb):
        import jax, jax.numpy as jnp
        from jax import lax
        import numpy as np
        B, T, C, TD = (8, 256, 256, 64)

        def _bi_wkv(r, k, v, w, u, time_emb):
            tf = jax.nn.sigmoid(jnp.sum(time_emb, axis=-1))[:, None, None]
            decay = jnp.exp(-jnp.exp(w.astype(jnp.float32)))[None, :] * (0.5 + 0.5 * tf[:, :, 0])
            kf = k.astype(jnp.float32)
            vf = v.astype(jnp.float32)
            ek = jnp.exp(jnp.minimum(kf, 30.0))
            ekv = ek * vf

            def step(carry, x):
                a, b = carry
                ekv_t, ek_t = x
                a = a * decay + ekv_t
                b = b * decay + ek_t
                return ((a, b), (a, b))
            ekv_t = jnp.swapaxes(ekv, 0, 1)
            ek_t = jnp.swapaxes(ek, 0, 1)
            init = (jnp.zeros_like(decay), jnp.zeros_like(decay))
            _, (nf, df) = lax.scan(step, init, (ekv_t, ek_t))
            _, (nb, db) = lax.scan(step, init, (ekv_t, ek_t), reverse=True)
            nf = jnp.swapaxes(nf, 0, 1)
            df = jnp.swapaxes(df, 0, 1)
            nb = jnp.swapaxes(nb, 0, 1)
            db = jnp.swapaxes(db, 0, 1)
            euk = jnp.exp(jnp.minimum(u.astype(jnp.float32)[None, None, :] + kf, 30.0))
            num = nf + nb - ekv + euk * vf
            den = df + db - ek + euk
            base = jax.nn.sigmoid(r.astype(jnp.float32)) * (num / jnp.maximum(den, 1e-08))
            out = base * (0.8 + 0.2 * tf)
            return out.astype(r.dtype)
        return _bi_wkv(r, k, v, w, u, time_emb)

    def _L2_ffn_ref(x, gate_w, w1, b1, w2, b2, shared_w1, shared_b1, shared_w2, shared_b2):
        import jax, jax.numpy as jnp
        import numpy as np
        K = 2

        def gelu(v):
            return jax.nn.gelu(v, approximate=False)
        B, S, D = x.shape
        E = gate_w.shape[1]
        xf = x.reshape(-1, D)
        logits = xf @ gate_w
        top_logits, top_idx = jax.lax.top_k(logits, K)
        top_gates = jax.nn.softmax(top_logits, axis=-1)
        gates = jnp.sum(jax.nn.one_hot(top_idx, E, dtype=xf.dtype) * top_gates[..., None], axis=1)
        h = gelu(jnp.einsum('nd,edh->neh', xf, w1) + b1)
        out_e = jnp.einsum('neh,ehd->ned', h, w2) + b2
        routed = jnp.einsum('ne,ned->nd', gates, out_e)
        shared = gelu(xf @ shared_w1 + shared_b1) @ shared_w2 + shared_b2
        return (routed + shared).reshape(B, S, D)

    def _L3_cond_ref(r, k, v, w, u, time_emb):
        import jax, jax.numpy as jnp
        from jax import lax
        import numpy as np
        B, T, C, TD = (8, 256, 256, 64)

        def _bi_wkv(r, k, v, w, u, time_emb):
            tf = jax.nn.sigmoid(jnp.sum(time_emb, axis=-1))[:, None, None]
            decay = jnp.exp(-jnp.exp(w.astype(jnp.float32)))[None, :] * (0.5 + 0.5 * tf[:, :, 0])
            kf = k.astype(jnp.float32)
            vf = v.astype(jnp.float32)
            ek = jnp.exp(jnp.minimum(kf, 30.0))
            ekv = ek * vf

            def step(carry, x):
                a, b = carry
                ekv_t, ek_t = x
                a = a * decay + ekv_t
                b = b * decay + ek_t
                return ((a, b), (a, b))
            ekv_t = jnp.swapaxes(ekv, 0, 1)
            ek_t = jnp.swapaxes(ek, 0, 1)
            init = (jnp.zeros_like(decay), jnp.zeros_like(decay))
            _, (nf, df) = lax.scan(step, init, (ekv_t, ek_t))
            _, (nb, db) = lax.scan(step, init, (ekv_t, ek_t), reverse=True)
            nf = jnp.swapaxes(nf, 0, 1)
            df = jnp.swapaxes(df, 0, 1)
            nb = jnp.swapaxes(nb, 0, 1)
            db = jnp.swapaxes(db, 0, 1)
            euk = jnp.exp(jnp.minimum(u.astype(jnp.float32)[None, None, :] + kf, 30.0))
            num = nf + nb - ekv + euk * vf
            den = df + db - ek + euk
            base = jax.nn.sigmoid(r.astype(jnp.float32)) * (num / jnp.maximum(den, 1e-08))
            out = base * (0.8 + 0.2 * tf)
            return out.astype(r.dtype)
        return _bi_wkv(r, k, v, w, u, time_emb)

    def _L3_ffn_ref(hidden_states, gate_w, shared_gate_w, w13, w2, se_gate_up_w, se_down_w):
        import jax, jax.numpy as jnp
        import numpy as np
        TOP_K = 4
        orig_shape = hidden_states.shape
        E, H = gate_w.shape
        I = w2.shape[2]
        x = hidden_states.reshape(-1, H)
        M = x.shape[0]
        gu = x @ se_gate_up_w.T
        I_sh = se_down_w.shape[1]
        shared = jax.nn.silu(gu[:, :I_sh]) * gu[:, I_sh:] @ se_down_w.T
        shared = shared * jax.nn.sigmoid(x @ shared_gate_w.T)
        logits = x @ gate_w.T
        probs = jax.nn.softmax(logits.astype(jnp.float32), axis=-1)
        weights, sel = jax.lax.top_k(probs, TOP_K)
        cw = jnp.zeros((M, E), jnp.float32).at[jnp.arange(M)[:, None], sel].add(weights)

        def step(acc, ews):
            w13_e, w2_e, cw_e = ews
            gu_e = x @ w13_e.T
            h = jax.nn.silu(gu_e[:, :I]) * gu_e[:, I:]
            return (acc + cw_e[:, None] * (h @ w2_e.T), None)
        sparse, _ = jax.lax.scan(step, jnp.zeros((M, H), jnp.float32), (w13, w2, cw.T))
        return (shared + sparse).reshape(orig_shape)
    x = x + _L0_ffn_ref(_L0_cond_ref(x, fside_BxSxS_0, fside_BxSxS_0, L0_cond_w, L0_cond_u, cond_512), L0_ffn_Wr, L0_ffn_We, L0_ffn_be)
    x = x + _L1_ffn_ref(_L1_cond_ref(x, fside_BxSxS_0, fside_BxSxS_0, L1_cond_w, L1_cond_u, cond_512), L1_ffn_Wr, L1_ffn_Wg, L1_ffn_Wu, L1_ffn_Wd)
    x = x + _L2_ffn_ref(_L2_cond_ref(x, fside_BxSxS_0, fside_BxSxS_0, L2_cond_w, L2_cond_u, cond_512), L2_ffn_gate_w, L2_ffn_w1, L2_ffn_b1, L2_ffn_w2, L2_ffn_b2, L2_ffn_shared_w1, L2_ffn_shared_b1, L2_ffn_shared_w2, L2_ffn_shared_b2)
    x = x + _L3_ffn_ref(_L3_cond_ref(x, fside_BxSxS_0, fside_BxSxS_0, L3_cond_w, L3_cond_u, cond_512), L3_ffn_gate_w, L3_ffn_shared_gate_w, L3_ffn_w13, L3_ffn_w2, L3_ffn_se_gate_up_w, L3_ffn_se_down_w)
    return x

_drawn_inputs = setup_inputs


def setup_inputs(seed=0):
    import zlib

    import numpy as np

    out = dict(_drawn_inputs(seed))
    spreads = {'L0_ffn_be': (0.0, 0.1)}
    factors = {'cond_512': 2.861,
     'L1_cond_w': 8.0,
     'L1_cond_u': 8.0,
     'L1_ffn_Wr': 8.0,
     'L1_ffn_Wg': 8.0,
     'L1_ffn_Wu': 8.0,
     'L1_ffn_Wd': 8.0,
     'L2_cond_u': 4.506,
     'L2_ffn_w1': 31.577,
     'L2_ffn_b1': 8.0,
     'L2_ffn_w2': 8.0,
     'L2_ffn_shared_w1': 31.21,
     'L2_ffn_shared_b1': 8.0,
     'L2_ffn_shared_w2': 8.0,
     'L3_cond_w': 8.0,
     'L3_cond_u': 8.0,
     'L3_ffn_gate_w': 8.0,
     'L3_ffn_shared_gate_w': 8.0,
     'L3_ffn_w13': 8.0,
     'L3_ffn_w2': 8.0,
     'L3_ffn_se_gate_up_w': 8.0,
     'L3_ffn_se_down_w': 8.0,
     'L2_cond_w': 2.687}
    for name, (base, spread) in spreads.items():
        noise = np.random.default_rng([zlib.crc32(name.encode()), seed]).standard_normal(out[name].shape)
        drawn = base * np.exp(spread * noise) if base else spread * noise
        out[name] = jnp.asarray(drawn.astype(out[name].dtype))
    for name, factor in factors.items():
        out[name] = (out[name] * factor).astype(out[name].dtype)
    return out
```

```python
from contextlib import ExitStack

import numpy as np

import concourse.bass as bass
from concourse import mybir

P = 128
F32 = mybir.dt.float32
BF16 = mybir.dt.bfloat16
I32 = mybir.dt.int32
U32 = mybir.dt.uint32
ALU = mybir.AluOpType
ACT = mybir.ActivationFunctionType
AX = mybir.AxisListType

B, T, C = 4, 256, 256
N = B * T
KC = C // P
TT = N // P
HALF = 512
LAYERS = 4
SEGS = KC * B
E = 8
GCOLS = 16
I1 = 176
CAP = int(1.25 * (N * 2 / E))
CH1 = E * I1 // P
CH2 = E + 2
E3, K3 = 60, 4
ISH = 704
CH3 = -(-ISH // P)
IH = I1 // 2
MAXTILES = E3 + (K3 * N - E3) // P
RING = 4
M_STEPS = 11


def build(nc, t):
    with ExitStack() as ctx:
        def sb(name, shape, dt=F32):
            return ctx.enter_context(nc.sbuf_tensor(name, shape, dt))

        def sem(name):
            return ctx.enter_context(nc.semaphore(name))

        xT = sb("xT", [P, KC, N])
        kv = sb("kv", [P, KC, N])
        ek = sb("ek", [P, KC, N])
        ekv = sb("ekv", [P, KC, N])
        euk = sb("euk", [P, LAYERS, KC, N])
        cnum = sb("cnum", [P, 2, KC, N])
        ekr = sb("ekr", [P, KC, N])
        ekvr = sb("ekvr", [P, KC, N])
        mix = sb("mix", [P, KC, N])
        yT = sb("yT", [P, KC, N])
        ident = sb("ident", [P, P])
        identb = sb("identb", [P, P], BF16)
        tri = sb("tri", [P, 3, P], BF16)
        sel = sb("sel", [P, E + CH1 + CH2 + 1, P], BF16)
        iota = sb("iota", [P, P])
        pcol = sb("pcol", [P, 1])
        scanmask1 = sb("scanmask1", [P, E * 2 * TT])
        scanmask3 = sb("scanmask3", [P, E3 * TT])
        tbl8 = sb("tbl8", [P, TT])
        wu = sb("wu", [P, 2, LAYERS, KC])
        cond = sb("cond", [P, B, 64])
        tf = sb("tf", [P, B])
        tfhalf = sb("tfhalf", [P, B])
        tfout = sb("tfout", [P, B])
        tfout8 = sb("tfout8", [P, SEGS])
        ew = sb("ew", [P, LAYERS, KC])
        base_decay = sb("base_decay", [P, LAYERS, KC])
        decay = sb("decay", [P, LAYERS, SEGS])
        nf = sb("nf", [P, T])
        nb = sb("nb", [P, T])
        num = sb("num", [P, T])
        df = sb("df", [P, T])
        db = sb("db", [P, T])
        rden = sb("rden", [P, T])
        routers = sb("routers", [P, 3, KC, E])
        router3 = sb("router3", [P, KC, E3 + 1])
        bias = sb("bias", [P, 2, C])
        biasp = sb("biasp", [P, 2, 3, C], BF16)
        biasr = sb("biasr", [P, 2, C])
        b1 = sb("b1", [P, CH2])
        b1_col = sb("b1_col", [P, 2])
        wring = sb("wring", [P, 2, 3 * C])
        act_h = sb("act_h", [P, 2, HALF])
        prod_h = sb("prod_h", [P, 2, HALF])
        hid = sb("hid", [P, 2, KC, HALF])
        gates = sb("gates", [P, TT, E + 1])
        g3 = sb("g3", [P, TT, P], BF16)
        gT = sb("gT", [P, N], BF16)
        lg = sb("lg", [P, TT, E3 + 1])
        mx = sb("mx", [P, TT, 8])
        ix = sb("ix", [P, TT, 8], U32)
        ixf = sb("ixf", [P, K3, TT])
        small = sb("small", [P, 8, TT])
        oh = sb("oh", [P, K3, TT, E3])
        ohb = sb("ohb", [P, 2 * TT, E], BF16)
        r1 = sb("r1", [P, TT, E3])
        r2 = sb("r2", [P, TT, E3])
        r3 = sb("r3", [P, TT, E3])
        mask3 = sb("mask3", [P, TT, E3], BF16)
        tot = sb("tot", [P, E3 * TT])
        cum = sb("cum", [P, E3 * TT])
        tiles3 = sb("tiles3", [P, E3])
        tincl = sb("tincl", [P, E3])
        tbase = sb("tbase", [P, E3])
        ones60 = sb("ones60", [P, E3])
        te_f = sb("te_f", [P, 1])
        te_i = sb("te_i", [P, 1], I32)
        te_row = sb("te_row", [1, P], I32)
        rank_k = sb("rank_k", [P, K3, TT])
        base_k = sb("base_k", [P, K3, TT])
        rank_i = sb("rank_i", [P, 3, K3 * TT], I32)
        rank_f = sb("rank_f", [P, 3, K3 * TT])
        slot_f = sb("slot_f", [P, K3 * TT])
        slot_i = sb("slot_i", [P, K3 * TT], I32)
        tok_f = sb("tok_f", [P, P])
        tok_i = sb("tok_i", [P, P], I32)
        tok_col = sb("tok_col", [P, RING], I32)
        slot_cols = sb("slot_cols", [P, 2 * K3], I32)
        xg = sb("xg", [P, RING, C])
        xgT = sb("xgT", [P, 2, C])
        sg3 = sb("sg3", [P, 2, I1])
        h3 = sb("h3", [P, 2, I1])
        hT3 = sb("hT3", [IH, 2, 2 * P])
        o3 = sb("o3", [P, RING, C])

        w13 = [tile[:, :, :].rearrange("p c n -> p (c n)")[:, k * KC * 2 * I1:(k + 1) * KC * 2 * I1]
               for tile in (ek, ekv) for k in range(RING // 2)]
        w2 = euk[0:IH, 3].rearrange("p c (r n) -> p (c r) n", n=2 * C)

        yk = euk[:, 0, :, :].rearrange("p c (k t) -> p (c k) t", t=C)
        fin = euk[:, 1, :, :].rearrange("p c (k t) -> p (c k) t", t=C)
        y_tok = euk[:, 2, :, :].rearrange("p c (k t) -> p (c k) t", t=C)

        def onehot_place(tile):
            return tile.rearrange("p c n -> p (c n)").bitcast(BF16).rearrange("p (k m) -> p k m", m=P)

        in_tile, of_tile, of_tile_t = onehot_place(cnum[:, 0]), onehot_place(cnum[:, 1]), onehot_place(ekr[:, :, :])

        ps_acc = ctx.enter_context(nc.psum_tensor("ps_acc", [P, KC, N], F32))
        ps_g = ctx.enter_context(nc.psum_tensor("ps_g", [P, HALF], F32))
        ps_u = ctx.enter_context(nc.psum_tensor("ps_u", [P, HALF], F32))
        ps_w = ctx.enter_context(nc.psum_tensor("ps_w", [P, HALF], F32))
        ps_m = ctx.enter_context(nc.psum_tensor("ps_m", [P, HALF], F32))
        ps_wb = ps_w[:, :].bitcast(BF16)

        in_cond, in_w, in_kv, in_x = sem("in_cond"), sem("in_w"), sem("in_kv"), sem("in_x")
        in_const = sem("in_const")
        tf_sum, tf_sig, tf_ready = sem("tf_sum"), sem("tf_sig"), sem("tf_ready")
        dec_act, dec_ready = sem("dec_act"), sem("dec_ready")
        kmin, ek_ready, ekv_ready, ukmin, euk_ready = (sem("kmin"), sem("ek_ready"), sem("ekv_ready"),
                                                       sem("ukmin"), sem("euk_ready"))
        c_step, m_step = sem("c_step"), sem("m_step")
        b1_ready = sem("b1_ready")
        x_upd, y_sig, y_ready = sem("x_upd"), sem("y_sig"), sem("y_ready")
        lg_done = sem("lg_done")
        dve_step = sem("dve_step")
        bias_zero, bias_in, bias_split = sem("bias_zero"), sem("bias_in"), sem("bias_split")
        exp_in, exp_out = sem("exp_in"), sem("exp_out")
        rank_in, rank_done = sem("rank_in"), sem("rank_done")
        gate_split, gT_ps, gT_ready = sem("gate_split"), sem("gT_ps"), sem("gT_ready")

        class Ffn:

            def __init__(self, name, chunks):
                self.n = chunks
                self.w_in = [sem(f"{name}_w_in0"), sem(f"{name}_w_in1")]
                self.g_done = sem(f"{name}_g_done")
                self.u_done = sem(f"{name}_u_done")
                self.w_done = sem(f"{name}_w_done")
                self.g_read = sem(f"{name}_g_read")
                self.u_read = sem(f"{name}_u_read")
                self.h_ready = sem(f"{name}_h_ready")
                self.h_used = sem(f"{name}_h_used")

        f0, f1, f2, f3 = Ffn("f0", E), Ffn("f1", CH1), Ffn("f2", CH2), Ffn("f3", CH3)
        ffns = [f0, f1, f2, f3]

        yt_ps, yt_sb, yt_out = sem("yt_ps"), sem("yt_sb"), sem("yt_out")
        te_ready, te_out, te_in = sem("te_ready"), sem("te_out"), sem("te_in")
        onehots, tok_ps, tok_ready = sem("onehots"), sem("tok_ps"), sem("tok_ready")
        sgate_in, sgate_out = sem("sgate_in"), sem("sgate_out")
        w_tile = [sem(f"w_tile{r}") for r in range(RING)]
        x_tile = [sem(f"x_tile{r}") for r in range(RING)]
        o_tile = [sem(f"o_tile{r}") for r in range(RING)]
        tcol, xt_ps, xt_sb = sem("tcol"), sem("xt_ps"), sem("xt_sb")
        gu_ps, sg_sb, h_sb = sem("gu_ps"), sem("sg_sb"), sem("h_sb")
        ht_ps, ht_sb, o_ps, o_sb = sem("ht_ps"), sem("ht_sb"), sem("o_ps"), sem("o_sb")
        yk_in = [sem(f"yk_in{r}") for r in range(8)]
        x_final, xo_ps, fin_ready, out_done = sem("x_final"), sem("xo_ps"), sem("fin_ready"), sem("out_done")
        scol, comb_step = sem("scol"), sem("comb_step")

        block = ctx.enter_context(nc.Block())

        def over_pairs(eng, n, body, last_peeled=False):
            looped = n // 2 - (1 if last_peeled and n % 2 == 0 else 0)
            body(0, 0)
            body(1, 1)
            with eng.Fori(1, looped) as i:
                body(2 * i, 0)
                body(2 * i + 1, 1)
            for j in range(2 * looped, n):
                body(j, j % 2)

        def seg(tile, s):
            return tile.rearrange("p c (b t) -> p (c b) t", t=T)[:, bass.ds(s, 1), :].rearrange("p a t -> p (a t)")

        QUARTERS = [(c, h) for h in range(2) for c in range(KC)]

        def quarter(tile, c, h):
            return tile[:, c, h * HALF:(h + 1) * HALF]

        @block.sync
        def _(sp):
            sp.dma_start(cond[:, :, :], t["cond"].rearrange("b d -> (b d)").partition_broadcast(P)
                         .rearrange("p (b d) -> p b d", b=B)).then_inc(in_cond, 16)
            sp.dma_start(wu[:, :, :, :], t["wu"]).then_inc(in_w, 16)
            sp.dma_start(kv[:, :, :], t["kvT"]).then_inc(in_kv, 16)
            sp.dma_start(ekvr[:, :, :], t["kvrT"]).then_inc(in_kv, 16)
            sp.dma_start(xT[:, :, :], t["xT"]).then_inc(in_x, 16)
            consts = [(ident, "ident"), (identb, "identb"), (tri, "tri"), (sel, "sel"), (iota, "iota"),
                      (pcol, "pcol"), (scanmask1, "scanmask1"), (scanmask3, "scanmask3"), (tbl8, "tbl8"),
                      (routers, "routers"), (router3, "router3"), (b1, "b1")]
            for tile, name in consts:
                sp.dma_start(tile[:], t[name]).then_inc(in_const, 16)
            sp.wait_ge(bias_zero, 1)
            for part in range(3):
                r = part * GCOLS
                sp.dma_start(bias[r:r + E, 0, :], t["be"]).then_inc(bias_in, 16)
                sp.dma_start(bias[r:r + E + 1, 1, :], t["b2"]).then_inc(bias_in, 16)

            def load_chunks(f, src, width):
                def body(j, slot):
                    if not (isinstance(j, int) and j < 2):
                        sp.wait_ge(f.h_used, 2 * j - 2)
                    sp.dma_start(wring[:, slot, 0:width],
                                 src[bass.ds(j * P, P), :]).then_inc(f.w_in[slot], 16)
                over_pairs(sp, f.n, body)

            load_chunks(f0, t["we"], KC * C)
            sp.wait_ge(f0.h_used, 2 * f0.n)
            load_chunks(f1, t["w_l1"], 3 * C)
            sp.wait_ge(f1.h_used, 2 * f1.n)
            load_chunks(f2, t["w_l2"], 2 * C)

            sp.wait_ge(yt_sb, 4)
            sp.dma_start(t["y_rows"].rearrange("(k p) c -> p k c", p=P), y_tok[:, :, :]).then_inc(yt_out, 16)
            sp.wait_ge(te_ready, 1)
            sp.dma_start(t["te"], te_i[:, :]).then_inc(te_out, 16)
            sp.wait_ge(te_out, 16)
            sp.dma_start(te_row[:, :], t["te"].rearrange("p a -> a p")).then_inc(te_in, 16)
            sp.wait_ge(te_in, 16)

            def load_tile(j, r):
                if not (isinstance(j, int) and j < RING):
                    sp.wait_ge(o_ps, j - RING + 1)
                e = sp.value_load(te_row[0:1, bass.ds(j, 1)], min_val=0, max_val=E3 - 1)
                sp.dma_start(w13[r], t["w13"][bass.ds(e * P, P), :]).then_inc(w_tile[r], 16)
                sp.dma_start(w2[:, r, :], t["w2"][bass.ds(e * IH, IH), :]).then_inc(w_tile[r], 16)

            def store_tile(j, r):
                sp.wait_ge(o_sb, j + 1)
                sp.dma_start(t["o_rows"][bass.ds(j * P, P), :], o3[:, r, :]).then_inc(o_tile[r], 16)

            for j in range(RING):
                load_tile(j, j)
            n_loop = (MAXTILES - RING) // RING
            with sp.Fori(0, n_loop) as i:
                for r in range(RING):
                    store_tile(RING * i + r, r)
                    load_tile(RING * i + RING + r, r)
            for j in range(RING * n_loop, MAXTILES):
                store_tile(j, j % RING)
                if j + RING < MAXTILES:
                    load_tile(j + RING, j % RING)

            load_chunks(f3, t["w_sh"], 3 * C)
            with sp.Fori(0, TT) as i:
                sp.wait_ge(fin_ready, i + 1)
                sp.dma_start(t["out"][bass.ds(i * P, P), :],
                             fin[:, bass.ds(i, 1), :].rearrange("p a c -> p (a c)")).then_inc(out_done, 16)
            sp.wait_ge(out_done, 16 * TT)

        @block.tensor
        def _(pe):
            mm = nc.tensor.matmul
            pe.wait_ge(in_const, 16 * 12)

            def router(l, w, n):
                pe.wait_ge(y_ready, 4 * (l + 1))
                for k in range(TT):
                    for c in range(KC):
                        last = mm(ps_m[:, k * n:(k + 1) * n], yT[:, c, k * P:(k + 1) * P], w[:, c, :],
                                  start=(c == 0), stop=(c == KC - 1))
                last.then_inc(lg_done, 1)

            def turn_gates(l):
                pe.wait_ge(gate_split, l + 1)
                for k in range(TT):
                    last = nc.tensor.transpose(ps_wb[:, k * P:(k + 1) * P], g3[:, k, :], identb[:, :])
                last.then_inc(gT_ps, 1)
                pe.wait_ge(gT_ready, l + 1)

            def add_bias(b):
                for c in range(KC):
                    for h in range(2):
                        for part in range(3):
                            mm(quarter(ps_acc, c, h), biasp[:, b, part, c * P:(c + 1) * P],
                               gT[:, h * HALF:(h + 1) * HALF], start=(part == 0), stop=False)

            def spread(f, q, row, h):
                if not (isinstance(q, int) and q < 1):
                    pe.wait_ge(f.h_ready, q)
                mm(ps_w[:, :], sel[:, bass.ds(row, 1), :].rearrange("p a m -> p (a m)"),
                   gT[:, h * HALF:(h + 1) * HALF], start=True, stop=True).then_inc(f.w_done, 1)

            router(0, routers[:, 0], E)
            turn_gates(0)
            pe.wait_ge(bias_split, 1)
            add_bias(0)
            spread(f0, 0, 0, 0)

            def layer0(e, slot):
                for h in range(2):
                    q = 2 * e + h
                    if h == 0:
                        spread(f0, q + 1, e, 1)
                    elif not (isinstance(e, int) and e == E - 1):
                        spread(f0, q + 1, e + 1, 0)
                    if h == 0:
                        pe.wait_ge(f0.w_in[slot], 8 * e + (16 - 8 * slot))
                    pe.wait_ge(f0.h_ready, q + 1)
                    for c in range(KC):
                        for k in range(KC):
                            last = mm(quarter(ps_acc, c, h), wring[:, slot, k * C + c * P:k * C + (c + 1) * P],
                                      hid[:, h, k, :], start=False,
                                      stop=(k == KC - 1 and isinstance(e, int) and e == E - 1))
                    last.then_inc(f0.h_used, 1)

            over_pairs(pe, E, layer0, last_peeled=True)

            def gated(f, has_up, row_of, opened):
                def down(q, j, slot, h, last_one):
                    pe.wait_ge(f.h_ready, q + 1)
                    off = (2 if has_up else 1) * C
                    first = isinstance(j, int) and j == 0 and not opened
                    for c in range(KC):
                        last = mm(quarter(ps_acc, c, h), wring[:, slot, off + c * P:off + (c + 1) * P],
                                  hid[:, h, 0, :], start=first, stop=last_one)
                    last.then_inc(f.h_used, 1)

                def body(j, slot):
                    for h in range(2):
                        q = 2 * j + h
                        start = isinstance(q, int) and q < 1
                        if h == 0:
                            pe.wait_ge(f.w_in[slot], 8 * j + (16 - 8 * slot))
                        if not start:
                            pe.wait_ge(f.g_read, q)
                        for k in range(KC):
                            last = mm(ps_g[:, :], wring[:, slot, k * P:(k + 1) * P],
                                      yT[:, k, h * HALF:(h + 1) * HALF], start=(k == 0), stop=(k == KC - 1))
                        last.then_inc(f.g_done, 1)
                        if has_up:
                            if not start:
                                pe.wait_ge(f.u_read, q)
                            for k in range(KC):
                                last = mm(ps_u[:, :], wring[:, slot, C + k * P:C + (k + 1) * P],
                                          yT[:, k, h * HALF:(h + 1) * HALF], start=(k == 0), stop=(k == KC - 1))
                            last.then_inc(f.u_done, 1)
                        spread(f, q, row_of(j), h)
                        if not start:
                            down(q - 1, j if h else j - 1, slot if h else 1 - slot, 1 - h,
                                 isinstance(q, int) and q == 2 * f.n - 1)
                n = f.n
                over_pairs(pe, n, body, last_peeled=True)
                down(2 * n - 1, n - 1, (n - 1) % 2, 1, True)

            router(1, routers[:, 1], E)
            pe.wait_ge(rank_in, 1)
            mm(ps_g[:, 0:2 * TT * E], tri[:, 0, :], ohb[:, :, :].rearrange("p k e -> p (k e)"), start=True, stop=True)
            mm(ps_u[:, 0:2 * TT * E], tri[:, 2, :], ohb[:, :, :].rearrange("p k e -> p (k e)"),
               start=True, stop=True).then_inc(rank_done, 1)
            turn_gates(1)
            gated(f1, True, lambda j: j + E, False)

            router(2, routers[:, 2], E)
            turn_gates(2)
            add_bias(1)
            gated(f2, False, lambda j: j + (E + CH1), True)

            router(3, router3, E3 + 1)
            for k in range(TT):
                for c in range(KC):
                    last = nc.tensor.transpose(ps_acc[:, k // 4, (k % 4) * C + c * P:(k % 4) * C + (c + 1) * P],
                                               yT[:, c, k * P:(k + 1) * P], ident[:, :])
                if k % 2:
                    last.then_inc(yt_ps, 1)
            pe.wait_ge(rank_in, 2)
            mm(ps_g[:, 0:TT * E3], tri[:, 1, :], mask3[:, :, :].rearrange("p k e -> p (k e)"), start=True, stop=True)
            mm(ps_u[:, 0:TT * E3], tri[:, 2, :], mask3[:, :, :].rearrange("p k e -> p (k e)"),
               start=True, stop=True).then_inc(rank_done, 1)
            turn_gates(3)
            pe.wait_ge(onehots, 1)
            for k in range(K3 * TT):
                mm(ps_m[:, 0:P], in_tile[:, k, :], of_tile[:, k, :], start=(k == 0), stop=(k == K3 * TT - 1))
            for k in range(K3 * TT):
                last = mm(ps_m[:, P:2 * P], in_tile[:, k, :], of_tile_t[:, k, :], start=(k == 0),
                          stop=(k == K3 * TT - 1))
            last.then_inc(tok_ps, 1)
            pe.wait_ge(tok_ready, 1)

            xt_bank = [ps_acc[:, 0, 0:C], ps_acc[:, 0, HALF:HALF + C]]
            gu_bank = [ps_acc[:, 1, 0:2 * I1], ps_acc[:, 1, HALF:HALF + 2 * I1]]
            ht_bank = [ps_g[0:IH, 0:2 * P], ps_u[0:IH, 0:2 * P]]
            o_bank = [ps_w[:, 0:C], ps_m[:, 0:C]]

            def known(j, least):
                return isinstance(j, int) and j < least

            def turn_x(j, r, lap):
                pe.wait_ge(x_tile[r], 16 * lap + 16)
                if not known(j, 2):
                    pe.wait_ge(xt_sb, j - 1)
                for c in range(KC):
                    last = nc.tensor.transpose(xt_bank[r % 2][:, c * P:(c + 1) * P],
                                               xg[:, r, c * P:(c + 1) * P], ident[:, :])
                last.then_inc(xt_ps, 1)

            def gate_up(j, r, lap):
                pe.wait_ge(w_tile[r], 32 * lap + 32)
                pe.wait_ge(xt_sb, j + 1)
                if not known(j, 2):
                    pe.wait_ge(h_sb, j - 1)
                for c in range(KC):
                    last = mm(gu_bank[r % 2], xgT[:, r % 2, c * P:(c + 1) * P],
                              w13[r][:, c * 2 * I1:(c + 1) * 2 * I1], start=(c == 0), stop=(c == KC - 1))
                last.then_inc(gu_ps, 1)

            def turn_h(j, r):
                pe.wait_ge(h_sb, j + 1)
                if not known(j, 2):
                    pe.wait_ge(ht_sb, j - 1)
                for c in range(2):
                    last = nc.tensor.transpose(ht_bank[r % 2][:, c * P:(c + 1) * P],
                                               h3[:, r % 2, c * IH:(c + 1) * IH], ident[:, :])
                last.then_inc(ht_ps, 1)

            def down3(j, r):
                pe.wait_ge(ht_sb, j + 1)
                if not known(j, 2):
                    pe.wait_ge(o_sb, j - 1)
                for c in range(2):
                    last = mm(o_bank[r % 2], hT3[:, r % 2, c * P:(c + 1) * P],
                              w2[:, r, c * C:(c + 1) * C], start=(c == 0), stop=(c == 1))
                last.then_inc(o_ps, 1)

            def tile_step(j, r, lap):
                static = isinstance(j, int)
                if not static or j + 1 < MAXTILES:
                    turn_x(j + 1, (r + 1) % RING, lap + (r + 1) // RING)
                if not static or j < MAXTILES:
                    gate_up(j, r, lap)
                if not static or 0 <= j - 2 < MAXTILES:
                    down3(j - 2, (r - 2) % RING)
                if not static or 0 <= j - 1 < MAXTILES:
                    turn_h(j - 1, (r - 1) % RING)

            turn_x(0, 0, 0)
            for j in range(RING):
                tile_step(j, j, 0)
            n_loop = (MAXTILES - 1) // RING
            with pe.Fori(1, n_loop) as i:
                for r in range(RING):
                    tile_step(RING * i + r, r, i)
            for j in range(RING * n_loop, MAXTILES + 2):
                tile_step(j, j % RING, j // RING)

            pe.wait_ge(o_sb, MAXTILES)
            gated(f3, True, lambda j: E + CH1 + CH2, False)

            pe.wait_ge(x_final, 4)
            for k in range(TT):
                if k >= 2:
                    pe.wait_ge(fin_ready, k - 1)
                for c in range(KC):
                    last = nc.tensor.transpose([ps_g, ps_u][k % 2][:, c * P:(c + 1) * P],
                                               xT[:, c, k * P:(k + 1) * P], ident[:, :])
                last.then_inc(xo_ps, 1)

        @block.scalar
        def _(act):
            fn = nc.scalar.activation
            act.wait_ge(in_const, 16 * 12)
            act.wait_ge(in_w, 16)
            fn(ew[:, :, :], wu[:, 0], ACT.Exp).then_inc(dec_act, 1)
            act.wait_ge(dec_act, 1)
            fn(base_decay[:, :, :], ew[:, :, :], ACT.Exp, scale=-1.0).then_inc(dec_act, 1)
            act.wait_ge(kmin, 2)
            fn(ek[:, :, :], ek[:, :, :], ACT.Exp).then_inc(ek_ready, 1)
            fn(ekr[:, :, :], ekr[:, :, :], ACT.Exp).then_inc(ek_ready, 1)
            for l in range(LAYERS):
                act.wait_ge(ukmin, l + 1)
                fn(euk[:, l], euk[:, l], ACT.Exp).then_inc(euk_ready, 1)
            act.wait_ge(tf_sum, 1)
            fn(tf[:, :], tf[:, :], ACT.Sigmoid).then_inc(tf_sig, 1)

            def input_sigmoid(l):
                if l == 0:
                    act.wait_ge(in_x, 16)
                for n, (c, h) in enumerate(QUARTERS):
                    if l:
                        act.wait_ge(x_upd, 4 * (l - 1) + n + 1)
                    fn(quarter(yT, c, h), quarter(xT, c, h), ACT.Sigmoid).then_inc(y_sig, 1)

            def softmax_exp(n, tile):
                act.wait_ge(exp_in, n)
                fn(tile, tile, ACT.Exp).then_inc(exp_out, 1)

            def copy_gT(l):
                act.wait_ge(gT_ps, l + 1)
                nc.scalar.copy(gT[:, :], ps_wb).then_inc(gT_ready, 1)

            def activate(f, func, bias_of, skip_u):
                def body(j, slot):
                    if bias_of:
                        nc.scalar.copy(b1_col[:, slot:slot + 1], b1[:, bass.ds(j, 1)]).then_inc(b1_ready, 1)
                    for h in range(2):
                        q = 2 * j + h
                        act.wait_ge(f.g_done, q + 1)
                        if not (isinstance(q, int) and q < 2):
                            act.wait_ge(f.h_ready if skip_u else f.u_read, q - 1)
                        kw = {}
                        if bias_of:
                            act.wait_ge(b1_ready, j + 1)
                            kw = {"bias": b1_col[:, slot:slot + 1]}
                        fn(act_h[:, h, :], ps_g[:, :], func, **kw).then_inc(f.g_read, 1)
                over_pairs(act, f.n, body)

            input_sigmoid(0)
            softmax_exp(1, small[:, 0, :])
            copy_gT(0)
            input_sigmoid(1)
            softmax_exp(2, lg[:, :, 0:E])
            copy_gT(1)
            activate(f1, ACT.Silu, False, False)
            input_sigmoid(2)
            softmax_exp(3, small[:, 0, :])
            copy_gT(2)
            activate(f2, ACT.Gelu, True, True)
            input_sigmoid(3)
            for k in range(4):
                act.wait_ge(yt_ps, k + 1)
                nc.scalar.copy(y_tok[:, 2 * k:2 * k + 2, :].rearrange("p k c -> p (k c)"),
                               ps_acc[:, k // 2, (k % 2) * HALF:(k % 2 + 1) * HALF]).then_inc(yt_sb, 1)
            act.wait_ge(sgate_in, 1)
            fn(gates[:, :, 0], small[:, 7, :], ACT.Sigmoid).then_inc(sgate_out, 1)
            softmax_exp(4, lg[:, :, 0:E3])
            copy_gT(3)

            xt_bank = [ps_acc[:, 0, 0:C], ps_acc[:, 0, HALF:HALF + C]]
            gu_bank = [ps_acc[:, 1, 0:2 * I1], ps_acc[:, 1, HALF:HALF + 2 * I1]]
            o_bank = [ps_w[:, 0:C], ps_m[:, 0:C]]

            def tile_step(j, r):
                static = isinstance(j, int)
                if not static or j + 1 < MAXTILES:
                    act.wait_ge(xt_ps, j + 2)
                    if not (static and j + 1 < 2):
                        act.wait_ge(gu_ps, j)
                    nc.scalar.copy(xgT[:, (r + 1) % 2, :], xt_bank[(r + 1) % 2]).then_inc(xt_sb, 1)
                if not static or j < MAXTILES:
                    act.wait_ge(gu_ps, j + 1)
                    if not (static and j < 2):
                        act.wait_ge(h_sb, j - 1)
                    fn(sg3[:, r % 2, :], gu_bank[r % 2][:, 0:I1], ACT.Silu).then_inc(sg_sb, 1)
                if not static or 0 <= j - 2 < MAXTILES:
                    act.wait_ge(o_ps, j - 1)
                    if not (static and j - 2 < RING):
                        act.wait_ge(o_tile[(r - 2) % RING], (4 * (j - (2 + (r - 2) % RING))))
                    nc.scalar.copy(o3[:, (r - 2) % RING, :], o_bank[r % 2]).then_inc(o_sb, 1)

            act.wait_ge(xt_ps, 1)
            act.wait_ge(tok_ready, 1)
            nc.scalar.copy(xgT[:, 0, :], xt_bank[0]).then_inc(xt_sb, 1)
            for j in range(2 + RING):
                tile_step(j, j % RING)
            n_loop = (MAXTILES - 3 - RING) // RING
            with act.Fori(0, n_loop) as i:
                for k in range(RING):
                    tile_step(RING * i + (2 + RING + k), (2 + k) % RING)
            for j in range(2 + RING + RING * n_loop, MAXTILES + 2):
                tile_step(j, j % RING)
            activate(f3, ACT.Silu, False, False)

        @block.gpsimd
        def _(pool):
            for l in range(LAYERS):
                pool.wait_ge(euk_ready, l + 1)
                if l == 0:
                    pool.wait_ge(ek_ready, 1)
                if l >= 2:
                    pool.wait_ge(m_step, M_STEPS * SEGS * (l - 1))
                nc.gpsimd.tensor_tensor(euk[:, l], euk[:, l], ek[:, :, :], ALU.subtract).then_inc(c_step, 1)
                pool.wait_ge(c_step, 2 * l + 1)
                nc.gpsimd.tensor_tensor(cnum[:, l % 2], euk[:, l], kv[:, :, :], ALU.mult).then_inc(c_step, 1)

            pool.wait_ge(tok_ready, 1)
            pool.wait_ge(yt_out, 16)

            def gather(j, r):
                if not (isinstance(j, int) and j < RING):
                    pool.wait_ge(xt_ps, j - RING + 1)
                nc.gpsimd.tensor_copy(tok_col[:, r:r + 1], tok_i[:, bass.ds(j, 1)]).then_inc(tcol, 1)
                pool.wait_ge(tcol, j + 1)
                pool.nop(nofuse=True)
                nc.gpsimd.indirect_dma_start(
                    xg[:, r, :], None, t["y_rows"],
                    bass.IndirectOffsetOnAxis(ap=tok_col[:, r:r + 1], axis=0)).then_inc(x_tile[r], 16)
            for j in range(RING):
                gather(j, j)
            n_loop = MAXTILES // RING
            with pool.Fori(1, n_loop) as i:
                for r in range(RING):
                    gather(RING * i + r, r)
            for j in range(RING * n_loop, MAXTILES):
                gather(j, j % RING)

            for r in range(RING):
                pool.wait_ge(o_tile[r], 16 * len(range(r, MAXTILES, RING)))

            def gather_back(k, par):
                if not (isinstance(k, int) and k < 2):
                    pool.wait_ge(comb_step, K3 * k - K3)
                nc.gpsimd.tensor_copy(
                    slot_cols[:, par * K3:(par + 1) * K3],
                    slot_i[:, :].rearrange("p (k t) -> p t k", k=K3)[:, bass.ds(k, 1), :]
                    .rearrange("p a k -> p (a k)")).then_inc(scol, 1)
                pool.wait_ge(scol, k + 1)
                pool.nop(nofuse=True)
                for c in range(K3):
                    s = par * K3 + c
                    nc.gpsimd.indirect_dma_start(
                        yk[:, s, :], None, t["o_rows"],
                        bass.IndirectOffsetOnAxis(ap=slot_cols[:, s:s + 1], axis=0)).then_inc(yk_in[s], 16)

            over_pairs(pool, TT, gather_back)

        @block.vector
        def _(dve):
            v = nc.vector
            n_steps = [0]

            def link(ins):
                n_steps[0] += 1
                ins.then_inc(dve_step, 1)
                dve.wait_ge(dve_step, n_steps[0])

            def go(ins):
                n_steps[0] += 1
                ins.then_inc(dve_step, 1)

            def split(hi, mid, lo, whole, rest, done):
                link(v.tensor_copy(hi, whole))
                link(v.tensor_tensor(rest, whole, hi, ALU.subtract))
                link(v.tensor_copy(mid, rest))
                link(v.tensor_tensor(rest, rest, mid, ALU.subtract))
                v.tensor_copy(lo, rest).then_inc(done, 1)

            dve.wait_ge(in_kv, 32)
            v.tensor_scalar(ek[:, :, :], kv[:, :, :], 30.0, None, ALU.min).then_inc(kmin, 1)
            v.tensor_scalar(ekr[:, :, :], ekvr[:, :, :], 30.0, None, ALU.min).then_inc(kmin, 1)
            dve.wait_ge(in_w, 16)
            for l in range(LAYERS):
                for c in range(KC):
                    ins = v.tensor_scalar(euk[:, l, c], kv[:, c], wu[:, 1, l, c:c + 1], 30.0, ALU.add, ALU.min)
                ins.then_inc(ukmin, 1)
            dve.wait_ge(in_cond, 16)
            v.tensor_reduce(tf[:, :], cond[:, :, :], AX.X, ALU.add).then_inc(tf_sum, 1)
            go(v.memset(g3[:, :, :], 0.0))
            go(v.memset(gates[:, :, :], 1.0))
            go(v.memset(ones60[:, :], 1.0))
            v.memset(bias[:, :, :], 0.0).then_inc(bias_zero, 1)
            dve.wait_ge(tf_sig, 1)
            link(v.tensor_scalar(tfhalf[:, :], tf[:, :], 0.5, 0.5, ALU.mult, ALU.add))
            link(v.tensor_scalar(tfout[:, :], tf[:, :], 0.2, 0.8, ALU.mult, ALU.add))
            dve.wait_ge(dec_act, 2)
            for l in range(LAYERS):
                for c in range(KC):
                    link(v.tensor_scalar(decay[:, l, c * B:(c + 1) * B], tfhalf[:, :], base_decay[:, l, c:c + 1],
                                         None, ALU.mult))
            dve.wait_ge(ek_ready, 2)
            go(v.tensor_tensor(ekv[:, :, :], ek[:, :, :], kv[:, :, :], ALU.mult))
            link(v.tensor_tensor(ekvr[:, :, :], ekr[:, :, :], ekvr[:, :, :], ALU.mult))

            def numerator(l, s, n):
                dec = decay[:, l, bass.ds(s, 1)].to_broadcast([P, T])
                v.tensor_tensor_scan(nf[:, :], dec, seg(ekv, s), 0.0, ALU.mult, ALU.add).then_inc(m_step, 1)
                v.tensor_tensor_scan(nb[:, ::-1], dec, seg(ekvr, s), 0.0, ALU.mult, ALU.add).then_inc(m_step, 1)
                dve.wait_ge(m_step, n + 2)
                v.tensor_tensor(nf[:, :], nf[:, :], nb[:, :], ALU.add).then_inc(m_step, 1)
                dve.wait_ge(m_step, n + 3)
                v.tensor_tensor(num[:, :], nf[:, :], seg(cnum[:, l % 2], s), ALU.add).then_inc(m_step, 1)

            def denominator(l, s, n):
                dec = decay[:, l, bass.ds(s, 1)].to_broadcast([P, T])
                v.tensor_tensor_scan(df[:, :], dec, seg(ek, s), 0.0, ALU.mult, ALU.add).then_inc(m_step, 1)
                v.tensor_tensor_scan(db[:, ::-1], dec, seg(ekr, s), 0.0, ALU.mult, ALU.add).then_inc(m_step, 1)
                dve.wait_ge(m_step, n + 6)
                v.tensor_tensor(df[:, :], df[:, :], db[:, :], ALU.add).then_inc(m_step, 1)
                dve.wait_ge(m_step, n + 7)
                v.tensor_tensor(df[:, :], df[:, :], seg(euk[:, l], s), ALU.add).then_inc(m_step, 1)
                dve.wait_ge(m_step, n + 8)
                v.tensor_scalar(df[:, :], df[:, :], 1e-8, None, ALU.max).then_inc(m_step, 1)
                dve.wait_ge(m_step, n + 9)
                v.reciprocal(rden[:, :], df[:, :]).then_inc(m_step, 1)
                dve.wait_ge(m_step, n + 10)
                v.scalar_tensor_tensor(seg(mix, s), num[:, :], tfout8[:, bass.ds(s, 1)], rden[:, :],
                                       ALU.mult, ALU.mult).then_inc(m_step, 1)

            for c in range(KC):
                link(v.tensor_copy(tfout8[:, c * B:(c + 1) * B], tfout[:, :]))
            dve.wait_ge(c_step, 2)
            with dve.Fori(0, SEGS) as s:
                numerator(0, s, M_STEPS * s)
                denominator(0, s, M_STEPS * s)

            dve.wait_ge(bias_in, 16 * 6)
            split(biasp[:, :, 0], biasp[:, :, 1], biasp[:, :, 2], bias[:, :, :], biasr[:, :, :], bias_split)

            def input_of(l, prev):
                if prev is not None:
                    dve.wait_ge(prev.h_used, 2 * prev.n)
                    for c, h in QUARTERS:
                        v.tensor_tensor(quarter(xT, c, h), quarter(xT, c, h), quarter(ps_acc, c, h),
                                        ALU.add).then_inc(x_upd, 1)
                dve.wait_ge(m_step, M_STEPS * SEGS * (l + 1))
                for n, (c, h) in enumerate(QUARTERS):
                    dve.wait_ge(y_sig, 4 * l + n + 1)
                    v.tensor_tensor(quarter(yT, c, h), quarter(yT, c, h), quarter(mix, c, h),
                                    ALU.mult).then_inc(y_ready, 1)

            def top8(values, n_exp):
                for k in range(TT):
                    (go if k < TT - 1 else link)(v.max(mx[:, k, :], values[:, k, :]))
                for k in range(TT):
                    (go if k < TT - 1 else link)(v.max_index(ix[:, k, :], mx[:, k, :], values[:, k, :]))

            def one_hots(choices, n_exp):
                for k in range(choices):
                    (go if k < choices - 1 else link)(v.tensor_copy(ixf[:, k, :], ix[:, :, k]))
                for k in range(choices):
                    (go if k < choices - 1 else link)(v.tensor_tensor(
                        oh[:, k, :, 0:n_exp], iota[:, 0:n_exp].unsqueeze(1).broadcast_to([P, TT, n_exp]),
                        ixf[:, k, :].unsqueeze(2).broadcast_to([P, TT, n_exp]), ALU.is_equal))

            def split_gates(l, n):
                split(g3[:, :, 0:n], g3[:, :, GCOLS:GCOLS + n], g3[:, :, 2 * GCOLS:2 * GCOLS + n],
                      gates[:, :, 0:n], r1[:, :, 0:n], gate_split)

            def weigh(out, k, w, n_exp):
                return v.tensor_tensor(out, oh[:, k, :, 0:n_exp], w.unsqueeze(2).broadcast_to([P, TT, n_exp]),
                                       ALU.mult)

            def route_top2(l, n_exp_round):
                dve.wait_ge(lg_done, l + 1)
                link(v.tensor_copy(lg[:, :, 0:E], ps_m[:, 0:TT * E].rearrange("p (k e) -> p k e", e=E)))
                top8(lg[:, :, 0:E], E)
                v.tensor_tensor(small[:, 0, :], mx[:, :, 1], mx[:, :, 0], ALU.subtract).then_inc(exp_in, 1)
                one_hots(2, E)
                dve.wait_ge(exp_out, n_exp_round)
                link(v.tensor_scalar(small[:, 1, :], small[:, 0, :], 1.0, None, ALU.add))
                link(v.reciprocal(small[:, 2, :], small[:, 1, :]))
                link(v.tensor_tensor(small[:, 3, :], small[:, 0, :], small[:, 2, :], ALU.mult))
                go(weigh(r1[:, :, 0:E], 0, small[:, 2, :], E))
                link(weigh(r2[:, :, 0:E], 1, small[:, 3, :], E))
                link(v.tensor_tensor(gates[:, :, 0:E], r1[:, :, 0:E], r2[:, :, 0:E], ALU.add))
                split_gates(l, E + 1)

            def softmax(n_exp, n_exp_round):
                link(v.tensor_reduce(small[:, 0, :], lg[:, :, 0:n_exp], AX.X, ALU.max))
                v.tensor_tensor(lg[:, :, 0:n_exp], lg[:, :, 0:n_exp],
                                small[:, 0, :].unsqueeze(2).broadcast_to([P, TT, n_exp]),
                                ALU.subtract).then_inc(exp_in, 1)
                dve.wait_ge(exp_out, n_exp_round)
                link(v.tensor_reduce(small[:, 1, :], lg[:, :, 0:n_exp], AX.X, ALU.add))
                link(v.reciprocal(small[:, 2, :], small[:, 1, :]))
                link(v.tensor_tensor(lg[:, :, 0:n_exp], lg[:, :, 0:n_exp],
                                     small[:, 2, :].unsqueeze(2).broadcast_to([P, TT, n_exp]), ALU.mult))

            def mix_part(l, s, part):
                if part == 0:
                    numerator(l, s, M_STEPS * s + M_STEPS * SEGS * l)
                else:
                    denominator(l, s, M_STEPS * s + M_STEPS * SEGS * l)

            input_of(0, None)
            route_top2(0, 1)
            dve.wait_ge(c_step, 4)

            def weigh_input(e, slot):
                for h in range(2):
                    q = 2 * e + h
                    dve.wait_ge(f0.w_done, q + 1)
                    if not (isinstance(q, int) and q < 2):
                        dve.wait_ge(f0.h_used, q - 1)
                    v.tensor_tensor(hid[:, h, :, :], yT[:, :, h * HALF:(h + 1) * HALF],
                                    ps_w[:, :].unsqueeze(1).broadcast_to([P, KC, HALF]),
                                    ALU.mult).then_inc(f0.h_ready, 1)
                    mix_part(1, e, h)
            over_pairs(dve, E, weigh_input)

            def gated_units(f, has_up, l_mix):
                def body(j, slot, mixing):
                    for h in range(2):
                        q = 2 * j + h
                        dve.wait_ge(f.g_read, q + 1)
                        src = act_h[:, h, :]
                        if has_up:
                            dve.wait_ge(f.u_done, q + 1)
                            if not (isinstance(q, int) and q < 2):
                                dve.wait_ge(f.h_ready, q - 1)
                            v.tensor_tensor(prod_h[:, h, :], act_h[:, h, :], ps_u[:, :], ALU.mult).then_inc(f.u_read, 1)
                            dve.wait_ge(f.u_read, q + 1)
                            src = prod_h[:, h, :]
                        dve.wait_ge(f.w_done, q + 1)
                        if not (isinstance(q, int) and q < 2):
                            dve.wait_ge(f.h_used, q - 1)
                        v.tensor_tensor(hid[:, h, 0, :], src, ps_w[:, :], ALU.mult).then_inc(f.h_ready, 1)
                        if mixing is not None:
                            mix_part(l_mix, mixing, h)
                body(0, 0, None)
                body(1, 1, None)
                with dve.Fori(1, f.n // 2) as i:
                    for slot in range(2):
                        body(2 * i + slot, slot, None if l_mix is None else 2 * i + (slot - 2))
                if f.n % 2:
                    body(f.n - 1, 0, None)

            input_of(1, f0)
            dve.wait_ge(lg_done, 2)
            link(v.tensor_copy(lg[:, :, 0:E], ps_m[:, 0:TT * E].rearrange("p (k e) -> p k e", e=E)))
            softmax(E, 2)
            top8(lg[:, :, 0:E], E)
            one_hots(2, E)
            v.tensor_copy(ohb[:, :, :].rearrange("p (k t) e -> p k t e", k=2),
                          oh[:, 0:2, :, 0:E]).then_inc(rank_in, 1)
            for k in range(2):
                go(v.tensor_copy(small[:, 3 + k, :], mx[:, :, k]))
            dve.wait_ge(rank_done, 1)
            n1 = 2 * TT * E
            by_e = "p (k e) -> p e k"
            link(v.tensor_copy(tot[:, 0:n1].rearrange("p (e k) -> p e k", e=E), ps_u[:, 0:n1].rearrange(by_e, e=E)))
            link(v.tensor_tensor_scan(cum[:, 0:n1], scanmask1[:, :], tot[:, 0:n1], 0.0, ALU.mult, ALU.add))
            link(v.tensor_tensor(cum[:, 0:n1], cum[:, 0:n1], tot[:, 0:n1], ALU.subtract))
            link(v.tensor_tensor(cum[:, 0:n1].rearrange("p (e k) -> p e k", e=E),
                                 cum[:, 0:n1].rearrange("p (e k) -> p e k", e=E),
                                 ps_g[:, 0:n1].rearrange(by_e, e=E), ALU.add))
            link(v.tensor_scalar(cum[:, 0:n1], cum[:, 0:n1], float(CAP), None, ALU.is_le))
            for k in range(2):
                link(weigh([r1, r2][k][:, :, 0:E], k, small[:, 3 + k, :], E))
                link(v.tensor_tensor([r1, r2][k][:, :, 0:E], [r1, r2][k][:, :, 0:E],
                                     cum[:, 0:n1].rearrange("p (e k) -> p k e", e=E)[:, k * TT:(k + 1) * TT, :],
                                     ALU.mult))
            link(v.tensor_tensor(gates[:, :, 0:E], r1[:, :, 0:E], r2[:, :, 0:E], ALU.add))
            split_gates(1, E + 1)
            dve.wait_ge(c_step, 6)
            gated_units(f1, True, 2)

            input_of(2, f1)
            route_top2(2, 3)
            dve.wait_ge(c_step, 8)
            gated_units(f2, False, 3)

            input_of(3, f2)
            dve.wait_ge(lg_done, 4)
            link(v.tensor_copy(lg[:, :, :], ps_m[:, 0:TT * (E3 + 1)].rearrange("p (k e) -> p k e", e=E3 + 1)))
            v.tensor_copy(small[:, 7, :], lg[:, :, E3]).then_inc(sgate_in, 1)
            softmax(E3, 4)
            dve.wait_ge(sgate_out, 1)
            split_gates(3, 1)
            top8(lg[:, :, 0:E3], E3)
            for k in range(K3):
                go(v.tensor_copy(small[:, k, :], mx[:, :, k]))
            one_hots(K3, E3)
            link(v.tensor_tensor(r1[:, :, :], oh[:, 0], oh[:, 1], ALU.add))
            link(v.tensor_tensor(r2[:, :, :], oh[:, 2], oh[:, 3], ALU.add))
            v.tensor_tensor(mask3[:, :, :], r1[:, :, :], r2[:, :, :], ALU.add).then_inc(rank_in, 1)
            dve.wait_ge(rank_done, 2)
            link(v.tensor_copy(tot[:, :].rearrange("p (e k) -> p e k", e=E3),
                               ps_u[:, 0:TT * E3].rearrange("p (k e) -> p e k", e=E3)))
            link(v.tensor_tensor_scan(cum[:, :], scanmask3[:, :], tot[:, :], 0.0, ALU.mult, ALU.add))
            cume = cum[:, :].rearrange("p (e k) -> p e k", e=E3)
            link(v.tensor_tensor(r3[:, :, :].rearrange("p k e -> p (k e)").rearrange("p (e k) -> p e k", e=E3),
                                 cume[:, :, TT - 1:TT].broadcast_to([P, E3, TT]),
                                 tbl8[:, :].unsqueeze(1).broadcast_to([P, E3, TT]), ALU.is_gt))
            link(v.tensor_reduce(tiles3[:, :], r3[:, :, :].rearrange("p k e -> p (k e)")
                                 .rearrange("p (e k) -> p e k", e=E3), AX.X, ALU.add))
            link(v.tensor_tensor_scan(tincl[:, :], ones60[:, :], tiles3[:, :], 0.0, ALU.mult, ALU.add))
            link(v.tensor_tensor(tbase[:, :], tincl[:, :], tiles3[:, :], ALU.subtract))
            link(v.tensor_scalar(r3[:, 0, :], tincl[:, :], pcol[:, 0:1], None, ALU.is_le))
            link(v.tensor_reduce(te_f[:, :], r3[:, 0, :], AX.X, ALU.add))
            v.tensor_scalar(te_i[:, :], te_f[:, :], float(E3 - 1), None, ALU.min).then_inc(te_ready, 1)
            link(v.tensor_tensor(cum[:, :], cum[:, :], tot[:, :], ALU.subtract))
            link(v.tensor_tensor(r1[:, :, :], cum[:, :].rearrange("p (e k) -> p k e", e=E3),
                                 ps_g[:, 0:TT * E3].rearrange("p (k e) -> p k e", e=E3), ALU.add))
            for k in range(K3):
                link(v.tensor_tensor(r2[:, :, :], oh[:, k], r1[:, :, :], ALU.mult))
                link(v.tensor_reduce(rank_k[:, k, :], r2[:, :, :], AX.X, ALU.add))
                link(v.tensor_tensor(r2[:, :, :], oh[:, k], tbase[:, :].unsqueeze(1).broadcast_to([P, TT, E3]),
                                     ALU.mult))
                link(v.tensor_reduce(base_k[:, k, :], r2[:, :, :], AX.X, ALU.add))
            rk = rank_k[:, :, :].rearrange("p k t -> p (k t)")
            bk = base_k[:, :, :].rearrange("p k t -> p (k t)")
            link(v.tensor_copy(rank_i[:, 0, :], rk))
            go(v.tensor_scalar(rank_i[:, 1, :], rank_i[:, 0, :], 7, None, ALU.arith_shift_right))
            link(v.tensor_scalar(rank_i[:, 2, :], rank_i[:, 0, :], P - 1, None, ALU.bitwise_and))
            go(v.tensor_copy(rank_f[:, 1, :], rank_i[:, 1, :]))
            link(v.tensor_copy(rank_f[:, 2, :], rank_i[:, 2, :]))
            link(v.tensor_tensor(rank_f[:, 0, :], rank_f[:, 1, :], bk, ALU.add))
            link(v.scalar_tensor_tensor(slot_f[:, :], rank_f[:, 0, :], float(P), rank_f[:, 2, :],
                                        ALU.mult, ALU.add))
            link(v.tensor_copy(slot_i[:, :], slot_f[:, :]))
            kt = K3 * TT
            link(v.tensor_tensor(in_tile[:, :, :], iota[:, :].unsqueeze(1).broadcast_to([P, kt, P]),
                                 rank_f[:, 2, :].unsqueeze(2).broadcast_to([P, kt, P]), ALU.is_equal))
            link(v.tensor_tensor(of_tile_t[:, :, :], iota[:, :].unsqueeze(1).broadcast_to([P, kt, P]),
                                 rank_f[:, 0, :].unsqueeze(2).broadcast_to([P, kt, P]), ALU.is_equal))
            link(v.tensor_scalar(of_tile[:, :, :], of_tile_t[:, :, :], pcol[:, 0:1], None, ALU.mult))
            v.tensor_tensor(of_tile_t[:, :, :].rearrange("p (k t) a -> p k t a", k=K3),
                            of_tile_t[:, :, :].rearrange("p (k t) a -> p k t a", k=K3),
                            iota[:, 0:TT].unsqueeze(1).unsqueeze(3).broadcast_to([P, K3, TT, P]),
                            ALU.mult).then_inc(onehots, 1)
            dve.wait_ge(tok_ps, 1)
            link(v.tensor_copy(tok_f[:, :], ps_m[:, 0:P]))
            link(v.scalar_tensor_tensor(tok_f[:, :], ps_m[:, P:2 * P], float(P), tok_f[:, :], ALU.mult, ALU.add))
            v.tensor_copy(tok_i[:, :], tok_f[:, :]).then_inc(tok_ready, 1)

            gu_bank = [ps_acc[:, 1, 0:2 * I1], ps_acc[:, 1, HALF:HALF + 2 * I1]]
            ht_bank = [ps_g[0:IH, 0:2 * P], ps_u[0:IH, 0:2 * P]]

            def tile_step(j, r):
                static = isinstance(j, int)
                if not static or j < MAXTILES:
                    dve.wait_ge(sg_sb, j + 1)
                    if not (static and j < 2):
                        dve.wait_ge(ht_ps, j - 1)
                    v.tensor_tensor(h3[:, r % 2, :], sg3[:, r % 2, :], gu_bank[r % 2][:, I1:2 * I1],
                                    ALU.mult).then_inc(h_sb, 1)
                if not static or 0 <= j - 1 < MAXTILES:
                    dve.wait_ge(ht_ps, j)
                    if not (static and j - 1 < 2):
                        dve.wait_ge(o_ps, j - 2)
                    v.tensor_copy(hT3[:, (r - 1) % 2, :], ht_bank[(r - 1) % 2]).then_inc(ht_sb, 1)
            for j in range(3):
                tile_step(j, j % 2)
            n_loop = (MAXTILES - 3) // RING
            with dve.Fori(0, n_loop) as i:
                for k in range(RING):
                    tile_step(RING * i + (3 + k), (3 + k) % 2)
            for j in range(3 + RING * n_loop, MAXTILES + 1):
                tile_step(j, j % 2)

            def combine(i, par):
                k0 = 2 * i + par
                row = fin[:, bass.ds(k0, 1), :].rearrange("p a c -> p (a c)")
                for k in range(K3):
                    s = par * K3 + k
                    w = small[:, k, bass.ds(k0, 1)]
                    dve.wait_ge(yk_in[s], 16 * i + 16)
                    if k == 0:
                        ins = v.tensor_scalar(row, yk[:, s, :], w, None, ALU.mult)
                    else:
                        ins = v.scalar_tensor_tensor(row, yk[:, s, :], w, row, ALU.mult, ALU.add)
                    ins.then_inc(comb_step, 1)
                    dve.wait_ge(comb_step, K3 * k0 + (k + 1))

            gated_units(f3, True, None)
            with dve.Fori(0, TT // 2) as i:
                combine(i, 0)
                combine(i, 1)
            dve.wait_ge(f3.h_used, 2 * CH3)
            for c, h in QUARTERS:
                v.tensor_tensor(quarter(xT, c, h), quarter(xT, c, h), quarter(ps_acc, c, h),
                                ALU.add).then_inc(x_final, 1)
            for k in range(TT):
                dve.wait_ge(xo_ps, k + 1)
                v.tensor_tensor(fin[:, k, :], fin[:, k, :], [ps_g, ps_u][k % 2][:, 0:C], ALU.add).then_inc(fin_ready, 1)


def kernel(**inputs):
    import ml_dtypes
    import concourse.bacc as _bacc
    from concourse.bass_utils import run_bass_kernel_spmd as _run

    a = {k: np.ascontiguousarray(v) for k, v in inputs.items()}

    def channel_major(x):
        return np.ascontiguousarray(x.reshape(-1, KC, P).transpose(2, 1, 0))

    def lhs(w):
        return w.reshape(-1, P, KC, P).transpose(0, 3, 2, 1).reshape(-1, P, C)

    def padded(w, rows):
        out = np.zeros((rows, w.shape[1]), w.dtype)
        out[:w.shape[0]] = w
        return out

    w_u = [np.stack([a[f"L{l}_cond_{n}"].reshape(KC, P) for l in range(LAYERS)]) for n in "wu"]
    wd1 = a["L1_ffn_Wd"].transpose(0, 2, 1).reshape(CH1, P, C)
    l1 = [lhs(a["L1_ffn_Wg"].reshape(-1, C)), lhs(a["L1_ffn_Wu"].reshape(-1, C)), wd1]
    w1 = np.concatenate([a["L2_ffn_w1"].transpose(0, 2, 1).reshape(-1, C), a["L2_ffn_shared_w1"].T])
    w2 = np.concatenate([a["L2_ffn_w2"].reshape(-1, C), a["L2_ffn_shared_w2"]]).reshape(CH2, P, C)
    gu = a["L3_ffn_se_gate_up_w"]
    sh = [lhs(padded(gu[:ISH], CH3 * P)), lhs(padded(gu[ISH:], CH3 * P)),
          padded(a["L3_ffn_se_down_w"].T, CH3 * P).reshape(CH3, P, C)]
    b1 = np.concatenate([a["L2_ffn_b1"], a["L2_ffn_shared_b1"].reshape(-1, P)])

    def cols(w):
        return w.reshape(KC, P, -1).transpose(1, 0, 2)

    routers = np.stack([cols(a["L0_ffn_Wr"]), cols(a["L1_ffn_Wr"].T), cols(a["L2_ffn_gate_w"])], 1)
    router3 = np.concatenate([cols(a["L3_ffn_gate_w"].T), cols(a["L3_ffn_shared_gate_w"].T)], 2)

    f32, bf16 = np.float32, ml_dtypes.bfloat16
    q = np.arange(P)
    tri = np.stack([q[:, None] <= q, q[:, None] < q, np.ones((P, P), bool)], 1).astype(bf16)
    rows = list(range(E)) + [0] * CH1 + list(range(CH2)) + [0]
    sel = np.zeros((P, len(rows), P), bf16)
    for j, row in enumerate(rows):
        expert = np.full(P, min(row, E))
        if E <= j < E + CH1:
            expert = (P * (j - E) + q) // I1
        for part in range(3):
            sel[part * GCOLS + expert, j, q] = 1
    n1, n3 = 2 * TT, TT
    arrays = {
        "cond": a["cond_512"], "wu": np.stack(w_u).transpose(3, 0, 1, 2),
        "kvT": channel_major(a["fside_BxSxS_0"]), "xT": channel_major(a["x"]),
        "kvrT": channel_major(a["fside_BxSxS_0"][:, ::-1]),
        "ident": np.eye(P, dtype=f32), "identb": np.eye(P, dtype=bf16), "tri": tri, "sel": sel,
        "iota": np.tile(q.astype(f32), (P, 1)), "pcol": q.astype(f32)[:, None],
        "scanmask1": np.tile((np.arange(E * n1) % n1 > 0).astype(f32), (P, 1)),
        "scanmask3": np.tile((np.arange(E3 * n3) % n3 > 0).astype(f32), (P, 1)),
        "tbl8": np.tile((P * np.arange(TT)).astype(f32), (P, 1)),
        "routers": routers, "router3": router3, "b1": b1.T,
        "be": a["L0_ffn_be"], "b2": np.concatenate([a["L2_ffn_b2"], a["L2_ffn_shared_b2"][None]]),
        "we": a["L0_ffn_We"].reshape(E, KC, P, C).transpose(0, 2, 1, 3).reshape(E * P, KC * C),
        "w_l1": np.concatenate(l1, 2).reshape(CH1 * P, 3 * C),
        "w_l2": np.concatenate([lhs(w1), w2], 2).reshape(CH2 * P, 2 * C),
        "w_sh": np.concatenate(sh, 2).reshape(CH3 * P, 3 * C),
        "w13": a["L3_ffn_w13"].reshape(E3, 2 * I1, KC, P).transpose(0, 3, 2, 1).reshape(E3 * P, KC * 2 * I1),
        "w2": a["L3_ffn_w2"].reshape(E3, C, 2, IH).transpose(0, 3, 2, 1).reshape(E3 * IH, 2 * C),
    }
    arrays = {k: np.ascontiguousarray(v) for k, v in arrays.items()}

    nc = _bacc.Bacc("TRN2", target_bir_lowering=False, num_devices=1)
    t = {k: nc.dram_tensor(f"in_{k}", v.shape, mybir.dt.from_np(v.dtype), kind="ExternalInput").ap()
         for k, v in arrays.items()}
    t["out"] = nc.dram_tensor("out", (N, C), F32, kind="ExternalOutput").ap()
    t["te"] = nc.dram_tensor("tile_experts", (P, 1), I32, kind="Internal").ap()
    t["y_rows"] = nc.dram_tensor("y_rows", (N, C), F32, kind="Internal").ap()
    t["o_rows"] = nc.dram_tensor("o_rows", (MAXTILES * P, C), F32, kind="Internal").ap()
    build(nc, t)
    r = _run(nc, [{f"in_{k}": v for k, v in arrays.items()}], core_ids=[0])
    return r.results[0]["out"].reshape(B, T, C)
```

```python
from contextlib import ExitStack

import numpy as np

import concourse.bass as bass
from concourse import mybir

P = 128
F32 = mybir.dt.float32
BF16 = mybir.dt.bfloat16
F16 = mybir.dt.float16
I32 = mybir.dt.int32
U32 = mybir.dt.uint32
ALU = mybir.AluOpType
ACT = mybir.ActivationFunctionType
AX = mybir.AxisListType

B, T, C = 4, 256, 256
N = B * T
KC = C // P
TT = N // P
HALF = 512
LAYERS = 4
SEGS = KC * B
E = 8
GCOLS = 16
I1 = 176
CAP = int(1.25 * (N * 2 / E))
CH1 = E * I1 // P
CH2 = E + 2
E3, K3 = 60, 4
ISH = 704
CH3 = -(-ISH // P)
IH = I1 // 2
MAXTILES = E3 + (K3 * N - E3) // P
TILE_COLS = MAXTILES + MAXTILES % 2
RING = 6
SUMS = 6
QUOT = 3


def build(nc, t):
    with ExitStack() as ctx:
        def sb(name, shape, dt=F32):
            return ctx.enter_context(nc.sbuf_tensor(name, shape, dt))

        def sem(name):
            return ctx.enter_context(nc.semaphore(name))

        xT = sb("xT", [P, KC, N])
        kv = sb("kv", [P, KC, N])
        ek = sb("ek", [P, KC, N])
        ekv = sb("ekv", [P, KC, N])
        euk = sb("euk", [P, LAYERS, KC, N])
        ekr = sb("ekr", [P, KC, N])
        ekvr = sb("ekvr", [P, KC, N])
        mix = sb("mix", [P, KC, N])
        yT = sb("yT", [P, KC, N])
        ident = sb("ident", [P, P])
        identb = sb("identb", [P, P], BF16)
        tri = sb("tri", [P, 3, P], BF16)
        sel = sb("sel", [P, E + CH1 + CH2 + 1, P], BF16)
        iota = sb("iota", [P, P])
        pcol = sb("pcol", [P, 1])
        scanmask1 = sb("scanmask1", [P, E * 2 * TT])
        scanmask3 = sb("scanmask3", [P, E3 * TT])
        tbl8 = sb("tbl8", [P, TT])
        wu = sb("wu", [P, 2, LAYERS, KC])
        cond = sb("cond", [P, B, 64])
        tf = sb("tf", [P, B])
        tfhalf = sb("tfhalf", [P, B])
        tfout = sb("tfout", [P, B])
        tfout8 = sb("tfout8", [P, SEGS])
        ew = sb("ew", [P, LAYERS, KC])
        base_decay = sb("base_decay", [P, LAYERS, KC])
        decay = sb("decay", [P, LAYERS, SEGS])
        nf = sb("nf", [P, 2, T])
        nb = sb("nb", [P, 2, T])
        df = sb("df", [P, 2, T])
        db = sb("db", [P, 2, T])
        rden = sb("rden", [P, 2, T])
        now_d = sb("now_d", [P, T])
        now_n = sb("now_n", [P, T])
        routers = sb("routers", [P, 3, KC, E])
        router3 = sb("router3", [P, KC, E3 + 1])
        bias = sb("bias", [P, 2, C])
        biasp = sb("biasp", [P, 2, 3, C], BF16)
        biasr = sb("biasr", [P, 2, C])
        b1 = sb("b1", [P, CH2])
        b1_col = sb("b1_col", [P, 2])
        wring = sb("wring", [P, 2, 3 * C])
        act_h = sb("act_h", [P, 2, HALF])
        prod_h = sb("prod_h", [P, 2, HALF])
        hid = sb("hid", [P, 2, KC, HALF])
        gates = sb("gates", [P, TT, E + 1])
        g3 = sb("g3", [P, TT, P], BF16)
        gT = sb("gT", [P, N], BF16)
        lg = sb("lg", [P, TT, E3 + 1])
        mx = sb("mx", [P, TT, 8])
        ix = sb("ix", [P, TT, 8], U32)
        ixf = sb("ixf", [P, K3, TT])
        small = sb("small", [P, 8, TT])
        sum_e = sb("sum_e", [P, TT])
        rsum_e = sb("rsum_e", [P, TT])
        oh = sb("oh", [P, K3, TT, E3], BF16)
        ex = sb("ex", [P, TT, E3 + K3])
        iota16 = sb("iota16", [P, P], F16)
        token = sb("token", [P, TT])
        slots4 = sb("slots4", [P, K3, TT, E3])
        r1 = sb("r1", [P, TT, E3])
        r2 = sb("r2", [P, TT, E3])
        tot = sb("tot", [P, E3 * TT])
        cum = sb("cum", [P, E3 * TT])
        tiles3 = sb("tiles3", [P, E3])
        tincl = sb("tincl", [P, E3])
        tbase = sb("tbase", [P, E3])
        ones60 = sb("ones60", [P, E3])
        te_f = sb("te_f", [P, 1])
        te_i = sb("te_i", [P, 1], I32)
        te_row = sb("te_row", [1, P], I32)
        place_i = sb("place_i", [P, 2, K3 * TT], I32)
        place_f = sb("place_f", [P, 3, K3 * TT])
        slot_i = sb("slot_i", [P, K3 * TT], I32)
        tok_i = sb("tok_i", [P, P], I32)
        tok_col = sb("tok_col", [P, RING], I32)
        xgT = sb("xgT", [P, 2, C])
        sg3 = sb("sg3", [P, 2, I1])
        h3 = sb("h3", [P, 2, I1])
        hT3 = sb("hT3", [IH, 2, 2 * P])
        o3 = sb("o3", [P, RING, C])

        weights3 = [tile.rearrange("p c n -> p (c n)") for tile in
                    (ek[:, :, :], ekv[:, :, :], ekvr[:, :, :], kv[:, :, :], euk[:, 0], euk[:, 1])]
        xg = euk[:, 3, :, :].rearrange("p c (k t) -> p (c k) t", t=C)
        w13 = [tile[:, 0:KC * 2 * I1] for tile in weights3]
        w2 = [tile[0:IH, KC * 2 * I1:KC * 2 * I1 + 2 * C] for tile in weights3]

        yk = euk[:, :, :, :].rearrange("p l c (k t) -> p (l c k) t", t=C)
        fin = mix[:, :, :].rearrange("p c (k t) -> p (c k) t", t=C)
        y_tok = euk[:, 2, :, :].rearrange("p c (k t) -> p (c k) t", t=C)

        in_tile = (ekr[:, :, :].rearrange("p c n -> p (c n)").bitcast(F16)
                   .rearrange("p (k m) -> p k m", m=P))
        of_tile = sb("of_tile", [P, K3 * TT, TILE_COLS], F16)

        ps_acc = ctx.enter_context(nc.psum_tensor("ps_acc", [P, KC, N], F32))
        ps_g = ctx.enter_context(nc.psum_tensor("ps_g", [P, HALF], F32))
        ps_u = ctx.enter_context(nc.psum_tensor("ps_u", [P, HALF], F32))
        ps_w = ctx.enter_context(nc.psum_tensor("ps_w", [P, HALF], F32))
        ps_m = ctx.enter_context(nc.psum_tensor("ps_m", [P, HALF], F32))
        ps_wb = ps_w[:, :].bitcast(BF16)

        in_cond, in_w, in_kv, in_x = sem("in_cond"), sem("in_w"), sem("in_kv"), sem("in_x")
        in_const = sem("in_const")
        tf_sum, tf_sig, tf_ready = sem("tf_sum"), sem("tf_sig"), sem("tf_ready")
        dec_act, dec_ready = sem("dec_act"), sem("dec_ready")
        kmin, ek_ready, ekv_ready, ukmin, euk_ready = (sem("kmin"), sem("ek_ready"), sem("ekv_ready"),
                                                       sem("ukmin"), sem("euk_ready"))
        blank = sem("blank")
        scan_step, sum_step, m_step = sem("scan_step"), sem("sum_step"), sem("m_step")
        b1_ready = sem("b1_ready")
        x_upd, y_sig, y_ready = sem("x_upd"), sem("y_sig"), sem("y_ready")
        lg_done = sem("lg_done")
        dve_step = sem("dve_step")
        bias_in, bias_split = sem("bias_in"), sem("bias_split")
        exp_in, exp_out = sem("exp_in"), sem("exp_out")
        rank_in, rank_done = sem("rank_in"), sem("rank_done")
        gate_split, gT_ps, gT_ready = sem("gate_split"), sem("gT_ps"), sem("gT_ready")

        class Ffn:

            def __init__(self, name, chunks):
                self.n = chunks
                self.w_in = [sem(f"{name}_w_in0"), sem(f"{name}_w_in1")]
                self.g_done = sem(f"{name}_g_done")
                self.u_done = sem(f"{name}_u_done")
                self.w_done = sem(f"{name}_w_done")
                self.g_read = sem(f"{name}_g_read")
                self.u_read = sem(f"{name}_u_read")
                self.h_ready = sem(f"{name}_h_ready")
                self.h_used = sem(f"{name}_h_used")

        f0, f1, f2, f3 = Ffn("f0", E), Ffn("f1", CH1), Ffn("f2", CH2), Ffn("f3", CH3)
        ffns = [f0, f1, f2, f3]

        yt_ps, yt_sb, yt_out = sem("yt_ps"), sem("yt_sb"), sem("yt_out")
        te_ready, te_out, te_in = sem("te_ready"), sem("te_out"), sem("te_in")
        onehots, tok_ps, tok_ready = sem("onehots"), sem("tok_ps"), sem("tok_ready")
        sgate_in, sgate_out = sem("sgate_in"), sem("sgate_out")
        w13_tile = [sem(f"w13_tile{r}") for r in range(RING)]
        w2_tile = [sem(f"w2_tile{r}") for r in range(RING)]
        x_tile = [sem(f"x_tile{r}") for r in range(RING)]
        o_tile = [sem(f"o_tile{r}") for r in range(RING)]
        tcol, xt_ps, xt_sb = sem("tcol"), sem("xt_ps"), sem("xt_sb")
        gu_ps, sg_sb, h_sb = sem("gu_ps"), sem("sg_sb"), sem("h_sb")
        ht_ps, ht_sb, o_ps, o_sb = sem("ht_ps"), sem("ht_sb"), sem("o_ps"), sem("o_sb")
        yk_in = [sem(f"yk_in{r}") for r in range(8)]
        x_final, xo_ps, fin_ready, out_done = sem("x_final"), sem("xo_ps"), sem("fin_ready"), sem("out_done")
        comb_step = sem("comb_step")

        block = ctx.enter_context(nc.Block())

        def over_pairs(eng, n, body, last_peeled=False):
            looped = n // 2 - (1 if last_peeled and n % 2 == 0 else 0)
            body(0, 0)
            body(1, 1)
            with eng.Fori(1, looped) as i:
                body(2 * i, 0)
                body(2 * i + 1, 1)
            for j in range(2 * looped, n):
                body(j, j % 2)

        def seg(tile, s):
            return tile.rearrange("p c (b t) -> p (c b) t", t=T)[:, bass.ds(s, 1), :].rearrange("p a t -> p (a t)")

        def by_seq(rows):
            return rows.rearrange("p (b t) -> p b t", t=T)

        QUARTERS = [(c, h) for h in range(2) for c in range(KC)]

        def quarter(tile, c, h):
            return tile[:, c, h * HALF:(h + 1) * HALF]

        @block.sync
        def _(sp):
            sp.dma_start(cond[:, :, :], t["cond"].rearrange("b d -> (b d)").partition_broadcast(P)
                         .rearrange("p (b d) -> p b d", b=B)).then_inc(in_cond, 16)
            sp.dma_start(wu[:, :, :, :], t["wu"]).then_inc(in_w, 16)
            sp.dma_start(kv[:, :, :], t["kvT"]).then_inc(in_kv, 16)
            sp.dma_start(xT[:, :, :], t["xT"]).then_inc(in_x, 16)
            consts = [(ident, "ident"), (identb, "identb"), (tri, "tri"), (sel, "sel"), (iota, "iota"),
                      (pcol, "pcol"), (scanmask1, "scanmask1"), (scanmask3, "scanmask3"), (tbl8, "tbl8"),
                      (routers, "routers"), (router3, "router3"), (b1, "b1")]
            for tile, name in consts:
                sp.dma_start(tile[:], t[name]).then_inc(in_const, 16)
            sp.wait_ge(blank, 1)
            for part in range(3):
                r = part * GCOLS
                sp.dma_start(bias[r:r + E, 0, :], t["be"]).then_inc(bias_in, 16)
                sp.dma_start(bias[r:r + E + 1, 1, :], t["b2"]).then_inc(bias_in, 16)

            def load_chunks(f, src, width):
                def body(j, slot):
                    if not (isinstance(j, int) and j < 2):
                        sp.wait_ge(f.h_used, 2 * j - 2)
                    sp.dma_start(wring[:, slot, 0:width],
                                 src[bass.ds(j * P, P), :]).then_inc(f.w_in[slot], 16)
                over_pairs(sp, f.n, body)

            load_chunks(f0, t["we"], KC * C)
            sp.wait_ge(f0.h_used, 2 * f0.n)
            load_chunks(f1, t["w_l1"], 3 * C)
            sp.wait_ge(f1.h_used, 2 * f1.n)
            load_chunks(f2, t["w_l2"], 2 * C)

            sp.wait_ge(yt_sb, 4)
            sp.dma_start(t["y_rows"].rearrange("(k p) c -> p k c", p=P), y_tok[:, :, :]).then_inc(yt_out, 16)
            sp.wait_ge(te_ready, 1)
            sp.dma_start(t["te"], te_i[:, :]).then_inc(te_out, 16)
            sp.wait_ge(te_out, 16)
            sp.dma_start(te_row[:, :], t["te"].rearrange("p a -> a p")).then_inc(te_in, 16)
            sp.wait_ge(te_in, 16)

            def load_tile(j, r):
                e = sp.value_load(te_row[0:1, bass.ds(j, 1)], min_val=0, max_val=E3 - 1)
                if not (isinstance(j, int) and j < RING):
                    sp.wait_ge(o_ps, j - (RING - 1))
                sp.dma_start(w13[r], t["w13"][bass.ds(e * P, P), :]).then_inc(w13_tile[r], 16)
                sp.dma_start(w2[r], t["w2"][bass.ds(e * IH, IH), :]).then_inc(w2_tile[r], 16)

            for j in range(RING):
                load_tile(j, j)
            n_loop = MAXTILES // RING
            with sp.Fori(1, n_loop) as i:
                for r in range(RING):
                    load_tile(RING * i + r, r)
            for j in range(RING * n_loop, MAXTILES):
                load_tile(j, j % RING)

            load_chunks(f3, t["w_sh"], 3 * C)
            with sp.Fori(0, TT) as i:
                sp.wait_ge(fin_ready, i + 1)
                sp.dma_start(t["out"][bass.ds(i * P, P), :],
                             fin[:, bass.ds(i, 1), :].rearrange("p a c -> p (a c)")).then_inc(out_done, 16)
            sp.wait_ge(out_done, 16 * TT)

        @block.tensor
        def _(pe):
            mm = nc.tensor.matmul
            pe.wait_ge(in_const, 16 * 12)

            def router(l, w, n):
                for k in range(TT):
                    if k % (TT // 2) == 0:
                        pe.wait_ge(y_ready, 4 * l + (2 if k == 0 else 4))
                    for c in range(KC):
                        last = mm(ps_m[:, k * n:(k + 1) * n], yT[:, c, k * P:(k + 1) * P], w[:, c, :],
                                  start=(c == 0), stop=(c == KC - 1))
                last.then_inc(lg_done, 1)

            def turn_gates(l):
                pe.wait_ge(gate_split, l + 1)
                for k in range(TT):
                    last = nc.tensor.transpose(ps_wb[:, k * P:(k + 1) * P], g3[:, k, :], identb[:, :])
                last.then_inc(gT_ps, 1)
                pe.wait_ge(gT_ready, l + 1)

            def add_bias(b):
                for c in range(KC):
                    for h in range(2):
                        for part in range(3):
                            mm(quarter(ps_acc, c, h), biasp[:, b, part, c * P:(c + 1) * P],
                               gT[:, h * HALF:(h + 1) * HALF], start=(part == 0), stop=False)

            def spread(f, q, row, h):
                if not (isinstance(q, int) and q < 1):
                    pe.wait_ge(f.h_ready, q)
                mm(ps_w[:, :], sel[:, bass.ds(row, 1), :].rearrange("p a m -> p (a m)"),
                   gT[:, h * HALF:(h + 1) * HALF], start=True, stop=True).then_inc(f.w_done, 1)

            router(0, routers[:, 0], E)
            turn_gates(0)
            pe.wait_ge(bias_split, 1)
            add_bias(0)
            spread(f0, 0, 0, 0)

            def layer0(e, slot):
                for h in range(2):
                    q = 2 * e + h
                    if h == 0:
                        spread(f0, q + 1, e, 1)
                    elif not (isinstance(e, int) and e == E - 1):
                        spread(f0, q + 1, e + 1, 0)
                    if h == 0:
                        pe.wait_ge(f0.w_in[slot], 8 * e + (16 - 8 * slot))
                    pe.wait_ge(f0.h_ready, q + 1)
                    for c in range(KC):
                        for k in range(KC):
                            last = mm(quarter(ps_acc, c, h), wring[:, slot, k * C + c * P:k * C + (c + 1) * P],
                                      hid[:, h, k, :], start=False,
                                      stop=(k == KC - 1 and isinstance(e, int) and e == E - 1))
                    last.then_inc(f0.h_used, 1)

            over_pairs(pe, E, layer0, last_peeled=True)

            def gated(f, has_up, row_of, opened):
                def down(q, j, slot, h, last_one):
                    pe.wait_ge(f.h_ready, q + 1)
                    off = (2 if has_up else 1) * C
                    first = isinstance(j, int) and j == 0 and not opened
                    for c in range(KC):
                        last = mm(quarter(ps_acc, c, h), wring[:, slot, off + c * P:off + (c + 1) * P],
                                  hid[:, h, 0, :], start=first, stop=last_one)
                    last.then_inc(f.h_used, 1)

                def body(j, slot):
                    for h in range(2):
                        q = 2 * j + h
                        start = isinstance(q, int) and q < 1
                        if h == 0:
                            pe.wait_ge(f.w_in[slot], 8 * j + (16 - 8 * slot))
                        if not start:
                            pe.wait_ge(f.g_read, q)
                        for k in range(KC):
                            last = mm(ps_g[:, :], wring[:, slot, k * P:(k + 1) * P],
                                      yT[:, k, h * HALF:(h + 1) * HALF], start=(k == 0), stop=(k == KC - 1))
                        last.then_inc(f.g_done, 1)
                        if has_up:
                            if not start:
                                pe.wait_ge(f.u_read, q)
                            for k in range(KC):
                                last = mm(ps_u[:, :], wring[:, slot, C + k * P:C + (k + 1) * P],
                                          yT[:, k, h * HALF:(h + 1) * HALF], start=(k == 0), stop=(k == KC - 1))
                            last.then_inc(f.u_done, 1)
                        spread(f, q, row_of(j), h)
                        if not start:
                            down(q - 1, j if h else j - 1, slot if h else 1 - slot, 1 - h,
                                 isinstance(q, int) and q == 2 * f.n - 1)
                n = f.n
                over_pairs(pe, n, body, last_peeled=True)
                down(2 * n - 1, n - 1, (n - 1) % 2, 1, True)

            router(1, routers[:, 1], E)
            for k in range(2):
                pe.wait_ge(rank_in, k + 1)
                for ps, kind in ((ps_g, 0), (ps_u, 2)):
                    last = mm(ps[:, k * TT * E:(k + 1) * TT * E], tri[:, kind, :], oh[:, k, :, 0:E],
                              start=True, stop=True)
            last.then_inc(rank_done, 1)
            turn_gates(1)
            gated(f1, True, lambda j: j + E, False)

            router(2, routers[:, 2], E)
            turn_gates(2)
            add_bias(1)
            gated(f2, False, lambda j: j + (E + CH1), True)

            router(3, router3, E3 + 1)
            for k in range(TT):
                for c in range(KC):
                    last = nc.tensor.transpose(ps_acc[:, k // 4, (k % 4) * C + c * P:(k % 4) * C + (c + 1) * P],
                                               yT[:, c, k * P:(k + 1) * P], ident[:, :])
                if k % 2:
                    last.then_inc(yt_ps, 1)
            for k in range(K3):
                pe.wait_ge(rank_in, 3 + k)
                for ps, kind in ((ps_g, 1), (ps_u, 2)):
                    last = mm(ps[:, 0:TT * E3], tri[:, kind, :], oh[:, k, :, :].rearrange("p t e -> p (t e)"),
                              start=(k == 0), stop=(k == K3 - 1))
            last.then_inc(rank_done, 1)
            for k in range(K3 * TT):
                pe.wait_ge(onehots, k + 1)
                last = mm(ps_m[:, 0:TILE_COLS], in_tile[:, k, :], of_tile[:, k, :], start=(k == 0),
                          stop=(k == K3 * TT - 1))
            last.then_inc(tok_ps, 1)
            pe.wait_ge(tok_ready, 1)

            xt_bank = [ps_acc[:, 0, 0:C], ps_acc[:, 0, HALF:HALF + C]]
            gu_bank = [ps_acc[:, 1, 0:2 * I1], ps_acc[:, 1, HALF:HALF + 2 * I1]]
            ht_bank = [ps_g[0:IH, 0:2 * P], ps_u[0:IH, 0:2 * P]]
            o_bank = [ps_w[:, 0:C], ps_m[:, 0:C]]

            def known(j, least):
                return isinstance(j, int) and j < least

            def turn_x(j, r, lap):
                pe.wait_ge(x_tile[r], 16 * lap + 16)
                if not known(j, 2):
                    pe.wait_ge(xt_sb, j - 1)
                for c in range(KC):
                    last = nc.tensor.transpose(xt_bank[r % 2][:, c * P:(c + 1) * P],
                                               xg[:, r, c * P:(c + 1) * P], ident[:, :])
                last.then_inc(xt_ps, 1)

            def gate_up(j, r, lap):
                pe.wait_ge(w13_tile[r], 16 * lap + 16)
                pe.wait_ge(xt_sb, j + 1)
                if not known(j, 2):
                    pe.wait_ge(h_sb, j - 1)
                for c in range(KC):
                    last = mm(gu_bank[r % 2], xgT[:, r % 2, c * P:(c + 1) * P],
                              w13[r][:, c * 2 * I1:(c + 1) * 2 * I1], start=(c == 0), stop=(c == KC - 1))
                last.then_inc(gu_ps, 1)

            def turn_h(j, r):
                pe.wait_ge(h_sb, j + 1)
                if not known(j, 2):
                    pe.wait_ge(ht_sb, j - 1)
                for c in range(2):
                    last = nc.tensor.transpose(ht_bank[r % 2][:, c * P:(c + 1) * P],
                                               h3[:, r % 2, c * IH:(c + 1) * IH], ident[:, :])
                last.then_inc(ht_ps, 1)

            def down3(j, r, lap):
                pe.wait_ge(w2_tile[r], 16 * lap + 16)
                pe.wait_ge(ht_sb, j + 1)
                if not known(j, 2):
                    pe.wait_ge(o_sb, j - 1)
                for c in range(2):
                    last = mm(o_bank[r % 2], hT3[:, r % 2, c * P:(c + 1) * P],
                              w2[r][:, c * C:(c + 1) * C], start=(c == 0), stop=(c == 1))
                last.then_inc(o_ps, 1)

            def tile_step(j, r, lap):
                static = isinstance(j, int)
                if not static or j + 1 < MAXTILES:
                    turn_x(j + 1, (r + 1) % RING, lap + (r + 1) // RING)
                if not static or j < MAXTILES:
                    gate_up(j, r, lap)
                if not static or 0 <= j - 2 < MAXTILES:
                    down3(j - 2, (r - 2) % RING, lap - (r < 2))
                if not static or 0 <= j - 1 < MAXTILES:
                    turn_h(j - 1, (r - 1) % RING)

            turn_x(0, 0, 0)
            for j in range(RING):
                tile_step(j, j, 0)
            n_loop = (MAXTILES - 1) // RING
            with pe.Fori(1, n_loop) as i:
                for r in range(RING):
                    tile_step(RING * i + r, r, i)
            for j in range(RING * n_loop, MAXTILES + 2):
                tile_step(j, j % RING, j // RING)

            pe.wait_ge(o_sb, MAXTILES)
            turn_gates(3)
            gated(f3, True, lambda j: E + CH1 + CH2, False)

            pe.wait_ge(x_final, 4)
            for k in range(TT):
                if k >= 2:
                    pe.wait_ge(fin_ready, k - 1)
                for c in range(KC):
                    last = nc.tensor.transpose([ps_g, ps_u][k % 2][:, c * P:(c + 1) * P],
                                               xT[:, c, k * P:(k + 1) * P], ident[:, :])
                last.then_inc(xo_ps, 1)

        @block.scalar
        def _(act):
            fn = nc.scalar.activation
            act.wait_ge(tf_sum, 1)
            fn(tf[:, :], tf[:, :], ACT.Sigmoid).then_inc(tf_sig, 1)
            act.wait_ge(in_w, 16)
            fn(ew[:, :, :], wu[:, 0], ACT.Exp).then_inc(dec_act, 1)
            act.wait_ge(dec_act, 1)
            fn(base_decay[:, :, :], ew[:, :, :], ACT.Exp, scale=-1.0).then_inc(dec_act, 1)
            for c in range(KC):
                act.wait_ge(kmin, c + 1)
                fn(ek[:, c, :], ek[:, c, :], ACT.Exp).then_inc(ek_ready, 1)
            for c in range(KC):
                act.wait_ge(ek_ready, c + 1)
                nc.scalar.copy(by_seq(ekr[:, c, :]), by_seq(ek[:, c, :])[:, :, ::-1]).then_inc(ek_ready, 1)

            def exp_euk(l):
                act.wait_ge(ukmin, l + 1)
                fn(euk[:, l], euk[:, l], ACT.Exp).then_inc(euk_ready, 1)

            exp_euk(0)

            def input_sigmoid(l):
                if l == 0:
                    act.wait_ge(in_x, 16)
                for n, (c, h) in enumerate(QUARTERS):
                    if l:
                        act.wait_ge(x_upd, 4 * (l - 1) + n + 1)
                    fn(quarter(yT, c, h), quarter(xT, c, h), ACT.Sigmoid).then_inc(y_sig, 1)

            def softmax_exp(n, tile):
                act.wait_ge(exp_in, n)
                fn(tile, tile, ACT.Exp).then_inc(exp_out, 1)

            def copy_gT(l):
                act.wait_ge(gT_ps, l + 1)
                nc.scalar.copy(gT[:, :], ps_wb).then_inc(gT_ready, 1)

            def activate(f, func, bias_of, skip_u):
                def body(j, slot):
                    if bias_of:
                        nc.scalar.copy(b1_col[:, slot:slot + 1], b1[:, bass.ds(j, 1)]).then_inc(b1_ready, 1)
                    for h in range(2):
                        q = 2 * j + h
                        act.wait_ge(f.g_done, q + 1)
                        if not (isinstance(q, int) and q < 2):
                            act.wait_ge(f.h_ready if skip_u else f.u_read, q - 1)
                        kw = {}
                        if bias_of:
                            act.wait_ge(b1_ready, j + 1)
                            kw = {"bias": b1_col[:, slot:slot + 1]}
                        fn(act_h[:, h, :], ps_g[:, :], func, **kw).then_inc(f.g_read, 1)
                over_pairs(act, f.n, body)

            input_sigmoid(0)
            softmax_exp(1, small[:, 0, :])
            copy_gT(0)
            for l in range(1, LAYERS):
                exp_euk(l)
            input_sigmoid(1)
            softmax_exp(2, ex[:, :, 0:E + 2])
            copy_gT(1)
            activate(f1, ACT.Silu, False, False)
            input_sigmoid(2)
            softmax_exp(3, small[:, 0, :])
            copy_gT(2)
            activate(f2, ACT.Gelu, True, True)
            input_sigmoid(3)
            for k in range(4):
                act.wait_ge(yt_ps, k + 1)
                nc.scalar.copy(y_tok[:, 2 * k:2 * k + 2, :].rearrange("p k c -> p (k c)"),
                               ps_acc[:, k // 2, (k % 2) * HALF:(k % 2 + 1) * HALF]).then_inc(yt_sb, 1)
            act.wait_ge(sgate_in, 1)
            fn(gates[:, :, 0], small[:, 7, :], ACT.Sigmoid).then_inc(sgate_out, 1)
            softmax_exp(4, ex[:, :, :])

            xt_bank = [ps_acc[:, 0, 0:C], ps_acc[:, 0, HALF:HALF + C]]
            gu_bank = [ps_acc[:, 1, 0:2 * I1], ps_acc[:, 1, HALF:HALF + 2 * I1]]
            o_bank = [ps_w[:, 0:C], ps_m[:, 0:C]]

            def tile_step(j, r, lap):
                static = isinstance(j, int)
                if not static or 0 <= j - 3 < MAXTILES:
                    act.wait_ge(o_sb, j - 2)
                    act.dma_start(t["o_rows"][bass.ds((j - 3) * P, P), :],
                                  o3[:, (r - 3) % RING, :]).then_inc(o_tile[(r - 3) % RING], 16)
                if not static or j + 1 < MAXTILES:
                    act.wait_ge(xt_ps, j + 2)
                    if not (static and j + 1 < 2):
                        act.wait_ge(gu_ps, j)
                    nc.scalar.copy(xgT[:, (r + 1) % 2, :], xt_bank[(r + 1) % 2]).then_inc(xt_sb, 1)
                if not static or j < MAXTILES:
                    act.wait_ge(gu_ps, j + 1)
                    if not (static and j < 2):
                        act.wait_ge(h_sb, j - 1)
                    fn(sg3[:, r % 2, :], gu_bank[r % 2][:, 0:I1], ACT.Silu).then_inc(sg_sb, 1)
                if not static or 0 <= j - 2 < MAXTILES:
                    act.wait_ge(o_ps, j - 1)
                    if not (static and j - 2 < RING):
                        act.wait_ge(o_tile[(r - 2) % RING], 16 * lap - 16 * (r < 2))
                    nc.scalar.copy(o3[:, (r - 2) % RING, :], o_bank[r % 2]).then_inc(o_sb, 1)

            act.wait_ge(xt_ps, 1)
            act.wait_ge(tok_ready, 1)
            nc.scalar.copy(xgT[:, 0, :], xt_bank[0]).then_inc(xt_sb, 1)
            for j in range(2 * RING):
                tile_step(j, j % RING, j // RING)
            n_loop = (MAXTILES - 1) // RING
            with act.Fori(2, n_loop) as i:
                for r in range(RING):
                    tile_step(RING * i + r, r, i)
            for j in range(RING * n_loop, MAXTILES + 3):
                tile_step(j, j % RING, j // RING)
            copy_gT(3)
            activate(f3, ACT.Silu, False, False)

        @block.gpsimd
        def _(pool):
            for tile, value in ((bias, 0.0), (g3, 0.0), (gates, 1.0), (ones60, 1.0)):
                nc.gpsimd.memset(tile[:], value).then_inc(blank, 1)

            def sums(l, s, par):
                g = SEGS * l + s
                tt = nc.gpsimd.tensor_tensor
                if not (isinstance(g, int) and g == 0):
                    pool.wait_ge(sum_step, SUMS * g)
                    pool.nop(nofuse=True)
                tt(now_d[:, :], seg(euk[:, l], s), seg(ek, s), ALU.subtract).then_inc(sum_step, 1)
                pool.wait_ge(sum_step, SUMS * g + 1)
                pool.nop(nofuse=True)
                tt(now_n[:, :], now_d[:, :], seg(kv, s), ALU.mult).then_inc(sum_step, 1)
                pool.wait_ge(scan_step, 4 * g + 2)
                tt(nf[:, par, :], nf[:, par, :], nb[:, par, :], ALU.add).then_inc(sum_step, 1)
                pool.wait_ge(sum_step, SUMS * g + 3)
                tt(nf[:, par, :], nf[:, par, :], now_n[:, :], ALU.add).then_inc(sum_step, 1)
                pool.wait_ge(scan_step, 4 * g + 4)
                tt(df[:, par, :], df[:, par, :], db[:, par, :], ALU.add).then_inc(sum_step, 1)
                pool.wait_ge(sum_step, SUMS * g + 5)
                tt(df[:, par, :], df[:, par, :], now_d[:, :], ALU.add).then_inc(sum_step, 1)

            pool.wait_ge(ek_ready, KC)
            for l in range(LAYERS):
                pool.wait_ge(euk_ready, l + 1)
                if l == 0:
                    sums(0, 0, 0)
                    sums(0, 1, 1)
                with pool.Fori(1 if l == 0 else 0, SEGS // 2) as i:
                    for par in range(2):
                        sums(l, 2 * i + par, par)

            pool.wait_ge(tok_ready, 1)
            pool.wait_ge(yt_out, 16)

            def gather(j, r):
                if not (isinstance(j, int) and j < RING):
                    pool.wait_ge(xt_ps, j - RING + 1)
                nc.gpsimd.tensor_copy(tok_col[:, r:r + 1], tok_i[:, bass.ds(j, 1)]).then_inc(tcol, 1)
                pool.wait_ge(tcol, j + 1)
                pool.nop(nofuse=True)
                nc.gpsimd.indirect_dma_start(
                    xg[:, r, :], None, t["y_rows"],
                    bass.IndirectOffsetOnAxis(ap=tok_col[:, r:r + 1], axis=0)).then_inc(x_tile[r], 16)
            for j in range(RING):
                gather(j, j)
            n_loop = MAXTILES // RING
            with pool.Fori(1, n_loop) as i:
                for r in range(RING):
                    gather(RING * i + r, r)
            for j in range(RING * n_loop, MAXTILES):
                gather(j, j % RING)

            for r in range(RING):
                pool.wait_ge(o_tile[r], 16 * len(range(r, MAXTILES, RING)))

            def gather_back(k, par):
                for c in range(K3):
                    nc.gpsimd.indirect_dma_start(
                        yk[:, k * K3 + c, :], None, t["o_rows"],
                        bass.IndirectOffsetOnAxis(ap=slot_i[:, c * TT + k:c * TT + k + 1], axis=0)
                    ).then_inc(yk_in[k], 16)
            for k in range(TT):
                gather_back(k, k % 2)

        @block.vector
        def _(dve):
            v = nc.vector
            n_steps = [0]

            def link(ins):
                n_steps[0] += 1
                ins.then_inc(dve_step, 1)
                dve.wait_ge(dve_step, n_steps[0])

            def go(ins):
                n_steps[0] += 1
                ins.then_inc(dve_step, 1)

            def split(hi, mid, lo, whole, rest, done):
                link(v.tensor_copy(hi, whole))
                link(v.tensor_tensor(rest, whole, hi, ALU.subtract))
                link(v.tensor_copy(mid, rest))
                link(v.tensor_tensor(rest, rest, mid, ALU.subtract))
                v.tensor_copy(lo, rest).then_inc(done, 1)

            dve.wait_ge(in_cond, 16)
            v.tensor_reduce(tf[:, :], cond[:, :, :], AX.X, ALU.add).then_inc(tf_sum, 1)
            dve.wait_ge(in_kv, 16)
            for c in range(KC):
                v.tensor_scalar(ek[:, c, :], kv[:, c, :], 30.0, None, ALU.min).then_inc(kmin, 1)
            dve.wait_ge(in_w, 16)

            def exponent(l):
                for c in range(KC):
                    ins = v.tensor_scalar(euk[:, l, c], kv[:, c], wu[:, 1, l, c:c + 1], 30.0, ALU.add, ALU.min)
                ins.then_inc(ukmin, 1)

            exponent(0)
            dve.wait_ge(tf_sig, 1)
            go(v.tensor_scalar(tfhalf[:, :], tf[:, :], 0.5, 0.5, ALU.mult, ALU.add))
            link(v.tensor_scalar(tfout[:, :], tf[:, :], 0.2, 0.8, ALU.mult, ALU.add))
            dve.wait_ge(dec_act, 2)
            for l in range(LAYERS):
                for c in range(KC):
                    go(v.tensor_scalar(decay[:, l, c * B:(c + 1) * B], tfhalf[:, :], base_decay[:, l, c:c + 1],
                                       None, ALU.mult))
            for c in range(KC):
                (go if c < KC - 1 else link)(v.tensor_copy(tfout8[:, c * B:(c + 1) * B], tfout[:, :]))
            for c in range(KC):
                dve.wait_ge(ek_ready, c + 1)
                go(v.tensor_tensor(ekv[:, c, :], ek[:, c, :], kv[:, c, :], ALU.mult))
            for c in range(KC):
                dve.wait_ge(ek_ready, KC + c + 1)
                (go if c < KC - 1 else link)(v.tensor_tensor(
                    by_seq(ekvr[:, c, :]), by_seq(ekr[:, c, :]), by_seq(kv[:, c, :])[:, :, ::-1], ALU.mult))

            def scans(l, s, par):
                g = SEGS * l + s
                if not (isinstance(g, int) and g < 2):
                    dve.wait_ge(m_step, QUOT * (g - 1))
                dec = decay[:, l, bass.ds(s, 1)].to_broadcast([P, T])
                for out, src in ((nf[:, par, :], ekv), (nb[:, par, ::-1], ekvr),
                                 (df[:, par, :], ek), (db[:, par, ::-1], ekr)):
                    v.tensor_tensor_scan(out, dec, seg(src, s), 0.0, ALU.mult, ALU.add).then_inc(scan_step, 1)

            def quotient(l, s, par):
                g = SEGS * l + s
                dve.wait_ge(sum_step, SUMS * (g + 1))
                v.tensor_scalar(df[:, par, :], df[:, par, :], 1e-8, None, ALU.max).then_inc(m_step, 1)
                dve.wait_ge(m_step, QUOT * g + 1)
                v.reciprocal(rden[:, par, :], df[:, par, :]).then_inc(m_step, 1)
                dve.wait_ge(m_step, QUOT * g + 2)
                v.scalar_tensor_tensor(seg(mix, s), nf[:, par, :], tfout8[:, bass.ds(s, 1)], rden[:, par, :],
                                       ALU.mult, ALU.mult).then_inc(m_step, 1)

            scans(0, 0, 0)
            scans(0, 1, 1)
            with dve.Fori(0, SEGS // 2 - 1) as i:
                for par in range(2):
                    quotient(0, 2 * i + par, par)
                    scans(0, 2 * i + (2 + par), par)
            for par in range(2):
                quotient(0, SEGS - 2 + par, par)

            def input_of(l, prev):
                for n, (c, h) in enumerate(QUARTERS):
                    if prev is not None:
                        dve.wait_ge(prev.h_used, 2 * prev.n - 1 + h)
                        v.tensor_tensor(quarter(xT, c, h), quarter(xT, c, h), quarter(ps_acc, c, h),
                                        ALU.add).then_inc(x_upd, 1)
                dve.wait_ge(m_step, QUOT * SEGS * (l + 1))
                for n, (c, h) in enumerate(QUARTERS):
                    dve.wait_ge(y_sig, 4 * l + n + 1)
                    v.tensor_tensor(quarter(yT, c, h), quarter(yT, c, h), quarter(mix, c, h),
                                    ALU.mult).then_inc(y_ready, 1)

            def top8(values):
                for k in range(TT):
                    (go if k < TT - 1 else link)(v.max(mx[:, k, :], values[:, k, :]))

            def top8_index(values):
                for k in range(TT):
                    (go if k < TT - 1 else link)(v.max_index(ix[:, k, :], mx[:, k, :], values[:, k, :]))

            def one_hots(choices, n_exp, count):
                link(v.tensor_copy(ixf[:, 0:choices, :], ix[:, :, 0:choices].rearrange("p t k -> p k t")))
                for k in range(choices):
                    count(v.tensor_tensor(
                        oh[:, k, :, 0:n_exp], iota[:, 0:n_exp].unsqueeze(1).broadcast_to([P, TT, n_exp]),
                        ixf[:, k, :].unsqueeze(2).broadcast_to([P, TT, n_exp]), ALU.is_equal))

            def split_gates(l, n):
                split(g3[:, :, 0:n], g3[:, :, GCOLS:GCOLS + n], g3[:, :, 2 * GCOLS:2 * GCOLS + n],
                      gates[:, :, 0:n], r1[:, :, 0:n], gate_split)

            def weigh(out, k, w, n_exp):
                return v.tensor_tensor(out, oh[:, k, :, 0:n_exp], w.unsqueeze(2).broadcast_to([P, TT, n_exp]),
                                       ALU.mult)

            def route_top2(l, n_exp_round):
                dve.wait_ge(lg_done, l + 1)
                link(v.tensor_copy(lg[:, :, 0:E], ps_m[:, 0:TT * E].rearrange("p (k e) -> p k e", e=E)))
                top8(lg[:, :, 0:E])
                v.tensor_tensor(small[:, 0, :], mx[:, :, 1], mx[:, :, 0], ALU.subtract).then_inc(exp_in, 1)
                top8_index(lg[:, :, 0:E])
                one_hots(2, E, link)
                dve.wait_ge(exp_out, n_exp_round)
                link(v.tensor_scalar(small[:, 1, :], small[:, 0, :], 1.0, None, ALU.add))
                link(v.reciprocal(small[:, 2, :], small[:, 1, :]))
                link(v.tensor_tensor(small[:, 3, :], small[:, 0, :], small[:, 2, :], ALU.mult))
                go(weigh(r1[:, :, 0:E], 0, small[:, 2, :], E))
                link(weigh(r2[:, :, 0:E], 1, small[:, 3, :], E))
                link(v.tensor_tensor(gates[:, :, 0:E], r1[:, :, 0:E], r2[:, :, 0:E], ALU.add))
                split_gates(l, E + 1)

            def softmax_in(n_exp, choices):
                top = mx[:, :, 0:1]
                go(v.tensor_tensor(ex[:, :, 0:n_exp], lg[:, :, 0:n_exp], top.broadcast_to([P, TT, n_exp]),
                                   ALU.subtract))
                v.tensor_tensor(ex[:, :, n_exp:n_exp + choices], mx[:, :, 0:choices],
                                top.broadcast_to([P, TT, choices]), ALU.subtract).then_inc(exp_in, 1)

            def softmax_out(n_exp, choices, first, n_exp_round):
                dve.wait_ge(exp_out, n_exp_round)
                link(v.tensor_reduce(sum_e[:, :], ex[:, :, 0:n_exp], AX.X, ALU.add))
                link(v.reciprocal(rsum_e[:, :], sum_e[:, :]))
                link(v.tensor_tensor(small[:, first:first + choices, :],
                                     ex[:, :, n_exp:n_exp + choices].rearrange("p t k -> p k t"),
                                     rsum_e[:, :].unsqueeze(1).broadcast_to([P, choices, TT]), ALU.mult))

            def mix_part(l, s, slot, part):
                (scans if part == 0 else quotient)(l, s, slot)

            input_of(0, None)
            dve.wait_ge(blank, 4)
            dve.wait_ge(in_const, 16 * 12)
            go(v.tensor_copy(iota16[:, :], iota[:, :]))
            link(v.tensor_scalar(token[:, :], tbl8[:, :], pcol[:, 0:1], None, ALU.add))
            dve.wait_ge(bias_in, 16 * 6)
            split(biasp[:, :, 0], biasp[:, :, 1], biasp[:, :, 2], bias[:, :, :], biasr[:, :, :], bias_split)

            route_top2(0, 1)

            for l in range(1, LAYERS):
                exponent(l)

            def weigh_input(e, slot):
                for h in range(2):
                    q = 2 * e + h
                    dve.wait_ge(f0.w_done, q + 1)
                    if not (isinstance(q, int) and q < 2):
                        dve.wait_ge(f0.h_used, q - 1)
                    v.tensor_tensor(hid[:, h, :, :], yT[:, :, h * HALF:(h + 1) * HALF],
                                    ps_w[:, :].unsqueeze(1).broadcast_to([P, KC, HALF]),
                                    ALU.mult).then_inc(f0.h_ready, 1)
                    mix_part(1, e, slot, h)
            over_pairs(dve, E, weigh_input)

            def gated_units(f, has_up, l_mix):
                def body(j, slot, mixing):
                    for h in range(2):
                        q = 2 * j + h
                        dve.wait_ge(f.g_read, q + 1)
                        src = act_h[:, h, :]
                        if has_up:
                            dve.wait_ge(f.u_done, q + 1)
                            if not (isinstance(q, int) and q < 2):
                                dve.wait_ge(f.h_ready, q - 1)
                            v.tensor_tensor(prod_h[:, h, :], act_h[:, h, :], ps_u[:, :], ALU.mult).then_inc(f.u_read, 1)
                            dve.wait_ge(f.u_read, q + 1)
                            src = prod_h[:, h, :]
                        dve.wait_ge(f.w_done, q + 1)
                        if not (isinstance(q, int) and q < 2):
                            dve.wait_ge(f.h_used, q - 1)
                        v.tensor_tensor(hid[:, h, 0, :], src, ps_w[:, :], ALU.mult).then_inc(f.h_ready, 1)
                        if mixing is not None:
                            mix_part(l_mix, mixing, slot, h)
                body(0, 0, None)
                body(1, 1, None)
                with dve.Fori(1, f.n // 2) as i:
                    for slot in range(2):
                        body(2 * i + slot, slot, None if l_mix is None else 2 * i + (slot - 2))
                if f.n % 2:
                    body(f.n - 1, 0, None)

            input_of(1, f0)
            dve.wait_ge(lg_done, 2)
            link(v.tensor_copy(lg[:, :, 0:E], ps_m[:, 0:TT * E].rearrange("p (k e) -> p k e", e=E)))
            top8(lg[:, :, 0:E])
            softmax_in(E, 2)
            top8_index(lg[:, :, 0:E])
            one_hots(2, E, lambda ins: ins.then_inc(rank_in, 1))
            softmax_out(E, 2, 3, 2)
            dve.wait_ge(rank_done, 1)
            n1 = 2 * TT * E
            by_e = "p (k e) -> p e k"
            link(v.tensor_copy(tot[:, 0:n1].rearrange("p (e k) -> p e k", e=E), ps_u[:, 0:n1].rearrange(by_e, e=E)))
            link(v.tensor_tensor_scan(cum[:, 0:n1], scanmask1[:, :], tot[:, 0:n1], 0.0, ALU.mult, ALU.add))
            link(v.tensor_tensor(cum[:, 0:n1].rearrange("p (e k) -> p e k", e=E),
                                 cum[:, 0:n1].rearrange("p (e k) -> p e k", e=E),
                                 ps_g[:, 0:n1].rearrange(by_e, e=E), ALU.add))
            link(v.tensor_scalar(cum[:, 0:n1], cum[:, 0:n1], float(CAP), None, ALU.is_le))
            for k in range(2):
                link(weigh([r1, r2][k][:, :, 0:E], k, small[:, 3 + k, :], E))
                link(v.tensor_tensor([r1, r2][k][:, :, 0:E], [r1, r2][k][:, :, 0:E],
                                     cum[:, 0:n1].rearrange("p (e k) -> p k e", e=E)[:, k * TT:(k + 1) * TT, :],
                                     ALU.mult))
            link(v.tensor_tensor(gates[:, :, 0:E], r1[:, :, 0:E], r2[:, :, 0:E], ALU.add))
            split_gates(1, E + 1)
            gated_units(f1, True, 2)

            input_of(2, f1)
            route_top2(2, 3)
            gated_units(f2, False, 3)

            input_of(3, f2)
            dve.wait_ge(lg_done, 4)
            link(v.tensor_copy(lg[:, :, :], ps_m[:, 0:TT * (E3 + 1)].rearrange("p (k e) -> p k e", e=E3 + 1)))
            v.tensor_copy(small[:, 7, :], lg[:, :, E3]).then_inc(sgate_in, 1)
            top8(lg[:, :, 0:E3])
            top8_index(lg[:, :, 0:E3])
            one_hots(K3, E3, lambda ins: ins.then_inc(rank_in, 1))
            softmax_in(E3, K3)
            dve.wait_ge(rank_done, 2)
            link(v.tensor_copy(tot[:, :].rearrange("p (e k) -> p e k", e=E3),
                               ps_u[:, 0:TT * E3].rearrange("p (k e) -> p e k", e=E3)))
            link(v.tensor_tensor_scan(cum[:, :], scanmask3[:, :], tot[:, :], 0.0, ALU.mult, ALU.add))
            cume = cum[:, :].rearrange("p (e k) -> p e k", e=E3)
            over = r1[:, :, :].rearrange("p k e -> p (k e)").rearrange("p (e k) -> p e k", e=E3)
            link(v.tensor_tensor(over, cume[:, :, TT - 1:TT].broadcast_to([P, E3, TT]),
                                 tbl8[:, :].unsqueeze(1).broadcast_to([P, E3, TT]), ALU.is_gt))
            link(v.tensor_reduce(tiles3[:, :], over, AX.X, ALU.add))
            link(v.tensor_tensor_scan(tincl[:, :], ones60[:, :], tiles3[:, :], 0.0, ALU.mult, ALU.add))
            go(v.tensor_tensor(tbase[:, :], tincl[:, :], tiles3[:, :], ALU.subtract))
            link(v.tensor_scalar(r2[:, 0, :], tincl[:, :], pcol[:, 0:1], None, ALU.is_le))
            link(v.tensor_reduce(te_f[:, :], r2[:, 0, :], AX.X, ALU.add))
            v.tensor_scalar(te_i[:, :], te_f[:, :], float(E3 - 1), None, ALU.min).then_inc(te_ready, 1)
            link(v.scalar_tensor_tensor(r1[:, :, :], tbase[:, :].unsqueeze(1).broadcast_to([P, TT, E3]), float(P),
                                        cum[:, :].rearrange("p (e k) -> p k e", e=E3), ALU.mult, ALU.add))
            link(v.tensor_tensor(r2[:, :, :], r1[:, :, :],
                                 ps_g[:, 0:TT * E3].rearrange("p (k e) -> p k e", e=E3), ALU.add))
            link(v.tensor_tensor(slots4[:, :, :, :], oh[:, :, :, :],
                                 r2[:, :, :].unsqueeze(1).broadcast_to([P, K3, TT, E3]), ALU.mult))
            link(v.tensor_reduce(place_f[:, 0, :], slots4[:, :, :, :].rearrange("p k t e -> p (k t) e"),
                                 AX.X, ALU.add))
            link(v.tensor_copy(slot_i[:, :], place_f[:, 0, :]))
            go(v.tensor_scalar(place_i[:, 0, :], slot_i[:, :], 7, None, ALU.arith_shift_right))
            link(v.tensor_scalar(place_i[:, 1, :], slot_i[:, :], P - 1, None, ALU.bitwise_and))
            link(v.tensor_copy(place_f[:, 1:3, :], place_i[:, :, :]))
            for k in range(K3 * TT):
                go(v.tensor_scalar(in_tile[:, k, :], iota16[:, :], place_f[:, 2, k:k + 1], None, ALU.is_equal))
                v.tensor_scalar(of_tile[:, k, :], iota16[:, 0:TILE_COLS], place_f[:, 1, k:k + 1],
                                token[:, k % TT:k % TT + 1], ALU.is_equal, ALU.mult).then_inc(onehots, 1)
            dve.wait_ge(tok_ps, 1)
            v.tensor_copy(tok_i[:, 0:TILE_COLS], ps_m[:, 0:TILE_COLS]).then_inc(tok_ready, 1)
            softmax_out(E3, K3, 0, 4)
            dve.wait_ge(sgate_out, 1)
            split_gates(3, 1)

            gu_bank = [ps_acc[:, 1, 0:2 * I1], ps_acc[:, 1, HALF:HALF + 2 * I1]]
            ht_bank = [ps_g[0:IH, 0:2 * P], ps_u[0:IH, 0:2 * P]]

            def tile_step(j, r):
                static = isinstance(j, int)
                if not static or j < MAXTILES:
                    dve.wait_ge(sg_sb, j + 1)
                    if not (static and j < 2):
                        dve.wait_ge(ht_ps, j - 1)
                    v.tensor_tensor(h3[:, r % 2, :], sg3[:, r % 2, :], gu_bank[r % 2][:, I1:2 * I1],
                                    ALU.mult).then_inc(h_sb, 1)
                if not static or 0 <= j - 1 < MAXTILES:
                    dve.wait_ge(ht_ps, j)
                    if not (static and j - 1 < 2):
                        dve.wait_ge(o_ps, j - 2)
                    v.tensor_copy(hT3[:, (r - 1) % 2, :], ht_bank[(r - 1) % 2]).then_inc(ht_sb, 1)
            for j in range(3):
                tile_step(j, j % 2)
            n_loop = (MAXTILES - 3) // RING
            with dve.Fori(0, n_loop) as i:
                for k in range(RING):
                    tile_step(RING * i + (3 + k), (3 + k) % 2)
            for j in range(3 + RING * n_loop, MAXTILES + 1):
                tile_step(j, j % 2)

            def combine(k):
                for c in range(K3):
                    w = small[:, c, k:k + 1]
                    if c == 0:
                        dve.wait_ge(yk_in[k], 16 * K3)
                        ins = v.tensor_scalar(fin[:, k, :], yk[:, k * K3, :], w, None, ALU.mult)
                    else:
                        dve.wait_ge(comb_step, K3 * k + c)
                        ins = v.scalar_tensor_tensor(fin[:, k, :], yk[:, k * K3 + c, :], w, fin[:, k, :],
                                                     ALU.mult, ALU.add)
                    ins.then_inc(comb_step, 1)

            gated_units(f3, True, None)
            for k in range(TT):
                combine(k)
            dve.wait_ge(f3.h_used, 2 * CH3)
            for c, h in QUARTERS:
                v.tensor_tensor(quarter(xT, c, h), quarter(xT, c, h), quarter(ps_acc, c, h),
                                ALU.add).then_inc(x_final, 1)
            for k in range(TT):
                dve.wait_ge(xo_ps, k + 1)
                v.tensor_tensor(fin[:, k, :], fin[:, k, :], [ps_g, ps_u][k % 2][:, 0:C], ALU.add).then_inc(fin_ready, 1)


def kernel(**inputs):
    import ml_dtypes
    import concourse.bacc as _bacc
    from concourse.bass_utils import run_bass_kernel_spmd as _run

    a = {k: np.ascontiguousarray(v) for k, v in inputs.items()}

    def channel_major(x):
        return np.ascontiguousarray(x.reshape(-1, KC, P).transpose(2, 1, 0))

    def lhs(w):
        return w.reshape(-1, P, KC, P).transpose(0, 3, 2, 1).reshape(-1, P, C)

    def padded(w, rows):
        out = np.zeros((rows, w.shape[1]), w.dtype)
        out[:w.shape[0]] = w
        return out

    w_u = [np.stack([a[f"L{l}_cond_{n}"].reshape(KC, P) for l in range(LAYERS)]) for n in "wu"]
    wd1 = a["L1_ffn_Wd"].transpose(0, 2, 1).reshape(CH1, P, C)
    l1 = [lhs(a["L1_ffn_Wg"].reshape(-1, C)), lhs(a["L1_ffn_Wu"].reshape(-1, C)), wd1]
    w1 = np.concatenate([a["L2_ffn_w1"].transpose(0, 2, 1).reshape(-1, C), a["L2_ffn_shared_w1"].T])
    w2 = np.concatenate([a["L2_ffn_w2"].reshape(-1, C), a["L2_ffn_shared_w2"]]).reshape(CH2, P, C)
    gu = a["L3_ffn_se_gate_up_w"]
    sh = [lhs(padded(gu[:ISH], CH3 * P)), lhs(padded(gu[ISH:], CH3 * P)),
          padded(a["L3_ffn_se_down_w"].T, CH3 * P).reshape(CH3, P, C)]
    b1 = np.concatenate([a["L2_ffn_b1"], a["L2_ffn_shared_b1"].reshape(-1, P)])

    def cols(w):
        return w.reshape(KC, P, -1).transpose(1, 0, 2)

    routers = np.stack([cols(a["L0_ffn_Wr"]), cols(a["L1_ffn_Wr"].T), cols(a["L2_ffn_gate_w"])], 1)
    router3 = np.concatenate([cols(a["L3_ffn_gate_w"].T), cols(a["L3_ffn_shared_gate_w"].T)], 2)

    f32, bf16 = np.float32, ml_dtypes.bfloat16
    q = np.arange(P)
    tri = np.stack([-1.0 * (q[:, None] > q), -1.0 * (q[:, None] >= q), np.ones((P, P))], 1).astype(bf16)
    rows = list(range(E)) + [0] * CH1 + list(range(CH2)) + [0]
    sel = np.zeros((P, len(rows), P), bf16)
    for j, row in enumerate(rows):
        expert = np.full(P, min(row, E))
        if E <= j < E + CH1:
            expert = (P * (j - E) + q) // I1
        for part in range(3):
            sel[part * GCOLS + expert, j, q] = 1
    n1, n3 = 2 * TT, TT
    arrays = {
        "cond": a["cond_512"], "wu": np.stack(w_u).transpose(3, 0, 1, 2),
        "kvT": channel_major(a["fside_BxSxS_0"]), "xT": channel_major(a["x"]),
        "ident": np.eye(P, dtype=f32), "identb": np.eye(P, dtype=bf16), "tri": tri, "sel": sel,
        "iota": np.tile(q.astype(f32), (P, 1)), "pcol": q.astype(f32)[:, None],
        "scanmask1": np.tile((np.arange(E * n1) % n1 > 0).astype(f32), (P, 1)),
        "scanmask3": np.tile((np.arange(E3 * n3) % n3 > 0).astype(f32), (P, 1)),
        "tbl8": np.tile((P * np.arange(TT)).astype(f32), (P, 1)),
        "routers": routers, "router3": router3, "b1": b1.T,
        "be": a["L0_ffn_be"], "b2": np.concatenate([a["L2_ffn_b2"], a["L2_ffn_shared_b2"][None]]),
        "we": a["L0_ffn_We"].reshape(E, KC, P, C).transpose(0, 2, 1, 3).reshape(E * P, KC * C),
        "w_l1": np.concatenate(l1, 2).reshape(CH1 * P, 3 * C),
        "w_l2": np.concatenate([lhs(w1), w2], 2).reshape(CH2 * P, 2 * C),
        "w_sh": np.concatenate(sh, 2).reshape(CH3 * P, 3 * C),
        "w13": a["L3_ffn_w13"].reshape(E3, 2 * I1, KC, P).transpose(0, 3, 2, 1).reshape(E3 * P, KC * 2 * I1),
        "w2": a["L3_ffn_w2"].reshape(E3, C, 2, IH).transpose(0, 3, 2, 1).reshape(E3 * IH, 2 * C),
    }
    arrays = {k: np.ascontiguousarray(v) for k, v in arrays.items()}

    nc = _bacc.Bacc("TRN2", target_bir_lowering=False, num_devices=1)
    t = {k: nc.dram_tensor(f"in_{k}", v.shape, mybir.dt.from_np(v.dtype), kind="ExternalInput").ap()
         for k, v in arrays.items()}
    t["out"] = nc.dram_tensor("out", (N, C), F32, kind="ExternalOutput").ap()
    t["te"] = nc.dram_tensor("tile_experts", (P, 1), I32, kind="Internal").ap()
    t["y_rows"] = nc.dram_tensor("y_rows", (N, C), F32, kind="Internal").ap()
    t["o_rows"] = nc.dram_tensor("o_rows", (MAXTILES * P, C), F32, kind="Internal").ap()
    build(nc, t)
    r = _run(nc, [{f"in_{k}": v for k, v in arrays.items()}], core_ids=[0])
    return r.results[0]["out"].reshape(B, T, C)
```

```python
from contextlib import ExitStack

import numpy as np

import concourse.bass as bass
from concourse import mybir

P = 128
F32 = mybir.dt.float32
BF16 = mybir.dt.bfloat16
F32R = mybir.dt.float32r
F16 = mybir.dt.float16
I32 = mybir.dt.int32
U32 = mybir.dt.uint32
ALU = mybir.AluOpType
ACT = mybir.ActivationFunctionType
AX = mybir.AxisListType

B, T, C = 4, 256, 256
N = B * T
KC = C // P
TT = N // P
HALF = 512
LAYERS = 4
SEGS = KC * B
E = 8
GCOLS = 16
I1 = 176
CAP = int(1.25 * (N * 2 / E))
CH1 = E * I1 // P
CH2 = E + 2
E3, K3 = 60, 4
ISH = 704
CH3 = -(-ISH // P)
IH = I1 // 2
MAXTILES = E3 + (K3 * N - E3) // P
TILE_COLS = MAXTILES + MAXTILES % 2
RING = 6
SUMS = 6
NOWS = 2
QUOT = 3


def build(nc, t):
    with ExitStack() as ctx:
        def sb(name, shape, dt=F32):
            return ctx.enter_context(nc.sbuf_tensor(name, shape, dt))

        def sem(name):
            return ctx.enter_context(nc.semaphore(name))

        xT = sb("xT", [P, KC, N])
        kv = sb("kv", [P, KC, N])
        ek = sb("ek", [P, KC, N])
        ekv = sb("ekv", [P, KC, N])
        ekr = sb("ekr", [P, KC, N])
        ekvr = sb("ekvr", [P, KC, N])
        euk = sb("euk", [P, LAYERS, KC, N])
        mix = sb("mix", [P, KC, N])
        with nc.sbuf_tensor("yT", [P, KC, N], F32) as yT:
            pass
        y_lo = sb("y_lo", [P, KC, N], F32R)
        ident = sb("ident", [P, P])
        identb = sb("identb", [P, P], BF16)
        tri = sb("tri", [P, 3, P], BF16)
        sel = sb("sel", [P, E + CH1 + CH2 + 1, P], BF16)
        iota = sb("iota", [P, P])
        pcol = sb("pcol", [P, 1])
        scanmask1 = sb("scanmask1", [P, E * 2 * TT])
        scanmask3 = sb("scanmask3", [P, E3 * TT])
        tbl8 = sb("tbl8", [P, TT])
        wu = sb("wu", [P, 2, LAYERS, KC])
        cond = sb("cond", [P, B, 64])
        tf = sb("tf", [P, B])
        tfhalf = sb("tfhalf", [P, B])
        tfout = sb("tfout", [P, B])
        tfout8 = sb("tfout8", [P, SEGS])
        ew = sb("ew", [P, LAYERS, KC])
        base_decay = sb("base_decay", [P, LAYERS, KC])
        decay = sb("decay", [P, LAYERS, SEGS])
        nf = sb("nf", [P, 2, T])
        nb = sb("nb", [P, 2, T])
        df = sb("df", [P, 2, T])
        db = sb("db", [P, 2, T])
        rden = sb("rden", [P, 2, T])
        now_d = sb("now_d", [P, T])
        now_n = sb("now_n", [P, T])
        routers = sb("routers", [P, 3, KC, E])
        router3 = sb("router3", [P, KC, E3 + 1])
        bias = sb("bias", [P, 2, C])
        biasp = sb("biasp", [P, 2, 3, C], BF16)
        biasr = sb("biasr", [P, 2, C])
        b1 = sb("b1", [P, CH2])
        b1_col = sb("b1_col", [P, 2])
        wring = sb("wring", [P, 2, 3 * C])
        w_hi = sb("w_hi", [P, 2, 3 * C], F32R)
        w_lo = sb("w_lo", [P, 2, 3 * C], F32R)
        y_hi = sb("y_hi", [P, KC, N], F32R)
        work = sb("work", [P, 2, KC, HALF])
        hid0 = work[:, :, :, :]
        now0 = work[:, 0, :, :].rearrange("p k (a t) -> p k a t", t=T)
        act_h, prod_h = work[:, 0], work[:, 1]
        hid = sb("hid", [P, 2, 2, HALF], F32R)
        gates = sb("gates", [P, TT, E + 1])
        g3 = sb("g3", [P, TT, P], BF16)
        gT = sb("gT", [P, N], BF16)
        lg = sb("lg", [P, TT, E3 + 1])
        mx = sb("mx", [P, TT, 8])
        ix = sb("ix", [P, TT, 8], U32)
        ixf = sb("ixf", [P, K3, TT])
        small = sb("small", [P, 8, TT])
        sum_e = sb("sum_e", [P, TT])
        rsum_e = sb("rsum_e", [P, TT])
        oh = sb("oh", [P, K3, TT, E3], BF16)
        ex = sb("ex", [P, TT, E3 + K3])
        token = sb("token", [P, TT])
        r1 = sb("r1", [P, TT, E3])
        r2 = sb("r2", [P, TT, E3])
        tot = sb("tot", [P, E3 * TT])
        cum = sb("cum", [P, E3 * TT])
        tiles3 = sb("tiles3", [P, E3])
        tincl = sb("tincl", [P, E3])
        tbase = sb("tbase", [P, E3])
        ones60 = sb("ones60", [P, E3])
        te_f = sb("te_f", [P, 1])
        te_i = sb("te_i", [P, 1], I32)
        te_row = sb("te_row", [1, P], I32)
        place_i = sb("place_i", [P, 2, K3 * TT], I32)
        place_f = sb("place_f", [P, 3, K3 * TT])
        slot_i = sb("slot_i", [P, K3 * TT], I32)
        tok_i = sb("tok_i", [P, P], I32)
        tok_col = sb("tok_col", [P, RING], I32)
        xg_hi = sb("xg_hi", [P, 2, C], F32R)
        sg3 = sb("sg3", [P, 2, I1])
        h3 = sb("h3", [P, 2, I1])
        hT3 = sb("hT3", [IH, 2, 2 * P])
        o3 = sb("o3", [P, RING, C])

        weights3 = [tile.rearrange("p c n -> p (c n)") for tile in
                    (ek[:, :, :], ekv[:, :, :], ekvr[:, :, :], kv[:, :, :], euk[:, 0], euk[:, 1])]
        xg = euk[:, 3, :, :].rearrange("p c (k t) -> p (c k) t", t=C)
        w13 = [tile[:, 0:KC * 2 * I1] for tile in weights3]
        w2 = [tile[0:IH, KC * 2 * I1:KC * 2 * I1 + 2 * C] for tile in weights3]

        hid_flat = hid[:, :, :, :].rearrange("p h s n -> p (h s n)")

        yk = euk[:, :, :, :].rearrange("p l c (k t) -> p (l c k) t", t=C)
        fin = mix[:, :, :].rearrange("p c (k t) -> p (c k) t", t=C)
        y_tok = euk[:, 2, :, :].rearrange("p c (k t) -> p (c k) t", t=C)

        w13_hi = hid_flat[:, 0:4 * KC * I1].rearrange("p (s m) -> p s m", s=2)
        xg_lo = hid_flat[:, 4 * KC * I1:4 * KC * I1 + 2 * C].rearrange("p (s m) -> p s m", s=2)
        w13_lo = w_lo[:, :, 0:2 * KC * I1]

        in_tile = (ekr[:, :, :].rearrange("p c n -> p (c n)").bitcast(F16)
                   .rearrange("p (k m) -> p k m", m=P))
        of_tile = (mix[:, :, :].rearrange("p c n -> p (c n)").bitcast(F16)[:, 0:K3 * TT * TILE_COLS]
                   .rearrange("p (k m) -> p k m", m=TILE_COLS))
        slots4 = (work[:, :, :, :].rearrange("p h c n -> p (h c n)")[:, 0:K3 * TT * E3]
                  .rearrange("p (k t e) -> p k t e", k=K3, e=E3))

        ps_acc = ctx.enter_context(nc.psum_tensor("ps_acc", [P, KC, N], F32))
        ps_g = ctx.enter_context(nc.psum_tensor("ps_g", [P, HALF], F32))
        ps_u = ctx.enter_context(nc.psum_tensor("ps_u", [P, HALF], F32))
        ps_w = ctx.enter_context(nc.psum_tensor("ps_w", [P, HALF], F32))
        ps_m = ctx.enter_context(nc.psum_tensor("ps_m", [P, HALF], F32))
        xt_bank = [ps_acc[:, 0, 0:C], ps_acc[:, 0, HALF:HALF + C]]
        gu_bank = [ps_acc[:, 1, 0:2 * I1], ps_acc[:, 1, HALF:HALF + 2 * I1]]
        ht_bank = [ps_g[0:IH, 0:2 * P], ps_u[0:IH, 0:2 * P]]
        o_bank = [ps_w[:, 0:C], ps_m[:, 0:C]]
        out_bank = [ps_g, ps_u, ps_w, ps_m]

        def ps_mix(s, par):
            return ([ps_w, ps_m] if isinstance(s, int) and s >= SEGS - 2 else [ps_g, ps_u])[par]

        ps_gates = [ps_w[:, :].bitcast(BF16), ps_m[:, :].bitcast(BF16)]

        in_cond, in_w, in_ident, in_x = sem("in_cond"), sem("in_w"), sem("in_ident"), sem("in_x")
        in_kv = [sem("in_kv0"), sem("in_kv1")]
        in_const = sem("in_const")
        tf_sum, tf_sig, dec_act = sem("tf_sum"), sem("tf_sig"), sem("dec_act")
        kmin, ek_ready, ekv_ready, ukmin, euk_ready = (sem("kmin"), sem("ek_ready"), sem("ekv_ready"),
                                                       sem("ukmin"), sem("euk_ready"))
        blank = sem("blank")
        scan_step = sem("scan_step")
        sum_step = sem("sum_step")
        sum0 = sem("sum0")
        m_step = sem("m_step")
        b1_ready = sem("b1_ready")
        x_upd, y_sig, y_ready = sem("x_upd"), sem("y_sig"), sem("y_ready")
        lg_done = sem("lg_done")
        dve_step = sem("dve_step")
        bias_in, bias_split = sem("bias_in"), sem("bias_split")
        exp_in, exp_out = sem("exp_in"), sem("exp_out")
        rank_in, rank_done = sem("rank_in"), sem("rank_done")
        gate_split, gT_ps, gT_ready = sem("gate_split"), sem("gT_ps"), sem("gT_ready")

        class Ffn:

            def __init__(self, name, chunks):
                self.n = chunks
                self.w_in = [sem(f"{name}_w_in0"), sem(f"{name}_w_in1")]
                self.g_done = sem(f"{name}_g_done")
                self.u_done = sem(f"{name}_u_done")
                self.w_done = sem(f"{name}_w_done")
                self.w_hi = sem(f"{name}_w_hi")
                self.w_lo = sem(f"{name}_w_lo")
                self.g_read = sem(f"{name}_g_read")
                self.u_read = sem(f"{name}_u_read")
                self.p_ready = sem(f"{name}_p_ready")
                self.h_hi = sem(f"{name}_h_hi")
                self.h_ready = sem(f"{name}_h_ready")
                self.h_used = sem(f"{name}_h_used")

        f0, f1, f2, f3 = Ffn("f0", E), Ffn("f1", CH1), Ffn("f2", CH2), Ffn("f3", CH3)
        f0.p_ready = f0.h_ready
        y_hi_ready, y_lo_ready = sem("y_hi_ready"), sem("y_lo_ready")

        yt_ps, yt_sb, yt_out = sem("yt_ps"), sem("yt_sb"), sem("yt_out")
        te_ready, te_out, te_in = sem("te_ready"), sem("te_out"), sem("te_in")
        slots_in, slots_ready = sem("slots_in"), sem("slots_ready")
        of_equal, of_token = sem("of_equal"), sem("of_token")
        onehots, tok_ps, tok_ready = sem("onehots"), sem("tok_ps"), sem("tok_ready")
        sgate_in, sgate_out = sem("sgate_in"), sem("sgate_out")
        w13_tile = [sem(f"w13_tile{r}") for r in range(RING)]
        w2_tile = [sem(f"w2_tile{r}") for r in range(RING)]
        x_tile = [sem(f"x_tile{r}") for r in range(RING)]
        o_pair = [sem(f"o_pair{r}") for r in range(RING // 2)]
        tcol, xt_ps, xt_sb, xt_lo = sem("tcol"), sem("xt_ps"), sem("xt_sb"), sem("xt_lo")
        wt_hi, wt_lo = sem("wt_hi"), sem("wt_lo")
        gu_ps, sg_sb, h_sb = sem("gu_ps"), sem("sg_sb"), sem("h_sb")
        ht_ps, ht_sb, o_ps, o_sb = sem("ht_ps"), sem("ht_sb"), sem("o_ps"), sem("o_sb")
        yk_in = [sem(f"yk_in{r}") for r in range(4)]
        x_final, xo_ps, fin_ready, out_done = sem("x_final"), sem("xo_ps"), sem("fin_ready"), sem("out_done")
        comb_step = sem("comb_step")

        consts = [(identb, "identb"), (tri, "tri"), (sel, "sel"), (iota, "iota"),
                  (pcol, "pcol"), (scanmask1, "scanmask1"), (scanmask3, "scanmask3"), (tbl8, "tbl8"),
                  (routers, "routers"), (router3, "router3"), (b1, "b1")]

        block = ctx.enter_context(nc.Block())

        def over_pairs(eng, n, body, last_peeled=False):
            looped = n // 2 - (1 if last_peeled and n % 2 == 0 else 0)
            body(0, 0)
            body(1, 1)
            with eng.Fori(1, looped) as i:
                body(2 * i, 0)
                body(2 * i + 1, 1)
            for j in range(2 * looped, n):
                body(j, j % 2)

        def over_mix(eng, n, body):
            body(0, 0)
            body(1, 1)
            with eng.Fori(1, SEGS // 2) as i:
                body(2 * i, 0)
                body(2 * i + 1, 1)
            for j in range(SEGS, n):
                body(j, j % 2)

        def seg(tile, s):
            return tile.rearrange("p c (b t) -> p (c b) t", t=T)[:, bass.ds(s, 1), :].rearrange("p a t -> p (a t)")

        def three(lhs_hi, lhs_lo, rhs_hi, rhs_lo):
            return (lhs_hi, rhs_hi), (lhs_hi, rhs_lo), (lhs_lo, rhs_hi)

        def by_seq(rows):
            return rows.rearrange("p (b t) -> p b t", t=T)

        QUARTERS = [(c, h) for h in range(2) for c in range(KC)]

        def quarter(tile, c, h):
            return tile[:, c, h * HALF:(h + 1) * HALF]

        @block.sync
        def _(sp):
            sp.dma_start(cond[:, :, :], t["cond"].rearrange("b d -> (b d)").partition_broadcast(P)
                         .rearrange("p (b d) -> p b d", b=B)).then_inc(in_cond, 16)
            sp.dma_start(wu[:, :, :, :], t["wu"]).then_inc(in_w, 16)
            sp.dma_start(ident[:, :], t["ident"]).then_inc(in_ident, 16)
            for c in range(KC):
                sp.dma_start(kv[:, c, :], t["kvT"][:, c, :]).then_inc(in_kv[c], 16)
            sp.dma_start(xT[:, :, :], t["xT"]).then_inc(in_x, 16)
            for tile, name in consts:
                sp.dma_start(tile[:], t[name]).then_inc(in_const, 16)
            sp.wait_ge(blank, 1)
            for part in range(3):
                r = part * GCOLS
                sp.dma_start(bias[r:r + E, 0, :], t["be"]).then_inc(bias_in, 16)
                sp.dma_start(bias[r:r + E + 1, 1, :], t["b2"]).then_inc(bias_in, 16)

            def load_chunks(f, src, width, chunks=None, used=None):
                used, per_chunk = (f.w_lo, 2) if used is None else used

                def body(j, slot):
                    if not (isinstance(j, int) and j < 2):
                        sp.wait_ge(used, per_chunk * (j - 1))
                    sp.dma_start(wring[:, slot, 0:width],
                                 src[bass.ds(j * P, P), :]).then_inc(f.w_in[slot], 16)
                if chunks is None:
                    over_pairs(sp, f.n, body)
                else:
                    for j in chunks:
                        body(j, j % 2)

            load_chunks(f0, t["we"], KC * C, used=(f0.h_used, 2))
            sp.wait_ge(f0.h_used, 2 * f0.n)
            load_chunks(f1, t["w_l1"], 3 * C)
            sp.wait_ge(f1.w_lo, 2 * f1.n)
            load_chunks(f2, t["w_l2"], 2 * C)
            sp.wait_ge(f2.w_lo, 2 * f2.n)
            load_chunks(f3, t["w_sh"], 3 * C, range(2))

            sp.wait_ge(yt_sb, 4)
            sp.dma_start(t["y_rows"].rearrange("(k p) c -> p k c", p=P), y_tok[:, :, :]).then_inc(yt_out, 16)
            sp.wait_ge(te_ready, 1)
            sp.dma_start(t["te"], te_i[:, :]).then_inc(te_out, 16)
            sp.wait_ge(te_out, 16)
            sp.dma_start(te_row[:, :], t["te"].rearrange("p a -> a p")).then_inc(te_in, 16)
            sp.wait_ge(te_in, 16)

            def load_tile(j, r):
                e = sp.value_load(te_row[0:1, bass.ds(j, 1)], min_val=0, max_val=E3 - 1)
                if not (isinstance(j, int) and j < RING):
                    sp.wait_ge(o_ps, j - (RING - 1))
                sp.dma_start(w13[r], t["w13"][bass.ds(e * P, P), :]).then_inc(w13_tile[r], 16)
                sp.dma_start(w2[r], t["w2"][bass.ds(e * IH, IH), :]).then_inc(w2_tile[r], 16)

            for j in range(RING):
                load_tile(j, j)
            n_loop = MAXTILES // RING
            with sp.Fori(1, n_loop) as i:
                for r in range(RING):
                    load_tile(RING * i + r, r)
            for j in range(RING * n_loop, MAXTILES):
                load_tile(j, j % RING)

            load_chunks(f3, t["w_sh"], 3 * C, range(2, f3.n))
            rows = t["out"].rearrange("(k p) c -> p k c", p=P)
            for k in range(0, TT, 2):
                sp.wait_ge(fin_ready, k + 2)
                sp.dma_start(rows[:, k:k + 2, :], fin[:, k:k + 2, :]).then_inc(out_done, 16)
            sp.wait_ge(out_done, 16 * (TT // 2))

        @block.tensor
        def _(pe):
            mm = nc.tensor.matmul
            pe.wait_ge(in_ident, 16)

            def router(l, w, n):
                for k in range(TT):
                    if k % (TT // 2) == 0:
                        pe.wait_ge(y_ready, 4 * l + (2 if k == 0 else 4))
                    for c in range(KC):
                        last = mm(ps_m[:, k * n:(k + 1) * n], yT[:, c, k * P:(k + 1) * P], w[:, c, :],
                                  start=(c == 0), stop=(c == KC - 1))
                last.then_inc(lg_done, 1)

            def turn_gates(l):
                pe.wait_ge(gate_split, l + 1)
                for k in range(TT):
                    half, col = k // (TT // 2), k % (TT // 2) * P
                    last = nc.tensor.transpose(ps_gates[half][:, col:col + P], g3[:, k, :], identb[:, :])
                    if k % (TT // 2) == TT // 2 - 1:
                        last.then_inc(gT_ps, 1)

            def add_bias(l, b):
                pe.wait_ge(bias_split, 1)
                for h in range(2):
                    pe.wait_ge(gT_ready, 2 * l + h + 1)
                    for c in range(KC):
                        for part in range(3):
                            mm(quarter(ps_acc, c, h), biasp[:, b, part, c * P:(c + 1) * P],
                               gT[:, h * HALF:(h + 1) * HALF], start=(part == 0), stop=False)

            def spread(f, q, row, h):
                if not (isinstance(q, int) and q < 1):
                    pe.wait_ge(f.p_ready, q)
                mm(ps_w[:, :], sel[:, bass.ds(row, 1), :].rearrange("p a m -> p (a m)"),
                   gT[:, h * HALF:(h + 1) * HALF], start=True, stop=True).then_inc(f.w_done, 1)

            def add_terms(g, par):
                if not (isinstance(g, int) and not 2 <= g < SEGS - 2):
                    pe.wait_ge(m_step, QUOT * (g - 1))
                for side, terms in enumerate(((nf, nb, now0[:, 0]), (df, db, now0[:, 1]))):
                    pe.wait_ge(scan_step, 4 * g + 2 * side + 2)
                    for n, term in enumerate(terms):
                        if n == 2:
                            pe.wait_ge(sum_step, NOWS * g + NOWS)
                        last = mm(ps_mix(g, par)[:, side * T:(side + 1) * T], ident[:, :], term[:, par, :],
                                  start=(n == 0), stop=(n == 2))
                last.then_inc(sum0, 1)

            over_pairs(pe, SEGS, add_terms, last_peeled=True)
            pe.wait_ge(in_const, 16 * len(consts))

            router(0, routers[:, 0], E)
            turn_gates(0)
            pe.wait_ge(gT_ready, 1)
            spread(f0, 0, 0, 0)
            add_bias(0, 0)

            def layer0(e, slot):
                for h in range(2):
                    q = 2 * e + h
                    if h == 0:
                        spread(f0, q + 1, e, 1)
                    elif not (isinstance(e, int) and e == E - 1):
                        spread(f0, q + 1, e + 1, 0)
                    if h == 0:
                        pe.wait_ge(f0.w_in[slot], 8 * e + (16 - 8 * slot))
                    pe.wait_ge(f0.h_ready, q + 1)
                    for c in range(KC):
                        for k in range(KC):
                            last = mm(quarter(ps_acc, c, h), wring[:, slot, k * C + c * P:k * C + (c + 1) * P],
                                      hid0[:, h, k, :], start=False,
                                      stop=(k == KC - 1 and isinstance(e, int) and e == E - 1))
                    last.then_inc(f0.h_used, 1)

            over_pairs(pe, E, layer0, last_peeled=True)

            def gated(f, l, has_up, row_of, opening, bias_row=None):
                def down(q, j, slot, h, last_one):
                    if h == 0:
                        pe.wait_ge(f.w_hi, 2 * j + 2)
                        pe.wait_ge(f.w_lo, 2 * j + 2)
                    pe.wait_ge(f.h_ready, q + 1)
                    off = (2 if has_up else 1) * C
                    first = isinstance(j, int) and j == 0 and bias_row is None
                    for c in range(KC):
                        cols = slice(off + c * P, off + (c + 1) * P)
                        for n, (w, x) in enumerate(three(w_hi[:, slot, cols], w_lo[:, slot, cols],
                                                         hid[:, h, 0, :], hid[:, h, 1, :])):
                            last = mm(quarter(ps_acc, c, h), w, x, start=first and n == 0,
                                      stop=last_one and n == 2)
                    last.then_inc(f.h_used, 1)

                def up(ps, off, slot, h):
                    for k in range(KC):
                        cols = slice(off + k * P, off + (k + 1) * P)
                        for n, (w, x) in enumerate(three(w_hi[:, slot, cols], w_lo[:, slot, cols],
                                                         quarter(y_hi, k, h), quarter(y_lo, k, h))):
                            last = mm(ps[:, :], w, x, start=(k == 0 and n == 0), stop=(k == KC - 1 and n == 2))
                    return last

                def body(j, slot):
                    for h in range(2):
                        q = 2 * j + h
                        start = isinstance(q, int) and q < 1
                        if h == 0:
                            pe.wait_ge(f.w_hi, 2 * j + 1)
                            pe.wait_ge(f.w_lo, 2 * j + 1)
                        if isinstance(j, int) and j == 0:
                            pe.wait_ge(y_hi_ready, 4 * l - 2 + 2 * h)
                            pe.wait_ge(y_lo_ready, 4 * l - 2 + 2 * h)
                        if not start:
                            pe.wait_ge(f.g_read, q)
                        up(ps_g, 0, slot, h).then_inc(f.g_done, 1)
                        if has_up:
                            if not start:
                                pe.wait_ge(f.u_read, q)
                            up(ps_u, C, slot, h).then_inc(f.u_done, 1)
                        if start:
                            opening()
                        if isinstance(j, int) and j == 0:
                            pe.wait_ge(gT_ready, 2 * l + h + 1)
                        spread(f, q, row_of(j), h)
                        if start and bias_row is not None:
                            add_bias(l, bias_row)
                        if not start:
                            down(q - 1, j if h else j - 1, slot if h else 1 - slot, 1 - h,
                                 isinstance(q, int) and q == 2 * f.n - 1)
                n = f.n
                over_pairs(pe, n, body, last_peeled=True)
                down(2 * n - 1, n - 1, (n - 1) % 2, 1, True)

            router(1, routers[:, 1], E)
            for k in range(2):
                pe.wait_ge(rank_in, k + 1)
                for place, kind in ((1, 0), (2, 2)):
                    last = mm(ps_m[:, (2 * place + k) * TT * E:(2 * place + k + 1) * TT * E],
                              tri[:, kind, :], oh[:, k, :, 0:E], start=True, stop=True)
            last.then_inc(rank_done, 1)
            gated(f1, 1, True, lambda j: j + E, lambda: turn_gates(1))

            router(2, routers[:, 2], E)
            gated(f2, 2, False, lambda j: j + (E + CH1), lambda: turn_gates(2), 1)

            router(3, router3, E3 + 1)
            for k in range(TT):
                for c in range(KC):
                    last = nc.tensor.transpose(ps_acc[:, k // 4, (k % 4) * C + c * P:(k % 4) * C + (c + 1) * P],
                                               yT[:, c, k * P:(k + 1) * P], ident[:, :])
                if k % 2:
                    last.then_inc(yt_ps, 1)
            for k in range(K3):
                pe.wait_ge(rank_in, 3 + k)
                for ps, kind in ((ps_g, 1), (ps_u, 2)):
                    last = mm(ps[:, 0:TT * E3], tri[:, kind, :], oh[:, k, :, :].rearrange("p t e -> p (t e)"),
                              start=(k == 0), stop=(k == K3 - 1))
            last.then_inc(rank_done, 1)
            for k in range(K3 * TT):
                if k % TT == 0:
                    pe.wait_ge(onehots, k // TT + 1)
                    pe.wait_ge(of_token, k // TT + 1)
                last = mm(ps_m[:, 0:TILE_COLS], in_tile[:, k, :], of_tile[:, k, :], start=(k == 0),
                          stop=(k == K3 * TT - 1))
            last.then_inc(tok_ps, 1)
            pe.wait_ge(tok_ready, 1)


            def known(j, least):
                return isinstance(j, int) and j < least

            def turn_x(j, r, lap):
                pe.wait_ge(x_tile[r], 16 * lap + 16)
                if not known(j, 2):
                    pe.wait_ge(xt_lo, j - 1)
                for c in range(KC):
                    last = nc.tensor.transpose(xt_bank[r % 2][:, c * P:(c + 1) * P],
                                               xg[:, r, c * P:(c + 1) * P], ident[:, :])
                last.then_inc(xt_ps, 1)

            def gate_up(j, r):
                pe.wait_ge(wt_lo, j + 1)
                pe.wait_ge(xt_lo, j + 1)
                if not known(j, 2):
                    pe.wait_ge(h_sb, j - 1)
                for c in range(KC):
                    rows, cols = slice(c * P, (c + 1) * P), slice(c * 2 * I1, (c + 1) * 2 * I1)
                    for n, (x, w) in enumerate(three(xg_hi[:, r % 2, rows], xg_lo[:, r % 2, rows],
                                                     w13_hi[:, r % 2, cols], w13_lo[:, r % 2, cols])):
                        last = mm(gu_bank[r % 2], x, w, start=(c == 0 and n == 0), stop=(c == KC - 1 and n == 2))
                last.then_inc(gu_ps, 1)

            def turn_h(j, r):
                pe.wait_ge(h_sb, j + 1)
                if not known(j, 2):
                    pe.wait_ge(ht_sb, j - 1)
                for c in range(2):
                    last = nc.tensor.transpose(ht_bank[r % 2][:, c * P:(c + 1) * P],
                                               h3[:, r % 2, c * IH:(c + 1) * IH], ident[:, :])
                last.then_inc(ht_ps, 1)

            def down3(j, r, lap):
                pe.wait_ge(w2_tile[r], 16 * lap + 16)
                pe.wait_ge(ht_sb, j + 1)
                if not known(j, 2):
                    pe.wait_ge(o_sb, j - 1)
                for c in range(2):
                    last = mm(o_bank[r % 2], hT3[:, r % 2, c * P:(c + 1) * P],
                              w2[r][:, c * C:(c + 1) * C], start=(c == 0), stop=(c == 1))
                last.then_inc(o_ps, 1)

            def tile_step(j, r, lap):
                static = isinstance(j, int)
                if not static or j + 1 < MAXTILES:
                    turn_x(j + 1, (r + 1) % RING, lap + (r + 1) // RING)
                if not static or j < MAXTILES:
                    gate_up(j, r)
                if not static or 0 <= j - 2 < MAXTILES:
                    down3(j - 2, (r - 2) % RING, lap - (r < 2))
                if not static or 0 <= j - 1 < MAXTILES:
                    turn_h(j - 1, (r - 1) % RING)

            turn_x(0, 0, 0)
            for j in range(RING):
                tile_step(j, j, 0)
            n_loop = (MAXTILES - 1) // RING
            with pe.Fori(1, n_loop) as i:
                for r in range(RING):
                    tile_step(RING * i + r, r, i)
            for j in range(RING * n_loop, MAXTILES + 2):
                tile_step(j, j % RING, j // RING)

            def open_shared():
                pe.wait_ge(o_sb, MAXTILES)
                turn_gates(3)

            pe.wait_ge(ht_sb, MAXTILES)
            gated(f3, 3, True, lambda j: E + CH1 + CH2, open_shared)

            for k in range(TT):
                if k % (TT // 2) == 0:
                    pe.wait_ge(x_final, 2 if k == 0 else 4)
                if k >= 4:
                    pe.wait_ge(fin_ready, k - 3)
                for c in range(KC):
                    last = nc.tensor.transpose(out_bank[k % 4][:, c * P:(c + 1) * P],
                                               xT[:, c, k * P:(k + 1) * P], ident[:, :])
                last.then_inc(xo_ps, 1)

        @block.scalar
        def _(act):
            fn = nc.scalar.activation
            act.wait_ge(tf_sum, 1)
            fn(tf[:, :], tf[:, :], ACT.Sigmoid).then_inc(tf_sig, 1)
            act.wait_ge(in_w, 16)
            fn(ew[:, :, :], wu[:, 0], ACT.Exp).then_inc(dec_act, 1)
            act.wait_ge(dec_act, 1)
            fn(base_decay[:, :, :], ew[:, :, :], ACT.Exp, scale=-1.0).then_inc(dec_act, 1)
            for c in range(KC):
                act.wait_ge(kmin, c + 1)
                fn(ek[:, c, :], ek[:, c, :], ACT.Exp).then_inc(ek_ready, 1)
            for c in range(KC):
                act.wait_ge(ek_ready, c + 1)
                nc.scalar.copy(by_seq(ekr[:, c, :]), by_seq(ek[:, c, :])[:, :, ::-1]).then_inc(ek_ready, 1)

            def exp_euk(l):
                act.wait_ge(ukmin, l + 1)
                fn(euk[:, l], euk[:, l], ACT.Exp).then_inc(euk_ready, 1)

            exp_euk(0)

            def input_sigmoid(l):
                if l == 0:
                    act.wait_ge(in_x, 16)
                for n, (c, h) in enumerate(QUARTERS):
                    if l:
                        act.wait_ge(x_upd, 4 * (l - 1) + n + 1)
                    fn(quarter(yT, c, h), quarter(xT, c, h), ACT.Sigmoid).then_inc(y_sig, 1)

            def softmax_exp(n, tile):
                act.wait_ge(exp_in, n)
                fn(tile, tile, ACT.Exp).then_inc(exp_out, 1)

            def copy_gT(l):
                for h in range(2):
                    act.wait_ge(gT_ps, 2 * l + h + 1)
                    nc.scalar.copy(gT[:, h * HALF:(h + 1) * HALF],
                                   ps_gates[h][:, 0:HALF]).then_inc(gT_ready, 1)

            def split_w(f, j, slot, width, down):
                cols = slice(width - C, width) if down else slice(0, width - C)
                if not down:
                    act.wait_ge(f.w_in[slot], 8 * j + (16 - 8 * slot))
                if not (isinstance(j, int) and j < 2):
                    act.wait_ge(f.h_used if down else (f.u_done if width == 3 * C else f.g_done), 2 * j - 2)
                nc.scalar.copy(w_hi[:, slot, cols], wring[:, slot, cols]).then_inc(f.w_hi, 1)

            def split_in(l, f, width):
                split_w(f, 0, 0, width, False)
                for n, (c, h) in enumerate(QUARTERS):
                    act.wait_ge(y_ready, 4 * l + n + 1)
                    nc.scalar.copy(quarter(y_hi, c, h), quarter(yT, c, h)).then_inc(y_hi_ready, 1)
                split_w(f, 0, 0, width, True)
                split_w(f, 1, 1, width, False)
                split_w(f, 1, 1, width, True)

            def activate(l, f, func, bias_of, skip_u, width):
                def body(j, slot):
                    if bias_of:
                        nc.scalar.copy(b1_col[:, slot:slot + 1], b1[:, bass.ds(j, 1)]).then_inc(b1_ready, 1)
                    for h in range(2):
                        q = 2 * j + h
                        act.wait_ge(f.g_done, q + 1)
                        if not (isinstance(q, int) and q < 2):
                            act.wait_ge(f.p_ready if skip_u else f.u_read, q - 1)
                        kw = {}
                        if bias_of:
                            act.wait_ge(b1_ready, j + 1)
                            kw = {"bias": b1_col[:, slot:slot + 1]}
                        fn(act_h[:, h, :], ps_g[:, :], func, **kw).then_inc(f.g_read, 1)
                        if isinstance(q, int) and q == 0:
                            copy_gT(l)
                        if not (isinstance(j, int) and not 2 <= j + 1 < f.n):
                            split_w(f, j + 1, 1 - slot, width, h == 1)
                        act.wait_ge(f.p_ready, q + 1)
                        if not (isinstance(q, int) and q < 2):
                            act.wait_ge(f.h_used, q - 1)
                        nc.scalar.copy(hid[:, h, 0, :], prod_h[:, h, :]).then_inc(f.h_hi, 1)
                over_pairs(act, f.n, body, last_peeled=True)

            input_sigmoid(0)
            softmax_exp(1, small[:, 0, :])
            copy_gT(0)
            for l in range(1, LAYERS):
                exp_euk(l)
            input_sigmoid(1)
            split_in(1, f1, 3 * C)
            softmax_exp(2, ex[:, :, 0:E + 2])
            activate(1, f1, ACT.Silu, False, False, 3 * C)
            input_sigmoid(2)
            act.wait_ge(f1.h_used, 2 * f1.n)
            split_in(2, f2, 2 * C)
            softmax_exp(3, small[:, 0, :])
            activate(2, f2, ACT.Gelu, True, True, 2 * C)
            input_sigmoid(3)
            for k in range(4):
                act.wait_ge(yt_ps, k + 1)
                nc.scalar.copy(y_tok[:, 2 * k:2 * k + 2, :].rearrange("p k c -> p (k c)"),
                               ps_acc[:, k // 2, (k % 2) * HALF:(k % 2 + 1) * HALF]).then_inc(yt_sb, 1)
            act.wait_ge(f2.h_used, 2 * f2.n)
            split_in(3, f3, 3 * C)
            act.wait_ge(sgate_in, 1)
            fn(gates[:, :, 0], small[:, 7, :], ACT.Sigmoid).then_inc(sgate_out, 1)
            softmax_exp(4, ex[:, :, :])


            def split_tile(j, r, lap):
                act.wait_ge(w13_tile[r], 16 * lap + 16)
                if not (isinstance(j, int) and j < 2):
                    act.wait_ge(gu_ps, j - 1)
                nc.scalar.copy(w13_hi[:, r % 2, :], w13[r]).then_inc(wt_hi, 1)
                act.wait_ge(xt_ps, j + 1)
                nc.scalar.copy(xg_hi[:, r % 2, :], xt_bank[r % 2]).then_inc(xt_sb, 1)

            def tile_step(j, r, lap):
                static = isinstance(j, int)
                if not static or j + 1 < MAXTILES:
                    split_tile(j + 1, (r + 1) % RING, lap + (r + 1) // RING)
                last = r - 3 if r >= 3 else r - 3 + RING
                alone = static and j - 3 == MAXTILES - 1 and last % 2 == 0
                if (last % 2 and not (static and not 0 <= j - 3 < MAXTILES)) or alone:
                    n = 1 if alone else 2
                    act.wait_ge(o_sb, j - 2)
                    act.dma_start(t["o_rows"][bass.ds((j - 2 - n) * P, n * P), :].rearrange("(k p) c -> p k c", p=P),
                                  o3[:, last + 1 - n:last + 1, :]).then_inc(o_pair[last // 2], 16)
                if not static or j < MAXTILES:
                    act.wait_ge(gu_ps, j + 1)
                    if not (static and j < 2):
                        act.wait_ge(h_sb, j - 1)
                    fn(sg3[:, r % 2, :], gu_bank[r % 2][:, 0:I1], ACT.Silu).then_inc(sg_sb, 1)
                if not static or 0 <= j - 2 < MAXTILES:
                    act.wait_ge(o_ps, j - 1)
                    if not (static and j - 2 < RING):
                        act.wait_ge(o_pair[(r - 2) % RING // 2], 16 * lap - 16 * (r < 2))
                    nc.scalar.copy(o3[:, (r - 2) % RING, :], o_bank[r % 2]).then_inc(o_sb, 1)

            split_tile(0, 0, 0)
            for j in range(2 * RING):
                tile_step(j, j % RING, j // RING)
            n_loop = (MAXTILES - 1) // RING
            with act.Fori(2, n_loop) as i:
                for r in range(RING):
                    tile_step(RING * i + r, r, i)
            for j in range(RING * n_loop, MAXTILES + 3):
                tile_step(j, j % RING, j // RING)
            activate(3, f3, ACT.Silu, False, False, 3 * C)

        @block.gpsimd
        def _(pool):
            for tile, value in ((bias, 0.0), (g3, 0.0), (gates, 1.0), (ones60, 1.0)):
                nc.gpsimd.memset(tile[:], value).then_inc(blank, 1)

            def own_wait(semaphore, count):
                pool.wait_ge(semaphore, count)
                pool.nop(nofuse=True)

            tt = nc.gpsimd.tensor_tensor

            def present(s, par):
                if not (isinstance(s, int) and s < 2):
                    own_wait(sum0, s - 1)
                tt(now0[:, 1, par, :], seg(euk[:, 0], s), seg(ek, s), ALU.subtract).then_inc(sum_step, 1)
                own_wait(sum_step, NOWS * s + 1)
                tt(now0[:, 0, par, :], now0[:, 1, par, :], seg(kv, s), ALU.mult).then_inc(sum_step, 1)

            def sums(l, s, par):
                g = SEGS * l + s
                n = NOWS * SEGS + SUMS * (g - SEGS)
                own_wait(sum_step, n)
                tt(now_d[:, :], seg(euk[:, l], s), seg(ek, s), ALU.subtract).then_inc(sum_step, 1)
                own_wait(sum_step, n + 1)
                tt(now_n[:, :], now_d[:, :], seg(kv, s), ALU.mult).then_inc(sum_step, 1)
                pool.wait_ge(scan_step, 4 * g + 2)
                tt(nf[:, par, :], nf[:, par, :], nb[:, par, :], ALU.add).then_inc(sum_step, 1)
                pool.wait_ge(sum_step, n + 3)
                tt(nf[:, par, :], nf[:, par, :], now_n[:, :], ALU.add).then_inc(sum_step, 1)
                pool.wait_ge(scan_step, 4 * g + 4)
                tt(df[:, par, :], df[:, par, :], db[:, par, :], ALU.add).then_inc(sum_step, 1)
                pool.wait_ge(sum_step, n + 5)
                tt(df[:, par, :], df[:, par, :], now_d[:, :], ALU.add).then_inc(sum_step, 1)

            def lo_w(f, j, slot, width, down):
                cols = slice(width - C, width) if down else slice(0, width - C)
                pool.wait_ge(f.w_hi, 2 * j + (2 if down else 1))
                nc.gpsimd.tensor_tensor(w_lo[:, slot, cols], wring[:, slot, cols],
                                        w_hi[:, slot, cols].bitcast(F32), ALU.subtract).then_inc(f.w_lo, 1)

            def lo_in(l, f, width):
                if width is not None:
                    lo_w(f, 0, 0, width, False)
                pool.wait_ge(lg_done, l + 1)
                if l == 3:
                    pool.wait_ge(yt_ps, 4)
                for n, (c, h) in enumerate(QUARTERS):
                    pool.wait_ge(y_hi_ready, 4 * (l - 1) + n + 1)
                    nc.gpsimd.tensor_tensor(quarter(y_lo, c, h), quarter(yT, c, h),
                                            quarter(y_hi, c, h).bitcast(F32), ALU.subtract).then_inc(y_lo_ready, 1)
                if width is not None:
                    lo_w(f, 0, 0, width, True)
                    lo_w(f, 1, 1, width, False)
                    lo_w(f, 1, 1, width, True)

            def layer(l, f, width, l_mix):
                lo_in(l, f, width)

                def body(j, slot):
                    peeled = isinstance(j, int)

                    def split(down=False):
                        if not (peeled and not 2 <= j + 1 < f.n):
                            lo_w(f, j + 1, 1 - slot, width, down)
                    split()
                    if not (peeled and not 1 <= j < SEGS + 1):
                        sums(l_mix, j - 1, 1 - slot)
                    split(True)
                over_mix(pool, f.n, body)

            last = KC - 1
            pool.wait_ge(ek_ready, KC)
            tt(ekv[:, last, :], ek[:, last, :], kv[:, last, :], ALU.mult).then_inc(ekv_ready, 1)
            pool.wait_ge(euk_ready, 1)
            present(0, 0)
            present(1, 1)
            pool.wait_ge(ek_ready, 2 * KC)
            tt(by_seq(ekvr[:, last, :]), by_seq(ekr[:, last, :]), by_seq(kv[:, last, :])[:, :, ::-1],
               ALU.mult).then_inc(ekv_ready, 1)
            with pool.Fori(1, SEGS // 2) as i:
                for par in range(2):
                    present(2 * i + par, par)
            pool.wait_ge(euk_ready, 2)
            with pool.Fori(0, SEGS // 2) as i:
                for par in range(2):
                    sums(1, 2 * i + par, par)
            pool.wait_ge(euk_ready, LAYERS)
            layer(1, f1, 3 * C, 2)
            layer(2, f2, 2 * C, 3)
            lo_in(3, f3, None)
            half = K3 // 2
            pool.wait_ge(slots_in, 1)
            tt(slots4[:, half:K3], oh[:, half:K3], r2[:, :, :].unsqueeze(1).broadcast_to([P, K3 - half, TT, E3]),
               ALU.mult).then_inc(slots_ready, 1)
            for k in range(K3):
                rows = slice(k * TT, (k + 1) * TT)
                pool.wait_ge(of_equal, k + 1)
                tt(of_tile[:, rows, :], of_tile[:, rows, :],
                   token[:, :].unsqueeze(2).broadcast_to([P, TT, TILE_COLS]), ALU.mult).then_inc(of_token, 1)

            pool.wait_ge(tok_ready, 1)
            pool.wait_ge(yt_out, 16)

            def gather(j, r):
                if not (isinstance(j, int) and j < RING):
                    pool.wait_ge(xt_ps, j - RING + 1)
                nc.gpsimd.tensor_copy(tok_col[:, r:r + 1], tok_i[:, bass.ds(j, 1)]).then_inc(tcol, 1)
                pool.wait_ge(tcol, j + 1)
                pool.nop(nofuse=True)
                nc.gpsimd.indirect_dma_start(
                    xg[:, r, :], None, t["y_rows"],
                    bass.IndirectOffsetOnAxis(ap=tok_col[:, r:r + 1], axis=0)).then_inc(x_tile[r], 16)
            for j in range(RING):
                gather(j, j)
            n_loop = MAXTILES // RING
            with pool.Fori(1, n_loop) as i:
                for r in range(RING):
                    gather(RING * i + r, r)
            for j in range(RING * n_loop, MAXTILES):
                gather(j, j % RING)

            pool.wait_ge(gu_ps, MAXTILES)
            for j in range(2):
                lo_w(f3, j, j, 3 * C, False)
                lo_w(f3, j, j, 3 * C, True)

            for pair in range(RING // 2):
                stores = len(range(2 * pair + 1, MAXTILES, RING))
                if MAXTILES % 2 and (MAXTILES - 1) % RING // 2 == pair:
                    stores += 1
                pool.wait_ge(o_pair[pair], 16 * stores)

            def gather_back(k):
                if k >= 4:
                    pool.wait_ge(yk_in[k % 4], 16 * K3)
                for c in range(K3):
                    nc.gpsimd.indirect_dma_start(
                        yk[:, k * K3 + c, :], None, t["o_rows"],
                        bass.IndirectOffsetOnAxis(ap=slot_i[:, c * TT + k:c * TT + k + 1], axis=0)
                    ).then_inc(yk_in[k % 4], 16)
            for k in range(TT):
                gather_back(k)
                if k % 2:
                    j = (k + 3) // 2
                    lo_w(f3, j, j % 2, 3 * C, False)
                    lo_w(f3, j, j % 2, 3 * C, True)

        @block.vector
        def _(dve):
            v = nc.vector
            n_steps = [0]

            def link(ins):
                n_steps[0] += 1
                ins.then_inc(dve_step, 1)
                dve.wait_ge(dve_step, n_steps[0])

            def go(ins):
                n_steps[0] += 1
                ins.then_inc(dve_step, 1)

            def split(hi, mid, lo, whole, rest, done):
                link(v.tensor_copy(hi, whole))
                link(v.tensor_tensor(rest, whole, hi, ALU.subtract))
                link(v.tensor_copy(mid, rest))
                link(v.tensor_tensor(rest, rest, mid, ALU.subtract))
                v.tensor_copy(lo, rest).then_inc(done, 1)

            dve.wait_ge(in_cond, 16)
            v.tensor_reduce(tf[:, :], cond[:, :, :], AX.X, ALU.add).then_inc(tf_sum, 1)
            for c in range(KC):
                dve.wait_ge(in_kv[c], 16)
                v.tensor_scalar(ek[:, c, :], kv[:, c, :], 30.0, None, ALU.min).then_inc(kmin, 1)
            dve.wait_ge(in_w, 16)

            def exponent(l):
                for c in range(KC):
                    ins = v.tensor_scalar(euk[:, l, c], kv[:, c], wu[:, 1, l, c:c + 1], 30.0, ALU.add, ALU.min)
                ins.then_inc(ukmin, 1)

            def decays(l):
                for c in range(KC):
                    go(v.tensor_scalar(decay[:, l, c * B:(c + 1) * B], tfhalf[:, :], base_decay[:, l, c:c + 1],
                                       None, ALU.mult))

            dve.wait_ge(tf_sig, 1)
            go(v.tensor_scalar(tfhalf[:, :], tf[:, :], 0.5, 0.5, ALU.mult, ALU.add))
            link(v.tensor_scalar(tfout[:, :], tf[:, :], 0.2, 0.8, ALU.mult, ALU.add))
            dve.wait_ge(dec_act, 2)
            decays(0)
            for c in range(KC):
                go(v.tensor_copy(tfout8[:, c * B:(c + 1) * B], tfout[:, :]))
            for c in range(KC - 1):
                dve.wait_ge(ek_ready, c + 1)
                link(v.tensor_tensor(ekv[:, c, :], ek[:, c, :], kv[:, c, :], ALU.mult))
            exponent(0)
            for c in range(KC - 1):
                dve.wait_ge(ek_ready, KC + c + 1)
                link(v.tensor_tensor(by_seq(ekvr[:, c, :]), by_seq(ekr[:, c, :]),
                                     by_seq(kv[:, c, :])[:, :, ::-1], ALU.mult))

            def scans(l, s, par, between=None):
                g = SEGS * l + s
                if l:
                    dve.wait_ge(m_step, QUOT * (g - 1))
                dec = decay[:, l, bass.ds(s, 1)].to_broadcast([P, T])
                for n, (out, src) in enumerate(((nf[:, par, :], ekv), (nb[:, par, ::-1], ekvr),
                                                (df[:, par, :], ek), (db[:, par, ::-1], ekr))):
                    if n == 2 and between is not None:
                        between()
                    v.tensor_tensor_scan(out, dec, seg(src, s), 0.0, ALU.mult, ALU.add).then_inc(scan_step, 1)

            def quotient(l, s, par, between=None):
                g = SEGS * l + s
                if l:
                    dve.wait_ge(sum_step, NOWS * SEGS + SUMS * (g - SEGS + 1))
                    above, below = nf[:, par, :], df[:, par, :]
                else:
                    dve.wait_ge(sum0, s + 1)
                    above, below = ps_mix(s, par)[:, 0:T], ps_mix(s, par)[:, T:2 * T]
                v.tensor_scalar(rden[:, par, :], below, 1e-8, None, ALU.max).then_inc(m_step, 1)
                if between is not None:
                    between()
                dve.wait_ge(m_step, QUOT * g + 1)
                v.reciprocal(rden[:, par, :], rden[:, par, :]).then_inc(m_step, 1)
                dve.wait_ge(m_step, QUOT * g + 2)
                v.scalar_tensor_tensor(seg(mix, s), above, tfout8[:, bass.ds(s, 1)], rden[:, par, :],
                                       ALU.mult, ALU.mult).then_inc(m_step, 1)

            scans(0, 0, 0)
            scans(0, 1, 1)

            def pair(s, ahead):
                for par in range(2):
                    quotient(0, s + par, par, (lambda: scans(0, s + 2 + par, par)) if ahead else None)

            pair(0, True)
            dve.wait_ge(ekv_ready, 2)
            with dve.Fori(1, SEGS // 2 - 1) as i:
                pair(2 * i, True)
            pair(SEGS - 2, False)

            def input_of(l, prev):
                def add(n, c, h):
                    if prev is not None:
                        dve.wait_ge(prev.h_used, 2 * prev.n - 1 + h)
                        v.tensor_tensor(quarter(xT, c, h), quarter(xT, c, h), quarter(ps_acc, c, h),
                                        ALU.add).then_inc(x_upd, 1)

                def multiply(n, c, h):
                    dve.wait_ge(y_sig, 4 * l + n + 1)
                    v.tensor_tensor(quarter(yT, c, h), quarter(yT, c, h), quarter(mix, c, h),
                                    ALU.mult).then_inc(y_ready, 1)

                dve.wait_ge(m_step, QUOT * SEGS * (l + 1))
                for half in range(2):
                    for step in (add, multiply):
                        for n in (2 * half, 2 * half + 1):
                            step(n, *QUARTERS[n])

            def top8(values):
                for k in range(TT):
                    (go if k < TT - 1 else link)(v.max(mx[:, k, :], values[:, k, :]))

            def top8_index(values):
                for k in range(TT):
                    (go if k < TT - 1 else link)(v.max_index(ix[:, k, :], mx[:, k, :], values[:, k, :]))

            def one_hots(choices, n_exp, count):
                link(v.tensor_copy(ixf[:, 0:choices, :], ix[:, :, 0:choices].rearrange("p t k -> p k t")))
                for k in range(choices):
                    count(v.tensor_tensor(
                        oh[:, k, :, 0:n_exp], iota[:, 0:n_exp].unsqueeze(1).broadcast_to([P, TT, n_exp]),
                        ixf[:, k, :].unsqueeze(2).broadcast_to([P, TT, n_exp]), ALU.is_equal))

            def split_gates(l, n):
                split(g3[:, :, 0:n], g3[:, :, GCOLS:GCOLS + n], g3[:, :, 2 * GCOLS:2 * GCOLS + n],
                      gates[:, :, 0:n], r1[:, :, 0:n], gate_split)

            def weigh(out, k, w, n_exp):
                return v.tensor_tensor(out, oh[:, k, :, 0:n_exp], w.unsqueeze(2).broadcast_to([P, TT, n_exp]),
                                       ALU.mult)

            def route_top2(l, n_exp_round):
                dve.wait_ge(lg_done, l + 1)
                link(v.tensor_copy(lg[:, :, 0:E], ps_m[:, 0:TT * E].rearrange("p (k e) -> p k e", e=E)))
                top8(lg[:, :, 0:E])
                v.tensor_tensor(small[:, 0, :], mx[:, :, 1], mx[:, :, 0], ALU.subtract).then_inc(exp_in, 1)
                top8_index(lg[:, :, 0:E])
                one_hots(2, E, go)
                dve.wait_ge(exp_out, n_exp_round)
                link(v.tensor_scalar(small[:, 1, :], small[:, 0, :], 1.0, None, ALU.add))
                link(v.reciprocal(small[:, 2, :], small[:, 1, :]))
                link(v.tensor_tensor(small[:, 3, :], small[:, 0, :], small[:, 2, :], ALU.mult))
                go(weigh(r1[:, :, 0:E], 0, small[:, 2, :], E))
                link(weigh(r2[:, :, 0:E], 1, small[:, 3, :], E))
                link(v.tensor_tensor(gates[:, :, 0:E], r1[:, :, 0:E], r2[:, :, 0:E], ALU.add))
                split_gates(l, E + 1)

            def softmax_in(n_exp, choices):
                top = mx[:, :, 0:1]
                go(v.tensor_tensor(ex[:, :, 0:n_exp], lg[:, :, 0:n_exp], top.broadcast_to([P, TT, n_exp]),
                                   ALU.subtract))
                v.tensor_tensor(ex[:, :, n_exp:n_exp + choices], mx[:, :, 0:choices],
                                top.broadcast_to([P, TT, choices]), ALU.subtract).then_inc(exp_in, 1)

            def softmax_out(n_exp, choices, first, n_exp_round):
                dve.wait_ge(exp_out, n_exp_round)
                link(v.tensor_reduce(sum_e[:, :], ex[:, :, 0:n_exp], AX.X, ALU.add))
                link(v.reciprocal(rsum_e[:, :], sum_e[:, :]))
                link(v.tensor_tensor(small[:, first:first + choices, :],
                                     ex[:, :, n_exp:n_exp + choices].rearrange("p t k -> p k t"),
                                     rsum_e[:, :].unsqueeze(1).broadcast_to([P, choices, TT]), ALU.mult))

            input_of(0, None)
            dve.wait_ge(blank, 4)
            dve.wait_ge(in_const, 16 * len(consts))
            link(v.tensor_scalar(token[:, :], tbl8[:, :], pcol[:, 0:1], None, ALU.add))
            dve.wait_ge(bias_in, 16 * 6)
            split(biasp[:, :, 0], biasp[:, :, 1], biasp[:, :, 2], bias[:, :, :], biasr[:, :, :], bias_split)

            for l in range(1, LAYERS):
                exponent(l)
                decays(l)
            route_top2(0, 1)

            def weigh_input(e, slot):
                for h in range(2):
                    q = 2 * e + h
                    dve.wait_ge(f0.w_done, q + 1)
                    if not (isinstance(q, int) and q < 2):
                        dve.wait_ge(f0.h_used, q - 1)
                    v.tensor_tensor(hid0[:, h, :, :], yT[:, :, h * HALF:(h + 1) * HALF],
                                    ps_w[:, :].unsqueeze(1).broadcast_to([P, KC, HALF]),
                                    ALU.mult).then_inc(f0.h_ready, 1)
                    if h == 1:
                        quotient(1, e, slot)
                    elif not (isinstance(e, int) and e + 1 == SEGS):
                        scans(1, e + 1, 1 - slot)

            scans(1, 0, 0)
            over_pairs(dve, E, weigh_input, last_peeled=True)

            def gated_units(f, has_up, l_mix, combining=False):
                def body(j, slot, i=None):
                    for h in range(2):
                        q = 2 * j + h
                        dve.wait_ge(f.g_read, q + 1)
                        src = act_h[:, h, :]
                        if not (isinstance(q, int) and q < 2):
                            dve.wait_ge(f.h_ready, q - 1)
                        if has_up:
                            dve.wait_ge(f.u_done, q + 1)
                            v.tensor_tensor(prod_h[:, h, :], act_h[:, h, :], ps_u[:, :], ALU.mult).then_inc(f.u_read, 1)
                            dve.wait_ge(f.u_read, q + 1)
                            src = prod_h[:, h, :]
                        dve.wait_ge(f.w_done, q + 1)
                        v.tensor_tensor(prod_h[:, h, :], src, ps_w[:, :], ALU.mult).then_inc(f.p_ready, 1)

                        def lo_part():
                            dve.wait_ge(f.h_hi, q + 1)
                            v.tensor_tensor(hid[:, h, 1, :], prod_h[:, h, :], hid[:, h, 0, :].bitcast(F32),
                                            ALU.subtract).then_inc(f.h_ready, 1)
                        peeled = isinstance(j, int)
                        if combining and not (peeled and j < 2):
                            combine(2 * j + (h - 4), 2 * slot + h, i, lo_part)
                        elif l_mix and h == 0 and not (peeled and not 1 <= j < SEGS + 1):
                            scans(l_mix, j - 1, 1 - slot, lo_part)
                        elif l_mix and h == 1 and not (peeled and not 2 <= j < SEGS + 2):
                            quotient(l_mix, j - 2, slot, lo_part)
                        else:
                            lo_part()
                if combining:
                    body(0, 0)
                    body(1, 1)
                    with dve.Fori(1, f.n // 2) as i:
                        for slot in range(2):
                            body(2 * i + slot, slot, i)
                else:
                    over_mix(dve, f.n, body)

            input_of(1, f0)
            dve.wait_ge(lg_done, 2)
            link(v.tensor_copy(lg[:, :, 0:E], ps_m[:, 0:TT * E].rearrange("p (k e) -> p k e", e=E)))
            top8(lg[:, :, 0:E])
            softmax_in(E, 2)
            top8_index(lg[:, :, 0:E])
            one_hots(2, E, lambda ins: ins.then_inc(rank_in, 1))
            softmax_out(E, 2, 3, 2)
            dve.wait_ge(rank_done, 1)
            n1 = 2 * TT * E
            by_e = "p (k e) -> p e k"
            link(v.tensor_copy(tot[:, 0:n1].rearrange("p (e k) -> p e k", e=E),
                               ps_m[:, 2 * n1:3 * n1].rearrange(by_e, e=E)))
            link(v.tensor_tensor_scan(cum[:, 0:n1], scanmask1[:, :], tot[:, 0:n1], 0.0, ALU.mult, ALU.add))
            link(v.tensor_tensor(cum[:, 0:n1].rearrange("p (e k) -> p e k", e=E),
                                 cum[:, 0:n1].rearrange("p (e k) -> p e k", e=E),
                                 ps_m[:, n1:2 * n1].rearrange(by_e, e=E), ALU.add))
            link(v.tensor_scalar(cum[:, 0:n1], cum[:, 0:n1], float(CAP), None, ALU.is_le))
            for k in range(2):
                link(weigh([r1, r2][k][:, :, 0:E], k, small[:, 3 + k, :], E))
                link(v.tensor_tensor([r1, r2][k][:, :, 0:E], [r1, r2][k][:, :, 0:E],
                                     cum[:, 0:n1].rearrange("p (e k) -> p k e", e=E)[:, k * TT:(k + 1) * TT, :],
                                     ALU.mult))
            link(v.tensor_tensor(gates[:, :, 0:E], r1[:, :, 0:E], r2[:, :, 0:E], ALU.add))
            split_gates(1, E + 1)
            gated_units(f1, True, 2)

            input_of(2, f1)
            route_top2(2, 3)
            gated_units(f2, False, 3)

            input_of(3, f2)
            dve.wait_ge(lg_done, 4)
            link(v.tensor_copy(lg[:, :, :], ps_m[:, 0:TT * (E3 + 1)].rearrange("p (k e) -> p k e", e=E3 + 1)))
            v.tensor_copy(small[:, 7, :], lg[:, :, E3]).then_inc(sgate_in, 1)
            top8(lg[:, :, 0:E3])
            top8_index(lg[:, :, 0:E3])
            one_hots(K3, E3, lambda ins: ins.then_inc(rank_in, 1))
            softmax_in(E3, K3)
            dve.wait_ge(rank_done, 2)
            link(v.tensor_copy(tot[:, :].rearrange("p (e k) -> p e k", e=E3),
                               ps_u[:, 0:TT * E3].rearrange("p (k e) -> p e k", e=E3)))
            link(v.tensor_tensor_scan(cum[:, :], scanmask3[:, :], tot[:, :], 0.0, ALU.mult, ALU.add))
            cume = cum[:, :].rearrange("p (e k) -> p e k", e=E3)
            over = r1[:, :, :].rearrange("p k e -> p (k e)").rearrange("p (e k) -> p e k", e=E3)
            link(v.tensor_tensor(over, cume[:, :, TT - 1:TT].broadcast_to([P, E3, TT]),
                                 tbl8[:, :].unsqueeze(1).broadcast_to([P, E3, TT]), ALU.is_gt))
            link(v.tensor_reduce(tiles3[:, :], over, AX.X, ALU.add))
            link(v.tensor_tensor_scan(tincl[:, :], ones60[:, :], tiles3[:, :], 0.0, ALU.mult, ALU.add))
            go(v.tensor_tensor(tbase[:, :], tincl[:, :], tiles3[:, :], ALU.subtract))
            link(v.tensor_scalar(r2[:, 0, :], tincl[:, :], pcol[:, 0:1], None, ALU.is_le))
            link(v.tensor_reduce(te_f[:, :], r2[:, 0, :], AX.X, ALU.add))
            v.tensor_scalar(te_i[:, :], te_f[:, :], float(E3 - 1), None, ALU.min).then_inc(te_ready, 1)
            link(v.scalar_tensor_tensor(r1[:, :, :], tbase[:, :].unsqueeze(1).broadcast_to([P, TT, E3]), float(P),
                                        cum[:, :].rearrange("p (e k) -> p k e", e=E3), ALU.mult, ALU.add))
            v.tensor_tensor(r2[:, :, :], r1[:, :, :],
                            ps_g[:, 0:TT * E3].rearrange("p (k e) -> p k e", e=E3), ALU.add).then_inc(slots_in, 1)
            dve.wait_ge(slots_in, 1)
            half = K3 // 2
            link(v.tensor_tensor(slots4[:, 0:half], oh[:, 0:half],
                                 r2[:, :, :].unsqueeze(1).broadcast_to([P, half, TT, E3]), ALU.mult))
            for k in range(0, K3, half):
                if k:
                    dve.wait_ge(slots_ready, 1)
                link(v.tensor_reduce(place_f[:, 0, k * TT:(k + half) * TT],
                                     slots4[:, k:k + half].rearrange("p k t e -> p (k t) e"), AX.X, ALU.add))
            link(v.tensor_copy(slot_i[:, :], place_f[:, 0, :]))
            go(v.tensor_scalar(place_i[:, 0, :], slot_i[:, :], 7, None, ALU.arith_shift_right))
            link(v.tensor_scalar(place_i[:, 1, :], slot_i[:, :], P - 1, None, ALU.bitwise_and))
            link(v.tensor_copy(place_f[:, 1:3, :], place_i[:, :, :]))
            for k in range(K3):
                rows = slice(k * TT, (k + 1) * TT)
                v.tensor_tensor(of_tile[:, rows, :], iota[:, 0:TILE_COLS].unsqueeze(1).broadcast_to([P, TT, TILE_COLS]),
                                place_f[:, 1, rows].unsqueeze(2).broadcast_to([P, TT, TILE_COLS]),
                                ALU.is_equal).then_inc(of_equal, 1)
                v.tensor_tensor(in_tile[:, rows, :], iota[:, :].unsqueeze(1).broadcast_to([P, TT, P]),
                                place_f[:, 2, rows].unsqueeze(2).broadcast_to([P, TT, P]),
                                ALU.is_equal).then_inc(onehots, 1)
            dve.wait_ge(tok_ps, 1)
            v.tensor_copy(tok_i[:, 0:TILE_COLS], ps_m[:, 0:TILE_COLS]).then_inc(tok_ready, 1)
            softmax_out(E3, K3, 0, 4)
            dve.wait_ge(sgate_out, 1)
            split_gates(3, 1)



            def split_tile(j, r):
                dve.wait_ge(wt_hi, j + 1)
                v.tensor_tensor(w13_lo[:, r % 2, :], w13[r], w13_hi[:, r % 2, :].bitcast(F32),
                                ALU.subtract).then_inc(wt_lo, 1)
                dve.wait_ge(xt_sb, j + 1)
                v.tensor_tensor(xg_lo[:, r % 2, :], xt_bank[r % 2], xg_hi[:, r % 2, :].bitcast(F32),
                                ALU.subtract).then_inc(xt_lo, 1)

            def tile_step(j, r):
                static = isinstance(j, int)
                if not static or j + 1 < MAXTILES:
                    split_tile(j + 1, (r + 1) % RING)
                if not static or j < MAXTILES:
                    dve.wait_ge(sg_sb, j + 1)
                    if not (static and j < 2):
                        dve.wait_ge(ht_ps, j - 1)
                    v.tensor_tensor(h3[:, r % 2, :], sg3[:, r % 2, :], gu_bank[r % 2][:, I1:2 * I1],
                                    ALU.mult).then_inc(h_sb, 1)
                if not static or 0 <= j - 1 < MAXTILES:
                    dve.wait_ge(ht_ps, j)
                    if not (static and j - 1 < 2):
                        dve.wait_ge(o_ps, j - 2)
                    v.tensor_copy(hT3[:, (r - 1) % 2, :], ht_bank[(r - 1) % 2]).then_inc(ht_sb, 1)

            split_tile(0, 0)
            for j in range(3):
                tile_step(j, j)
            n_loop = (MAXTILES - 3) // RING
            with dve.Fori(0, n_loop) as i:
                for k in range(RING):
                    tile_step(RING * i + (3 + k), (3 + k) % RING)
            for j in range(3 + RING * n_loop, MAXTILES + 1):
                tile_step(j, j % RING)

            def combine(k, place, lap, between):
                out = fin[:, bass.ds(k, 1), :].rearrange("p a c -> p (a c)")
                for c in range(K3):
                    w = small[:, c, bass.ds(k, 1)]
                    rows = yk[:, bass.ds(k * K3 + c, 1), :].rearrange("p a c -> p (a c)")
                    if c == 2:
                        between()
                    if c == 0:
                        dve.wait_ge(yk_in[place], 16 * K3 * lap)
                        ins = v.tensor_scalar(out, rows, w, None, ALU.mult)
                    else:
                        dve.wait_ge(comb_step, K3 * k + c)
                        ins = v.scalar_tensor_tensor(out, rows, w, out, ALU.mult, ALU.add)
                    ins.then_inc(comb_step, 1)

            gated_units(f3, True, None, combining=True)
            for c, h in QUARTERS:
                dve.wait_ge(f3.h_used, 2 * CH3 - 1 + h)
                v.tensor_tensor(quarter(xT, c, h), quarter(xT, c, h), quarter(ps_acc, c, h),
                                ALU.add).then_inc(x_final, 1)
            for k in range(TT):
                dve.wait_ge(xo_ps, k + 1)
                v.tensor_tensor(fin[:, k, :], fin[:, k, :], out_bank[k % 4][:, 0:C], ALU.add).then_inc(fin_ready, 1)


def kernel(**inputs):
    import ml_dtypes
    import concourse.bacc as _bacc
    from concourse.bass_utils import run_bass_kernel_spmd as _run

    a = {k: np.ascontiguousarray(v) for k, v in inputs.items()}

    def channel_major(x):
        return np.ascontiguousarray(x.reshape(-1, KC, P).transpose(2, 1, 0))

    def lhs(w):
        return w.reshape(-1, P, KC, P).transpose(0, 3, 2, 1).reshape(-1, P, C)

    def padded(w, rows):
        out = np.zeros((rows, w.shape[1]), w.dtype)
        out[:w.shape[0]] = w
        return out

    w_u = [np.stack([a[f"L{l}_cond_{n}"].reshape(KC, P) for l in range(LAYERS)]) for n in "wu"]
    wd1 = a["L1_ffn_Wd"].transpose(0, 2, 1).reshape(CH1, P, C)
    l1 = [lhs(a["L1_ffn_Wg"].reshape(-1, C)), lhs(a["L1_ffn_Wu"].reshape(-1, C)), wd1]
    w1 = np.concatenate([a["L2_ffn_w1"].transpose(0, 2, 1).reshape(-1, C), a["L2_ffn_shared_w1"].T])
    w2 = np.concatenate([a["L2_ffn_w2"].reshape(-1, C), a["L2_ffn_shared_w2"]]).reshape(CH2, P, C)
    gu = a["L3_ffn_se_gate_up_w"]
    sh = [lhs(padded(gu[:ISH], CH3 * P)), lhs(padded(gu[ISH:], CH3 * P)),
          padded(a["L3_ffn_se_down_w"].T, CH3 * P).reshape(CH3, P, C)]
    b1 = np.concatenate([a["L2_ffn_b1"], a["L2_ffn_shared_b1"].reshape(-1, P)])

    def cols(w):
        return w.reshape(KC, P, -1).transpose(1, 0, 2)

    routers = np.stack([cols(a["L0_ffn_Wr"]), cols(a["L1_ffn_Wr"].T), cols(a["L2_ffn_gate_w"])], 1)
    router3 = np.concatenate([cols(a["L3_ffn_gate_w"].T), cols(a["L3_ffn_shared_gate_w"].T)], 2)

    f32, bf16 = np.float32, ml_dtypes.bfloat16
    q = np.arange(P)
    tri = np.stack([-1.0 * (q[:, None] > q), -1.0 * (q[:, None] >= q), np.ones((P, P))], 1).astype(bf16)
    rows = list(range(E)) + [0] * CH1 + list(range(CH2)) + [0]
    sel = np.zeros((P, len(rows), P), bf16)
    for j, row in enumerate(rows):
        expert = np.full(P, min(row, E))
        if E <= j < E + CH1:
            expert = (P * (j - E) + q) // I1
        for part in range(3):
            sel[part * GCOLS + expert, j, q] = 1
    n1, n3 = 2 * TT, TT
    arrays = {
        "cond": a["cond_512"], "wu": np.stack(w_u).transpose(3, 0, 1, 2),
        "kvT": channel_major(a["fside_BxSxS_0"]), "xT": channel_major(a["x"]),
        "ident": np.eye(P, dtype=f32), "identb": np.eye(P, dtype=bf16), "tri": tri, "sel": sel,
        "iota": np.tile(q.astype(f32), (P, 1)), "pcol": q.astype(f32)[:, None],
        "scanmask1": np.tile((np.arange(E * n1) % n1 > 0).astype(f32), (P, 1)),
        "scanmask3": np.tile((np.arange(E3 * n3) % n3 > 0).astype(f32), (P, 1)),
        "tbl8": np.tile((P * np.arange(TT)).astype(f32), (P, 1)),
        "routers": routers, "router3": router3, "b1": b1.T,
        "be": a["L0_ffn_be"], "b2": np.concatenate([a["L2_ffn_b2"], a["L2_ffn_shared_b2"][None]]),
        "we": a["L0_ffn_We"].reshape(E, KC, P, C).transpose(0, 2, 1, 3).reshape(E * P, KC * C),
        "w_l1": np.concatenate(l1, 2).reshape(CH1 * P, 3 * C),
        "w_l2": np.concatenate([lhs(w1), w2], 2).reshape(CH2 * P, 2 * C),
        "w_sh": np.concatenate(sh, 2).reshape(CH3 * P, 3 * C),
        "w13": a["L3_ffn_w13"].reshape(E3, 2 * I1, KC, P).transpose(0, 3, 2, 1).reshape(E3 * P, KC * 2 * I1),
        "w2": a["L3_ffn_w2"].reshape(E3, C, 2, IH).transpose(0, 3, 2, 1).reshape(E3 * IH, 2 * C),
    }
    arrays = {k: np.ascontiguousarray(v) for k, v in arrays.items()}

    nc = _bacc.Bacc("TRN2", target_bir_lowering=False, num_devices=1)
    t = {k: nc.dram_tensor(f"in_{k}", v.shape, mybir.dt.from_np(v.dtype), kind="ExternalInput").ap()
         for k, v in arrays.items()}
    t["out"] = nc.dram_tensor("out", (N, C), F32, kind="ExternalOutput").ap()
    t["te"] = nc.dram_tensor("tile_experts", (P, 1), I32, kind="Internal").ap()
    t["y_rows"] = nc.dram_tensor("y_rows", (N, C), F32, kind="Internal").ap()
    t["o_rows"] = nc.dram_tensor("o_rows", (MAXTILES * P, C), F32, kind="Internal").ap()
    build(nc, t)
    r = _run(nc, [{f"in_{k}": v for k, v in arrays.items()}], core_ids=[0])
    return r.results[0]["out"].reshape(B, T, C)
```
